# Optimizing a Trainium2 kernel written in Bass

```python
import numpy as np
import jax
import jax.numpy as jnp

def _softmax(x, axis=-1):
    return jax.nn.softmax(x, axis=axis)

def _gelu(x):
    return jax.nn.gelu(x, approximate=True)

def _silu(x):
    return jax.nn.silu(x)

def _sigmoid(x):
    return jax.nn.sigmoid(x)

def _layernorm(x, axis=-1, eps=1e-05):
    m = jnp.mean(x, axis=axis, keepdims=True)
    v = jnp.var(x, axis=axis, keepdims=True)
    return (x - m) / jnp.sqrt(v + eps)

def _scatter_add(tgt, idx, src, axis=0):
    return tgt.at[idx].add(src)

def _segment_sum(src, seg, n):
    return jax.ops.segment_sum(src, seg, n)
kernel_name = 'mk_xattn_ffn_d2_seqx_r4_f62a4c'

def setup_inputs(seed: int=0):
    np.random.seed(seed)
    _w = jnp.asarray

    def _rec_inputs():
        import jax
        import jax.numpy as jnp
        _rk = jax.random.key(seed)
        x = -0.0002928 + 1 * jax.random.normal(jax.random.fold_in(_rk, 1), (8, 256, 256), jnp.float32)
        _lenS = 256 - jax.random.randint(jax.random.fold_in(_rk, 7), (8,), 0, max(1, 256 // 4) + 1, jnp.int32)
        _lenS2 = 256 - jax.random.randint(jax.random.fold_in(_rk, 8), (8,), 0, max(1, 256 // 4) + 1, jnp.int32)
        _ctx_1024P = jax.random.normal(jax.random.fold_in(_rk, 11), (8, 16, 256), jnp.float32)
        _ctx_1024c = jax.random.dirichlet(jax.random.fold_in(_rk, 511), 0.3 * jnp.ones((16,), jnp.float32), (8, 256))
        _ctx_1024t = jnp.einsum('bsk,bkd->bsd', _ctx_1024c, _ctx_1024P)
        _ctx_1024t = _ctx_1024t * jax.lax.rsqrt(jnp.mean(jnp.square(_ctx_1024t)) + 1e-12) * 0.953939
        ctx_1024 = -1.39393e-06 + 0.999914 * (_ctx_1024t + 0.3 * jax.random.normal(jax.random.fold_in(_rk, 611), (8, 256, 256), jnp.float32))
        _validS = jnp.arange(256)[None, :] < _lenS[:, None]
        _validS2 = jnp.arange(256)[None, :] < _lenS2[:, None]
        _causal = jnp.tril(jnp.ones((256, 256), dtype=bool))
        mask_BxSxS2_bf0 = jnp.logical_not(jnp.ones((8, 256, 256), dtype=bool))
        return (x, ctx_1024, mask_BxSxS2_bf0)
    x, ctx_1024, mask_BxSxS2_bf0 = _rec_inputs()

    def _L0_xattn_setup():
        import jax, jax.numpy as jnp
        import numpy as np
        H = 16
        D_MODEL = 256
        D_K = D_MODEL // H
        MAX_REL = 16
        REL_VOCAB = 2 * MAX_REL + 1

        def _rel_pos_ids(seq_len):
            r = jnp.arange(seq_len)
            dist = r[None, :] - r[:, None]
            return jnp.clip(dist, -MAX_REL, MAX_REL) + MAX_REL
        key = jax.random.key(seed)
        ks = jax.random.split(key, 16)
        B, S = (2, 512)
        f32 = jnp.float32
        inp = {'query': jax.random.normal(ks[0], (B, S, D_MODEL), f32), 'key': jax.random.normal(ks[1], (B, S, D_MODEL), f32), 'value': jax.random.normal(ks[2], (B, S, D_MODEL), f32), 'Wq': jax.random.normal(ks[3], (D_MODEL, D_MODEL), f32) * 0.02, 'bq': jnp.zeros((D_MODEL,), f32), 'Wk': jax.random.normal(ks[4], (D_MODEL, D_MODEL), f32) * 0.02, 'bk': jnp.zeros((D_MODEL,), f32), 'Wv': jax.random.normal(ks[5], (D_MODEL, D_MODEL), f32) * 0.02, 'bv': jnp.zeros((D_MODEL,), f32), 'Wo': jax.random.normal(ks[6], (D_MODEL, D_MODEL), f32) * 0.02, 'bo': jnp.zeros((D_MODEL,), f32), 'rel_k_table': jax.random.normal(ks[7], (REL_VOCAB, D_K), f32) * 0.02, 'rel_v_table': jax.random.normal(ks[8], (REL_VOCAB, D_K), f32) * 0.02}
        return inp
    _L0_xattn_all = _L0_xattn_setup()
    _L0_xattn_in = {k: v for k, v in _L0_xattn_all.items() if k in ('Wq', 'bq', 'Wk', 'bk', 'Wv', 'bv', 'Wo', 'bo', 'rel_k_table', 'rel_v_table')}
    del _L0_xattn_all

    def _L0_ffn_setup():
        import jax, jax.numpy as jnp
        import numpy as np
        H = 256
        I = 1024
        E = 4
        LN_EPS = 1e-12

        def _layer_norm(x, gamma, beta, eps=LN_EPS):
            mu = jnp.mean(x, axis=-1, keepdims=True)
            var = jnp.mean(jnp.square(x - mu), axis=-1, keepdims=True)
            return (x - mu) * jax.lax.rsqrt(var + eps) * gamma + beta
        key = jax.random.key(seed)
        ks = jax.random.split(key, 8)
        B, S = (4, 128)
        scale = 0.02
        return {'hidden_states': jax.random.normal(ks[0], (B, S, H), jnp.float32), 'W_router': jax.random.normal(ks[1], (H, E), jnp.float32) * scale, 'W1': jax.random.normal(ks[2], (E, H, I), jnp.float32) * scale, 'b1': jax.random.normal(ks[3], (E, I), jnp.float32) * scale, 'Wo': jax.random.normal(ks[4], (I, H), jnp.float32) * scale, 'bo': jax.random.normal(ks[5], (H,), jnp.float32) * scale, 'ln_gamma': jnp.ones((H,), jnp.float32), 'ln_beta': jnp.zeros((H,), jnp.float32)}
    _L0_ffn_all = _L0_ffn_setup()
    _L0_ffn_in = {k: v for k, v in _L0_ffn_all.items() if k in ('W_router', 'W1', 'b1', 'Wo', 'bo', 'ln_gamma', 'ln_beta')}
    del _L0_ffn_all

    def _L1_xattn_setup():
        import jax, jax.numpy as jnp
        import numpy as np
        NUM_HEADS = 16
        NEG_INF = float('-inf')
        key = jax.random.key(seed)
        ks = jax.random.split(key, 8)
        B, S, D = (2, 512, 256)
        return {'query': jax.random.normal(ks[0], (B, S, D), jnp.float32), 'key': jax.random.normal(ks[1], (B, S, D), jnp.float32), 'value': jax.random.normal(ks[2], (B, S, D), jnp.float32), 'attention_mask': jnp.zeros((B, S, S), dtype=bool), 'Wq': jax.random.normal(ks[3], (D, D), jnp.float32) * D ** (-0.5), 'Wk': jax.random.normal(ks[4], (D, D), jnp.float32) * D ** (-0.5), 'Wv': jax.random.normal(ks[5], (D, D), jnp.float32) * D ** (-0.5), 'Wout': jax.random.normal(ks[6], (D, D), jnp.float32) * D ** (-0.5), 'b_out': jnp.zeros((D,), jnp.float32), 'is_causal': 1}
    _L1_xattn_all = _L1_xattn_setup()
    _L1_xattn_in = {k: v for k, v in _L1_xattn_all.items() if k in ('Wq', 'Wk', 'Wv', 'Wout', 'b_out')}
    del _L1_xattn_all

    def _L1_ffn_setup():
        import jax, jax.numpy as jnp
        import numpy as np
        EPS = 1e-08
        key = jax.random.key(seed)
        kx, kw = jax.random.split(key)
        x = jax.random.normal(kx, (8, 1024, 256), dtype=jnp.float32)
        weight = jax.random.normal(kw, (256, 256), dtype=jnp.float32) * (1.0 / np.sqrt(256))
        return {'x': x, 'weight': weight}
    _L1_ffn_all = _L1_ffn_setup()
    _L1_ffn_in = {k: v for k, v in _L1_ffn_all.items() if k in ('weight',)}
    del _L1_ffn_all
    return {'x': x, 'ctx_1024': ctx_1024, 'mask_BxSxS2_bf0': mask_BxSxS2_bf0, 'L0_xattn_Wq': _L0_xattn_in['Wq'], 'L0_xattn_bq': _L0_xattn_in['bq'], 'L0_xattn_Wk': _L0_xattn_in['Wk'], 'L0_xattn_bk': _L0_xattn_in['bk'], 'L0_xattn_Wv': _L0_xattn_in['Wv'], 'L0_xattn_bv': _L0_xattn_in['bv'], 'L0_xattn_Wo': _L0_xattn_in['Wo'], 'L0_xattn_bo': _L0_xattn_in['bo'], 'L0_xattn_rel_k_table': _L0_xattn_in['rel_k_table'], 'L0_xattn_rel_v_table': _L0_xattn_in['rel_v_table'], 'L0_ffn_W_router': _L0_ffn_in['W_router'], 'L0_ffn_W1': _L0_ffn_in['W1'], 'L0_ffn_b1': _L0_ffn_in['b1'], 'L0_ffn_Wo': _L0_ffn_in['Wo'], 'L0_ffn_bo': _L0_ffn_in['bo'], 'L0_ffn_ln_gamma': _L0_ffn_in['ln_gamma'], 'L0_ffn_ln_beta': _L0_ffn_in['ln_beta'], 'L1_xattn_Wq': _L1_xattn_in['Wq'], 'L1_xattn_Wk': _L1_xattn_in['Wk'], 'L1_xattn_Wv': _L1_xattn_in['Wv'], 'L1_xattn_Wout': _L1_xattn_in['Wout'], 'L1_xattn_b_out': _L1_xattn_in['b_out'], 'L1_ffn_weight': _L1_ffn_in['weight']}

def reference(x, ctx_1024, mask_BxSxS2_bf0, L0_xattn_Wq, L0_xattn_bq, L0_xattn_Wk, L0_xattn_bk, L0_xattn_Wv, L0_xattn_bv, L0_xattn_Wo, L0_xattn_bo, L0_xattn_rel_k_table, L0_xattn_rel_v_table, L0_ffn_W_router, L0_ffn_W1, L0_ffn_b1, L0_ffn_Wo, L0_ffn_bo, L0_ffn_ln_gamma, L0_ffn_ln_beta, L1_xattn_Wq, L1_xattn_Wk, L1_xattn_Wv, L1_xattn_Wout, L1_xattn_b_out, L1_ffn_weight):
    import jax
    import jax.numpy as jnp

    def _L0_xattn_ref(query, key, value, Wq, bq, Wk, bk, Wv, bv, Wo, bo, rel_k_table, rel_v_table):
        import jax, jax.numpy as jnp
        import numpy as np
        H = 16
        D_MODEL = 256
        D_K = D_MODEL // H
        MAX_REL = 16
        REL_VOCAB = 2 * MAX_REL + 1

        def _rel_pos_ids(seq_len):
            r = jnp.arange(seq_len)
            dist = r[None, :] - r[:, None]
            return jnp.clip(dist, -MAX_REL, MAX_REL) + MAX_REL
        B, S, E = query.shape
        ids = _rel_pos_ids(S)
        rel_k = rel_k_table[ids]
        rel_v = rel_v_table[ids]

        def proj(x, W, b):
            y = x @ W.T + b
            return y.reshape(B, S, H, D_K).transpose(0, 2, 1, 3)
        q = proj(query, Wq, bq)
        k = proj(key, Wk, bk)
        v = proj(value, Wv, bv)
        logits = jnp.einsum('bhqd,bhkd->bhqk', q, k) + jnp.einsum('bhqd,qkd->bhqk', q, rel_k)
        w = jax.nn.softmax(logits, axis=-1)
        x = jnp.einsum('bhqk,bhkd->bhqd', w, v) + jnp.einsum('bhqk,qkd->bhqd', w, rel_v)
        x = x.transpose(0, 2, 1, 3).reshape(B, S, H * D_K)
        return x @ Wo.T + bo

    def _L0_ffn_ref(hidden_states, W_router, W1, b1, Wo, bo, ln_gamma, ln_beta):
        import jax, jax.numpy as jnp
        import numpy as np
        H = 256
        I = 1024
        E = 4
        LN_EPS = 1e-12

        def _layer_norm(x, gamma, beta, eps=LN_EPS):
            mu = jnp.mean(x, axis=-1, keepdims=True)
            var = jnp.mean(jnp.square(x - mu), axis=-1, keepdims=True)
            return (x - mu) * jax.lax.rsqrt(var + eps) * gamma + beta
        B, S, _ = hidden_states.shape
        x = hidden_states.reshape(-1, H)
        logits = x @ W_router
        expert_idx = jnp.argmax(logits, axis=-1)
        h = jnp.einsum('th,ehi->tei', x, W1) + b1
        h = jax.nn.gelu(h, approximate=False)
        onehot = jax.nn.one_hot(expert_idx, E, dtype=x.dtype)
        intermediate = jnp.einsum('te,tei->ti', onehot, h)
        y = intermediate @ Wo + bo + x
        y = _layer_norm(y, ln_gamma, ln_beta)
        return y.reshape(B, S, H)

    def _L1_xattn_ref(query, key, value, attention_mask, Wq, Wk, Wv, Wout, b_out, is_causal):
        import jax, jax.numpy as jnp
        import numpy as np
        NUM_HEADS = 16
        NEG_INF = float('-inf')
        B, q_len, D = query.shape
        k_len = key.shape[1]
        H = NUM_HEADS
        dk = D // H
        q = (query @ Wq.T).reshape(B, q_len, H, dk).transpose(0, 2, 1, 3)
        k = (key @ Wk.T).reshape(B, k_len, H, dk).transpose(0, 2, 1, 3)
        v = (value @ Wv.T).reshape(B, k_len, H, dk).transpose(0, 2, 1, 3)
        scores = jnp.einsum('bhqd,bhkd->bhqk', q, k) / jnp.sqrt(jnp.float32(dk))
        if is_causal:
            causal = jnp.triu(jnp.ones((q_len, k_len), dtype=bool), k=1)
            scores = jnp.where(causal, NEG_INF, scores)
        scores = jnp.where(attention_mask[:, None, :, :], NEG_INF, scores)
        attn = jax.nn.softmax(scores, axis=-1)
        attn = jnp.where(jnp.isnan(attn), 0.0, attn)
        out = jnp.einsum('bhqk,bhkd->bhqd', attn, v)
        out = out.transpose(0, 2, 1, 3).reshape(B, q_len, D)
        return out @ Wout.T + b_out

    def _L1_ffn_ref(x, weight):
        import jax, jax.numpy as jnp
        import numpy as np
        EPS = 1e-08
        w_scale = jnp.mean(jnp.abs(weight)) + EPS
        u = weight / w_scale
        w_quant = u + jax.lax.stop_gradient(jnp.clip(jnp.round(u), -1.0, 1.0) - u)
        a_scale = jnp.max(jnp.abs(x), axis=-1, keepdims=True) + EPS
        z = jnp.clip(x / a_scale * 127.0, -128.0, 127.0)
        a_quant = z + jax.lax.stop_gradient(jnp.round(z) - z)
        y = jnp.einsum('bsi,oi->bso', a_quant, w_quant)
        y = y * (w_scale * a_scale / 127.0)
        return y
    x = x + _L0_xattn_ref(_layernorm(x, axis=-1), ctx_1024, ctx_1024, L0_xattn_Wq, L0_xattn_bq, L0_xattn_Wk, L0_xattn_bk, L0_xattn_Wv, L0_xattn_bv, L0_xattn_Wo, L0_xattn_bo, L0_xattn_rel_k_table, L0_xattn_rel_v_table)
    x = x + _L0_ffn_ref(_layernorm(x, axis=-1), L0_ffn_W_router, L0_ffn_W1, L0_ffn_b1, L0_ffn_Wo, L0_ffn_bo, L0_ffn_ln_gamma, L0_ffn_ln_beta)
    x = x + _L1_xattn_ref(_layernorm(x, axis=-1), ctx_1024, ctx_1024, mask_BxSxS2_bf0, L1_xattn_Wq, L1_xattn_Wk, L1_xattn_Wv, L1_xattn_Wout, L1_xattn_b_out, 1)
    x = x + _L1_ffn_ref(_layernorm(x, axis=-1), L1_ffn_weight)
    return x

_drawn_inputs = setup_inputs


def setup_inputs(seed=0):
    import zlib

    import numpy as np

    out = dict(_drawn_inputs(seed))
    spreads = {'L0_xattn_bq': (0.0, 0.8),
     'L0_xattn_bk': (0.0, 2.0),
     'L0_xattn_bv': (0.0, 0.1),
     'L0_xattn_bo': (0.0, 0.1),
     'L0_ffn_ln_gamma': (1.0, 0.2),
     'L0_ffn_ln_beta': (0.0, 0.1),
     'L1_xattn_b_out': (0.0, 0.1)}
    factors = {'L0_xattn_Wq': 6.766,
     'L0_xattn_Wk': 6.466,
     'L0_xattn_rel_k_table': 28.669,
     'L0_xattn_rel_v_table': 8.0,
     'L0_ffn_b1': 8.0,
     'L0_ffn_bo': 5.664}
    for name, (base, spread) in spreads.items():
        noise = np.random.default_rng([zlib.crc32(name.encode()), seed]).standard_normal(out[name].shape)
        drawn = base * np.exp(spread * noise) if base else spread * noise
        out[name] = jnp.asarray(drawn.astype(out[name].dtype))
    for name, factor in factors.items():
        out[name] = (out[name] * factor).astype(out[name].dtype)
    return out
```

```python
from contextlib import ExitStack

import numpy as np

import concourse.bass as bass
from concourse import mybir

F32 = mybir.dt.float32
BF16 = mybir.dt.bfloat16
U8 = mybir.dt.uint8
ALU = mybir.AluOpType
ACT = mybir.ActivationFunctionType
AX = mybir.AxisListType

P = 128
B, S, D = 8, 256, 256
H = 16
DK = D // H
T = S // P
C = D // P
E, I = 4, 1024
IC = I // P
R = 16
NREL = 2 * R + 1
XLO = -(P + R)
XN = 2 * (P + R)
MASKED = -1.0e30
LN_EPS = 1e-5
FFN_EPS = 1e-12
BIT_EPS = 1e-8
ROUND = 1.5 * 2.0 ** 23

QPART = [0, 0, 1, 0, 2, 1]
KPART = [0, 1, 0, 2, 0, 1]
STACK = len(QPART) * DK

UNITS = 8
UH = 4
PAIRS = 16
SLOTS = PAIRS + T

PER = {
    "x_loaded": 16, "ctx_loaded": 16, "mask_loaded": 16,
    "stats": 4 * 5, "rstd": 5, "xn_ready": 5,
    "xT_psum": 3, "xT_sbuf": 3, "ctxT_psum": 1, "ctxT_sbuf": 1,
    "q_psum": 2, "k_psum": 2, "v_psum": 2, "q_f32": 2, "k_f32": 3, "v_sbuf": 6,
    "part1": 5, "resid": 5, "part2": 5, "part3": 5,
    "q_written": 32, "k_written": 48, "q_stacked": 2 * 96, "k_stacked": 3 * 96,
    "rel_psum": 10, "rel_sbuf": 10,
    "scores": 2 * UNITS, "masked": UNITS, "negmax": 2 * UNITS, "exped": 2 * UNITS * UH,
    "wT_psum": 2 * SLOTS, "wT_sbuf": 2 * SLOTS, "pv_psum": 2 * T, "rinv": 2 * T,
    "relv_psum": T, "relv_sbuf": T, "relv_written": T * 64, "relv_loaded": T * 16,
    "mask_add": 1, "inverted": T,
    "o_sum": T, "oT": 2 * T, "y_psum": 2 * T, "x_base": 2, "x_new": 3,
    "logits": 1, "route": 4, "onehot": 1, "ohT_psum": 3, "ohT_sbuf": 1, "x_expert": E,
    "h_psum": IC // 2, "gelu": IC // 2, "ffn_psum": 1, "ffn_base": 1, "ffn_sum": 1, "ffn_scale": 2,
    "amax": 3, "zq": 3, "aq": 1, "aT_psum": 1, "aT_sbuf": 1, "bit_psum": 1,
    "out_sbuf": 1, "stored": 16,
}


def _program(nc, x, ctx_in, mask, Wq0, bq0, Wk0, bk0, Wv0, bv0, Wo0, bo0, relk, relv,
             Wr, W1, b1, Wf, bf, gamma, beta, Wq1, Wk1, Wv1, Wo1, bo1, Wb, out):
    with ExitStack() as stack:
        def sb(name, shape, dt=F32):
            return stack.enter_context(nc.sbuf_tensor(name, shape, dt))

        def dram(name, shape, dt=F32):
            return nc.dram_tensor(name, shape, dt, kind="Internal").ap()

        def new_sem(name):
            return stack.enter_context(nc.semaphore(name))

        ident = sb("ident", [P, P])
        ident_bf = sb("ident_bf", [P, P], BF16)
        ones = sb("ones", [P, P])
        wT = sb("wT", [P, 8, C, D])
        wr = sb("wr", [P, C, E])
        w1 = sb("w1", [P, E, C, I])
        wf = sb("wf", [P, IC, D])
        b1p = sb("b1p", [3 * E, I], BF16)
        wbT = sb("wbT", [P, C, D], BF16)
        wscale = sb("wscale", [P, 1])
        rows = sb("rows", [P, 9, D])
        BV_D, BV_O0, BV_O1, BO0, BF_, GAMMA, BETA, BO1, WB0 = range(9)
        chb = sb("chb", [P, 6, C])
        relk_st = sb("relk_st", [STACK, 3, XN], BF16)
        relv_d = sb("relv_d", [P, P + 1, DK])
        relv_o = sb("relv_o", [P, T, R + 1, DK])
        causal = sb("causal", [P, T, S])
        halfs = sb("halfs", [P, T])

        X = sb("X", [P, T, D])
        XB = sb("XB", [P, T, D])
        CT = sb("CT", [P, T, D])
        CTT = sb("CTT", [P, C, S])
        XN_ = sb("XN", [P, T, D])
        XT = sb("XT", [P, C, S])
        MK = sb("MK", [P, T, S], U8)
        MA = sb("MA", [P, T, S])
        st6 = sb("st6", [P, T, 6])
        mv = sb("mv", [P, T, 2])
        ve = sb("ve", [P, T])
        rs = sb("rs", [P, T])
        QS = sb("QS", [STACK, H, S], BF16)
        KS = sb("KS", [STACK, T, H, S], BF16)
        V2 = sb("V2", [P, 2, T, H, 2 * DK])
        ET = sb("ET", [P, T, H, P])
        EC = sb("EC", [R, T, H, 2 * R])
        WT_ = sb("WT", [P, T, T, H, P])
        W = sb("W", [P, 2, UH, S])
        RV = sb("RV", [P, H, 2 * R])
        RVC = sb("RVC", [P, T, C, P])
        RT = sb("RT", [P, T, C, P])
        OT = sb("OT", [P, C, S])
        mx = sb("mx", [P, 2, UNITS * UH])
        nm = sb("nm", [P, 2, UNITS * UH])
        sums = sb("sums", [P, 2, T, H])
        rinv = sb("rinv", [P, T, H, DK])
        valid = sb("valid", [P, T, H])
        oh = sb("oh", [P, T, E])
        lg = sb("lg", [P, T, E])
        lmax = sb("lmax", [P, T])
        gate = sb("gate", [P, 1])
        firsts = sb("firsts", [P, T, E])
        oh12 = sb("oh12", [P, T, 3, E], BF16)
        ohT = sb("ohT", [3 * E, S], BF16)
        am = sb("am", [P, 3, T])
        AQ = sb("AQ", [P, T, D], BF16)
        AQT = sb("AQT", [P, C, S], BF16)
        QKF = W[:, :, :, :].rearrange("p a h s -> p (a h s)")[:, 0:3 * C * S].rearrange("p (o c s) -> p o c s", o=3, c=C)
        RES = ET[:, :, :, :].rearrange("p a h s -> p (a h s)")[:, 0:3 * C * S].rearrange("p (o c s) -> p o c s", o=3, c=C)
        SM = ET[:, :, :, :].rearrange("p a h s -> p (a h s)")[:, 0:2 * UH * S].rearrange("p (a h s) -> p a h s", a=2, h=UH)
        flat = WT_[:, :, :, :, :].rearrange("p a b h s -> p (a b h s)")
        XE = flat[:, 0:E * C * S].rearrange("p (e c s) -> p e c s", e=E, c=C)
        GT = flat[:, E * C * S:E * C * S + IC * S].rearrange("p (i s) -> p i s", i=IC)
        NPART = 3 * 3 * C * S
        parts = flat[:, 2 * T * H * P - NPART // 2:].bitcast(BF16).rearrange("p (o i c s) -> p o i c s", o=3, i=3, c=C)
        WST = flat[:, 0:8 * C * D].rearrange("p (m o d) -> p m o d", m=8, o=C)

        PS = stack.enter_context(nc.psum_tensor("PS", [P, 8, 512], F32))

        def bank(n):
            return PS[:, n, :]

        q_scr = dram("q_scr", (3, C, P, S), BF16)
        k_scr = dram("k_scr", (T, 3, C, P, S), BF16)
        rv_scr = dram("rv_scr", (T, H, DK, P))
        relv_small = dram("relv_small", (3, NREL, DK))
        relv_pad = dram("relv_pad", (3, XN, DK))

        sem = {n: new_sem(n) for n in PER}
        batch_done = new_sem("batch_done")
        w_loaded, aux_loaded, const_made = new_sem("w_loaded"), new_sem("aux_loaded"), new_sem("const_made")
        wtr_psum, wtr_sbuf = new_sem("wtr_psum"), new_sem("wtr_sbuf")
        rel_step, rel_dma, setup_dve = new_sem("rel_step"), new_sem("rel_dma"), new_sem("setup_dve")
        relk_done, relv_tab, abs_psum, setup_act = new_sem("relk_done"), new_sem("relv_tab"), new_sem("abs_psum"), new_sem("setup_act")
        raised = dict.fromkeys(PER, 0)

        def sig(ins, name, by=1):
            ins.then_inc(sem[name], by)
            raised[name] += by

        def wait(eng, it, name, n):
            assert 0 < n <= PER[name], (name, n)
            eng.wait_ge(sem[name], it * PER[name] + n)

        rk = X[0:DK, 0, 0:NREL]
        rkp = CT[:, :, :].rearrange("p a b -> p (a b)")[0:DK, 0:XN]
        rkd = XN_[0:DK, 0, 0:3 * NREL].rearrange("p (a b) -> p a b", a=3)
        rkpad = flat[0:DK, 4096:4096 + 3 * XN].rearrange("p (a b) -> p a b", a=3)
        rkres = flat[0:DK, 4096 + 3 * XN:4096 + 6 * XN].rearrange("p (a b) -> p a b", a=3)
        rkP = [parts[0:DK, i, :, :, :].rearrange("p a c s -> p (a c s)")[:, 0:3 * XN].rearrange("p (a b) -> p a b", a=3) for i in range(3)]
        rv3 = XB[0:NREL, 0, 0:3 * DK].rearrange("p (a d) -> p a d", a=3)
        rvb = XB[0:NREL, 1, 0:2 * DK].rearrange("p (a d) -> p a d", a=2)
        rvrow = OT[:, 0, 0:2 * DK].rearrange("p (a d) -> p a d", a=2)
        b1f = ET[:, :, :, :].rearrange("p a h s -> p (a h s)")
        b1v = [b1f[0:E, i * I:(i + 1) * I] for i in range(2)]
        b1bf = [QS[0:E, 4 * i:4 * i + 4, :].rearrange("p h s -> p (h s)") for i in range(3)]
        wb = CTT[:, :, :]
        wbq = XT[:, :, :]
        wbbf = AQ[:, :, :]
        wsum = rs[:, 0:1]
        wrec = rs[:, 1:2]

        block = stack.enter_context(nc.Block())
        BATCHES = B
        AUX = 16 * (6 + 2 * (2 + P // DK) + 2 * C + 6)
        CONSTS = 7 + T + 1 + T * E
        SETUP_DVE = 1

        @block.sync
        def _(sp):
            for m, w in enumerate([Wq0, Wk0, Wv0, Wo0, Wq1, Wk1, Wv1, Wo1]):
                sp.dma_start(WST[:, m, :, :], w.rearrange("(o p) d -> p o d", p=P)).then_inc(w_loaded, 16)
            sp.dma_start(wb, Wb.rearrange("(o p) d -> p o d", p=P)).then_inc(w_loaded, 16)
            sp.wait_ge(rel_step, 1)
            for a in range(3):
                sp.dma_start(relv_small[a], rv3[:, a, :]).then_inc(rel_dma, 16)
            sp.wait_ge(rel_dma, 48)
            low, mid = -R - XLO + 1, NREL - 2
            for a in range(3):
                sp.dma_start(relv_pad[a, 0:low, :], relv_small[a, 0:1, :].broadcast_to([low, DK])).then_inc(rel_dma, 16)
                sp.dma_start(relv_pad[a, low:low + mid, :], relv_small[a, 1:1 + mid, :]).then_inc(rel_dma, 16)
                sp.dma_start(relv_pad[a, low + mid:XN, :], relv_small[a, NREL - 1:NREL, :].broadcast_to([XN - low - mid, DK])).then_inc(rel_dma, 16)
            sp.wait_ge(rel_dma, 48 + 144)

            def toeplitz(a, first, n):
                return bass.AP(relv_pad.tensor, (a * XN + first) * DK, [[DK, P], [1, n * DK]])
            sp.dma_start(relv_d[:, :, :].rearrange("p s d -> p (s d)"), toeplitz(0, -(P - 1) - XLO, P + 1)).then_inc(relv_tab, 16)
            sp.dma_start(relv_o[:, 0, :, :].rearrange("p s d -> p (s d)"), toeplitz(1, 1 - XLO, R + 1)).then_inc(relv_tab, 16)
            sp.dma_start(relv_o[:, 1, :, :].rearrange("p s d -> p (s d)"), toeplitz(2, -(P + R - 1) - XLO, R + 1)).then_inc(relv_tab, 16)
            sp.wait_ge(relk_done, 1)
            for j, part in enumerate(KPART):
                sp.dma_start(relk_st[j * DK:(j + 1) * DK, :, :], rkP[part]).then_inc(relv_tab, 16)
            for i in range(3):
                sp.dma_start(b1p[i * E:(i + 1) * E, :], b1bf[i]).then_inc(relv_tab, 16)
            sp.wait_ge(relv_tab, 16 * 12)
            with sp.Fori(0, BATCHES) as it:
                sp.wait_ge(batch_done, it + 1)
                sig(sp.dma_start(CT[:, :, :], ctx_in[bass.ds(it, 1)].rearrange("o (t p) d -> p (o t) d", p=P)), "ctx_loaded", 16)
                sig(sp.dma_start(X[:, :, :], x[bass.ds(it, 1)].rearrange("o (t p) d -> p (o t) d", p=P)), "x_loaded", 16)
                sig(sp.dma_start(MK[:, :, :], mask[bass.ds(it, 1)].rearrange("o (t p) d -> p (o t) d", p=P)), "mask_loaded", 16)

                done_q = 0
                for layer in range(2):
                    ops = [("q", q_scr, QS[:, :, :])] + [("k", k_scr[v], KS[:, v, :, :]) for v in range(T if layer == 0 else 1)]
                    base = 0 if layer == 0 else 3
                    for o, (kind, scr, _) in enumerate(ops):
                        wait(sp, it, "part2", base + o + 1)
                        wait(sp, it, "part3", base + o + 1)
                        sig(sp.dma_start(scr.rearrange("i g p t -> p (i g) t"),
                                         parts[:, o, :, :, :].rearrange("p i g t -> p (i g) t")), kind + "_written", 16)
                    for o, (kind, scr, dst) in enumerate(ops):
                        if kind == "q":
                            done_q += 16
                            wait(sp, it, "q_written", done_q)
                        else:
                            wait(sp, it, "k_written", 32 if layer == 0 else 48)
                        for j, part in enumerate(QPART if kind == "q" else KPART):
                            sig(sp.dma_start(dst[j * DK:(j + 1) * DK, :, :],
                                             scr[part].rearrange("g (h d) t -> d (g h) t", d=DK)), kind + "_stacked", 16)
                    if layer == 0:
                        for qt in range(T):
                            wait(sp, it, "relv_sbuf", qt + 1)
                            for j in range(4):
                                sig(sp.dma_start(rv_scr[qt].rearrange("h d q -> d h q")[:, :, j * 2 * R:(j + 1) * 2 * R],
                                                 RV[2 * R * j:2 * R * j + DK, :, :]), "relv_written", 16)
                            wait(sp, it, "relv_written", 64 * (qt + 1))
                            sig(sp.dma_start(RVC[:, qt, :, :], rv_scr[qt].rearrange("(g h) d q -> (h d) g q", g=C)), "relv_loaded", 16)
                wait(sp, it, "out_sbuf", 1)
                sig(sp.dma_start(out[bass.ds(it, 1)].rearrange("o (t p) d -> p (o t) d", p=P), XB[:, :, :]), "stored", 16)
                wait(sp, it, "stored", 16)
                sp.nop().then_inc(batch_done, 1)

        @block.gpsimd
        def _(pool):
            nc.gpsimd.memset(ident[:, :], 0.0).then_inc(const_made, 1)
            nc.gpsimd.memset(ones[:, :], 1.0).then_inc(const_made, 1)
            nc.gpsimd.memset(causal[:, :, :], 0.0).then_inc(const_made, 1)
            nc.gpsimd.memset(halfs[:, :], -0.5).then_inc(const_made, 1)
            nc.gpsimd.memset(V2[:, :, :, :, :], 0.0).then_inc(const_made, 1)
            nc.gpsimd.memset(EC[:, :, :, :], 0.0).then_inc(const_made, 1)
            pool.wait_ge(const_made, 6)
            nc.gpsimd.affine_select(out=ident[:, :], in_=ident[:, :], compare_op=ALU.not_equal, fill=1.0, base=0,
                                    pattern=[[-1, P]], channel_multiplier=1).then_inc(const_made, 1)
            for t in range(T):
                nc.gpsimd.affine_select(out=causal[:, t, :], in_=causal[:, t, :], compare_op=ALU.is_ge, fill=MASKED,
                                        base=t * P, pattern=[[-1, S]], channel_multiplier=1).then_inc(const_made, 1)
            pool.wait_ge(const_made, 7 + T)
            nc.gpsimd.tensor_copy(ident_bf[:, :], ident[:, :]).then_inc(const_made, 1)
            for t in range(T):
                for e in range(E):
                    nc.gpsimd.memset(firsts[:, t, e:e + 1], float(E - e)).then_inc(const_made, 1)
            pool.dma_start(rows[:, BV_D, :], bv0.partition_broadcast(P)).then_inc(aux_loaded, 16)
            pool.dma_start(rows[:, BO0, :], bo0.partition_broadcast(P)).then_inc(aux_loaded, 16)
            pool.dma_start(rows[:, BF_, :], bf.partition_broadcast(P)).then_inc(aux_loaded, 16)
            pool.dma_start(rows[:, GAMMA, :], gamma.partition_broadcast(P)).then_inc(aux_loaded, 16)
            pool.dma_start(rows[:, BETA, :], beta.partition_broadcast(P)).then_inc(aux_loaded, 16)
            pool.dma_start(rows[:, BO1, :], bo1.partition_broadcast(P)).then_inc(aux_loaded, 16)
            for a, r in enumerate([0, NREL - 1]):
                pool.dma_start(rvrow[:, a, :], relv[r].partition_broadcast(P)).then_inc(aux_loaded, 16)
                pool.dma_start(rvb[:, a, :], relv[r].partition_broadcast(NREL)).then_inc(aux_loaded, 16)
                for h in range(P // DK):
                    pool.dma_start(chb[h * DK:(h + 1) * DK, 2 + a, 0:1], relk[r].rearrange("(d o) -> d o", o=1)).then_inc(aux_loaded, 16)
            for g in range(C):
                for a, b_ in enumerate([bq0, bk0]):
                    pool.dma_start(chb[:, a, g:g + 1], b_[g * P:(g + 1) * P].rearrange("(p o) -> p o", o=1)).then_inc(aux_loaded, 16)
            pool.dma_start(rk, relk.rearrange("r d -> d r"), allow_slow_non_contiguous=True).then_inc(aux_loaded, 16)
            pool.dma_start(rv3[:, 0, :], relv).then_inc(aux_loaded, 16)
            pool.dma_start(b1v[0], b1).then_inc(aux_loaded, 16)
            pool.dma_start(wr[:, :, :], Wr.rearrange("(c p) e -> p c e", p=P)).then_inc(aux_loaded, 16)
            pool.dma_start(w1[:, :, :, :], W1.rearrange("e (c p) i -> p e c i", p=P)).then_inc(aux_loaded, 16)
            pool.dma_start(wf[:, :, :], Wf.rearrange("(i p) d -> p i d", p=P)).then_inc(aux_loaded, 16)
            pool.wait_ge(aux_loaded, AUX)
            pool.wait_ge(const_made, CONSTS)
            pool.nop().then_inc(batch_done, 1)
            with pool.Fori(0, BATCHES) as it:
                pool.wait_ge(batch_done, it + 1)
                for n in range(5):
                    wait(pool, it, "stats", 4 * (n + 1))
                    sig(nc.gpsimd.tensor_tensor(rs[:, :], ve[:, :], halfs[:, :], ALU.pow), "rstd")
                    if n == 0:
                        wait(pool, it, "x_loaded", 16)
                        sig(nc.gpsimd.tensor_tensor(XB[:, :, :], X[:, :, :], rows[:, BO0:BO0 + 1, :].broadcast_to([P, T, D]), ALU.add), "x_base")
                    if n == 1:
                        wait(pool, it, "xn_ready", 2)
                        sig(nc.gpsimd.tensor_tensor(OT[:, :, :], XN_[:, :, :], rows[:, BF_:BF_ + 1, :].broadcast_to([P, T, D]), ALU.add), "ffn_base")
                    if n == 2:
                        wait(pool, it, "x_new", 2)
                        sig(nc.gpsimd.tensor_tensor(XB[:, :, :], X[:, :, :], rows[:, BO1:BO1 + 1, :].broadcast_to([P, T, D]), ALU.add), "x_base")

        @block.scalar
        def _(act):
            for m in range(8):
                act.wait_ge(wtr_psum, m + 1)
                nc.scalar.activation(wT[:, m, :, :], bank(m % 4).rearrange("p (c d) -> p c d", c=C), ACT.Copy).then_inc(wtr_sbuf, 1)
            act.wait_ge(batch_done, 1)
            act.wait_ge(setup_dve, SETUP_DVE)
            with act.Fori(0, BATCHES) as it:
                act.wait_ge(batch_done, it + 1)
                wait(act, it, "ctxT_psum", 1)
                sig(nc.scalar.activation(CTT[:, :, :], bank(0).rearrange("p (c s) -> p c s", c=C), ACT.Copy), "ctxT_sbuf")

                def bias_copy(dst, src, col, g, name, last):
                    ins = nc.scalar.activation(dst, src, ACT.Identity, bias=chb[:, col, g:g + 1])
                    if last:
                        sig(ins, name)

                def xT_copy(n):
                    wait(act, it, "xT_psum", n)
                    sig(nc.scalar.activation(XT[:, :, :], bank(1).rearrange("p (c s) -> p c s", c=C), ACT.Copy), "xT_sbuf")

                def split(base, n):
                    for o in range(n):
                        sig(nc.scalar.activation(parts[:, o, 0, :, :], QKF[:, o, :, :], ACT.Copy), "part1")
                    for o in range(n):
                        wait(act, it, "resid", base + o + 1)
                        sig(nc.scalar.activation(parts[:, o, 1, :, :], RES[:, o, :, :], ACT.Copy), "part2")

                xT_copy(1)
                wait(act, it, "k_psum", 1)
                kp = bank(3).rearrange("p (g s) -> p g s", g=C)
                for v in range(T):
                    for g in range(C):
                        for kt in range(T):
                            col = 1 if kt == v else (5 if kt > v else 4)
                            bias_copy(QKF[:, 1 + v, g, kt * P:(kt + 1) * P], kp[:, g, kt * P:(kt + 1) * P], col, g, "k_f32", g == C - 1 and kt == T - 1)
                wait(act, it, "q_psum", 1)
                qp = bank(2).rearrange("p (g s) -> p g s", g=C)
                for g in range(C):
                    bias_copy(QKF[:, 0, g, :], qp[:, g, :], 0, g, "q_f32", g == C - 1)
                wait(act, it, "q_f32", 1)
                wait(act, it, "k_f32", 2)
                split(0, 3)
                for n in range(8):
                    wait(act, it, "rel_psum", n + 1)
                    if n == 0:
                        wait(act, it, "part3", 3)
                    sig(nc.scalar.activation(ET[:, n // 4, :, (n % 4) * 32:(n % 4 + 1) * 32],
                                             bank([5, 6, 7, 0][n % 4]).rearrange("p (q h) -> p h q", h=H), ACT.Copy), "rel_sbuf")
                wait(act, it, "rel_psum", 10)
                for n in range(T):
                    at = R if n == 0 else 0
                    sig(nc.scalar.activation(EC[:, n, :, at:at + R],
                                             bank(1)[0:R, n * 256:(n + 1) * 256].rearrange("p (q h) -> p h q", h=H), ACT.Copy), "rel_sbuf")

                def exps(layer, u):
                    qt = u // (UNITS // T)
                    nk = S if layer == 0 or qt else P
                    wait(act, it, "negmax", layer * UNITS + u + 1)
                    if u >= 2:
                        wait(act, it, "wT_psum", layer * SLOTS + (u - 2) * 2 + 2 + (u - 2) // 4)
                    for i in range(UH):
                        h = u * UH + i
                        src = PS[:, 2 * (u % 2):2 * (u % 2) + 2, :].rearrange("p b (h s) -> p (b h) s", h=2)[:, i, 0:nk] if layer == 0 else SM[:, u % 2, i, 0:nk]
                        sig(nc.scalar.activation(W[:, u % 2, i, 0:nk], src, ACT.Exp, bias=nm[:, layer, h:h + 1],
                                                 scale=1.0 if layer == 0 else DK ** -0.5,
                                                 accum_out=sums[:, layer, qt, h % H:h % H + 1]), "exped")

                for u in range(UNITS):
                    exps(0, u)
                    if u == 5 or u == 7:
                        qt = 0 if u == 5 else 1
                        wait(act, it, "relv_psum", qt + 1)
                        if qt == 1:
                            wait(act, it, "relv_written", 64)
                        sig(nc.scalar.activation(RV[:, :, :], bank(7).rearrange("p (q h) -> p h q", h=H), ACT.Copy), "relv_sbuf")
                xT_copy(2)
                for n in range(IC // 2):
                    wait(act, it, "h_psum", n + 1)
                    sig(nc.scalar.activation(GT[:, 2 * n:2 * n + 2, :], bank(n % 2).rearrange("p (i s) -> p i s", i=2), ACT.Gelu), "gelu")
                xT_copy(3)
                wait(act, it, "k_psum", 2)
                sig(nc.scalar.activation(QKF[:, 1, :, :], kp, ACT.Copy), "k_f32")
                wait(act, it, "q_psum", 2)
                sig(nc.scalar.activation(QKF[:, 0, :, :], qp, ACT.Copy), "q_f32")
                wait(act, it, "q_f32", 2)
                wait(act, it, "k_f32", 3)
                split(3, 2)
                for u in range(UNITS):
                    exps(1, u)

        @block.vector
        def _(dve):
            V = nc.vector
            steps = [0]

            def step(ins):
                steps[0] += 1
                ins.then_inc(setup_act, 1)
                dve.wait_ge(setup_act, steps[0])

            dve.wait_ge(aux_loaded, AUX)
            dve.wait_ge(const_made, CONSTS)
            step(V.tensor_tensor(rv3[:, 1, :], rv3[:, 0, :], rvb[:, 1, :], ALU.subtract))
            V.tensor_tensor(rv3[:, 2, :], rv3[:, 0, :], rvb[:, 0, :], ALU.subtract).then_inc(rel_step, 1)
            bvh = rows[:, BV_D, :].rearrange("p (h d) -> p h d", h=H)
            step(V.tensor_tensor(rows[:, BV_O0, :].rearrange("p (h d) -> p h d", h=H), bvh, rvrow[:, 0:1, :].broadcast_to([P, H, DK]), ALU.add))
            step(V.tensor_tensor(rows[:, BV_O1, :].rearrange("p (h d) -> p h d", h=H), bvh, rvrow[:, 1:2, :].broadcast_to([P, H, DK]), ALU.add))
            for a in range(2):
                step(V.tensor_scalar(chb[:, 4 + a, :], chb[:, 1, :], chb[:, 2 + a, 0:1], None, ALU.add))
            step(V.tensor_copy(rkd[:, 0, :], rk))
            step(V.tensor_scalar(rkd[:, 1, :], rk, rk[:, NREL - 1:NREL], None, ALU.subtract))
            step(V.tensor_scalar(rkd[:, 2, :], rk, rk[:, 0:1], None, ALU.subtract))
            low, mid = -R - XLO + 1, NREL - 2
            dve.wait_ge(wtr_psum, 8)
            for a in range(3):
                step(V.tensor_copy(rkpad[:, a, 0:low], rkd[:, a, 0:1].broadcast_to([DK, low])))
                step(V.tensor_copy(rkpad[:, a, low:low + mid], rkd[:, a, 1:1 + mid]))
                step(V.tensor_copy(rkpad[:, a, low + mid:XN], rkd[:, a, NREL - 1:NREL].broadcast_to([DK, XN - low - mid])))
            step(V.tensor_copy(rkP[0], rkpad))
            step(V.tensor_tensor(rkres, rkpad, rkP[0], ALU.subtract))
            step(V.tensor_copy(rkP[1], rkres))
            step(V.tensor_tensor(rkP[2], rkres, rkP[1], ALU.subtract))
            step(V.tensor_copy(b1bf[0], b1v[0]))
            step(V.tensor_tensor(b1v[1], b1v[0], b1bf[0], ALU.subtract))
            step(V.tensor_copy(b1bf[1], b1v[1]))
            step(V.tensor_tensor(b1bf[2], b1v[1], b1bf[1], ALU.subtract))
            dve.nop().then_inc(relk_done, 1)
            dve.wait_ge(w_loaded, 16 * 9)
            step(V.tensor_reduce(wsum, wb, AX.XY, ALU.add, apply_absolute_value=True))
            dve.nop().then_inc(abs_psum, 1)
            dve.wait_ge(abs_psum, 2)
            step(V.tensor_scalar(wscale[:, :], bank(4)[:, 0:1], 1.0 / (D * D), BIT_EPS, ALU.mult, ALU.add))
            step(V.reciprocal(wrec, wscale[:, :]))
            step(V.tensor_scalar(wbq, wb, wrec, ROUND, ALU.mult, ALU.add))
            step(V.tensor_scalar(wbq, wbq, -ROUND, 1.0, ALU.add, ALU.min))
            step(V.tensor_scalar(wbbf, wbq, -1.0, None, ALU.max))
            dve.nop().then_inc(abs_psum, 1)
            dve.wait_ge(abs_psum, 4)
            step(V.tensor_copy(wbT[:, :, :], bank(5)[:, 0:D].bitcast(BF16).rearrange("p (c d) -> p c d", c=C)))
            dve.wait_ge(relv_tab, 16 * 12)
            dve.nop().then_inc(setup_dve, 1)

            with dve.Fori(0, BATCHES) as it:
                dve.wait_ge(batch_done, it + 1)
                n_stat = [0]

                def layernorm(n, src, dst, eps, rstd_n, ready=None):
                    for t in range(T):
                        sig(V.bn_stats(st6[:, t, :], src[:, t, :]), "stats") if t == T - 1 else V.bn_stats(st6[:, t, :], src[:, t, :])
                    n_stat[0] += 1
                    wait(dve, it, "stats", n_stat[0])
                    V.memset(gate[:, :], 0.0)
                    for t in range(T):
                        ins = V.bn_aggr(mv[:, t, :], st6[:, t, :])
                    sig(ins, "stats", 2)
                    n_stat[0] += 2
                    wait(dve, it, "stats", n_stat[0])
                    sig(V.tensor_scalar(ve[:, :], mv[:, :, 1], eps, None, ALU.add), "stats")
                    n_stat[0] += 1
                    wait(dve, it, "rstd", rstd_n)
                    for t in range(T):
                        ins = V.tensor_scalar(dst[:, t, :], src[:, t, :], mv[:, t, 0:1], rs[:, t:t + 1], ALU.subtract, ALU.mult)
                    return ins

                def split(base, n):
                    for o in range(n):
                        wait(dve, it, "part1", base + o + 1)
                        sig(V.tensor_tensor(RES[:, o, :, :], QKF[:, o, :, :], parts[:, o, 0, :, :], ALU.subtract), "resid")
                    for o in range(n):
                        wait(dve, it, "part2", base + o + 1)
                        sig(V.tensor_tensor(parts[:, o, 2, :, :], RES[:, o, :, :], parts[:, o, 1, :, :], ALU.subtract), "part3")

                def values(layer):
                    wait(dve, it, "v_psum", layer + 1)
                    vp = bank(4).rearrange("p (k h a d) -> p k h a d", k=T, a=2, d=DK)
                    for a in range(2):
                        for var in range(2 if layer == 0 else 1):
                            dst = V2[:, var, :, :, :].rearrange("p k (h a) d -> p k h a d", a=2)[:, :, :, a, a * DK:(a + 1) * DK]
                            if layer == 1:
                                sig(V.tensor_copy(dst, vp[:, :, :, a, :]), "v_sbuf")
                            elif var == 0:
                                row = rows[:, BV_D:BV_D + 1, :].rearrange("p k (h a d) -> p k h a d", a=2, d=DK)[:, :, :, a, :]
                                sig(V.tensor_tensor(dst, vp[:, :, :, a, :], row.broadcast_to([P, T, H // 2, DK]), ALU.add), "v_sbuf")
                            else:
                                row = rows[:, BV_O0:BV_O1 + 1, :].rearrange("p k (h a d) -> p k h a d", a=2, d=DK)[:, :, :, a, :]
                                sig(V.tensor_tensor(dst, vp[:, :, :, a, :], row, ALU.add), "v_sbuf")

                def maxes(layer, u):
                    qt = u // (UNITS // T)
                    wait(dve, it, "scores", layer * UNITS + u + 1)
                    sv = PS[:, 2 * (u % 2):2 * (u % 2) + 2, :].rearrange("p b (h s) -> p (b h) s", h=2)
                    if layer == 0:
                        sig(V.tensor_reduce(nm[:, 0, u * UH:(u + 1) * UH], sv, AX.X, ALU.max, negate=True), "negmax")
                        return
                    nk = S if qt else P
                    if u >= 2:
                        wait(dve, it, "exped", (UNITS + u - 1) * UH)
                    V.memset(gate[:, :], 0.0)
                    for i in range(UH):
                        ins = V.tensor_tensor_reduce(out=SM[:, u % 2, i, 0:nk], in0=sv[:, i, 0:nk], in1=MA[:, qt, 0:nk], scale=1.0,
                                                     scalar=-3.0e38, op0=ALU.add, op1=ALU.max, accum_out=mx[:, 1, u * UH + i:u * UH + i + 1])
                    sig(ins, "masked")
                    wait(dve, it, "masked", u + 1)
                    sig(V.tensor_scalar(nm[:, 1, u * UH:(u + 1) * UH], mx[:, 1, u * UH:(u + 1) * UH], -(DK ** -0.5), None, ALU.mult), "negmax")

                def probs_T(layer, p):
                    qt, hp = p // (PAIRS // T), p % (PAIRS // T)
                    n = p + qt
                    nk = T if layer == 0 or qt else 1
                    wait(dve, it, "wT_psum", layer * SLOTS + n + 1)
                    src = bank(4 + n % 2).rearrange("p (h k q) -> p k h q", h=2, k=T)[:, 0:nk, :, :]
                    sig(V.tensor_copy(WT_[:, qt, 0:nk, 2 * hp:2 * hp + 2, :], src), "wT_sbuf")

                def inverse(layer, qt):
                    wait(dve, it, "exped", (layer * T + qt + 1) * H)
                    if layer == 0:
                        sig(V.reciprocal(rinv[:, qt, :, :], sums[:, 0, qt, :].unsqueeze(2).broadcast_to([P, H, DK])), "rinv")
                        return
                    sig(V.reciprocal(sums[:, 1, qt, :], sums[:, 1, qt, :]), "inverted")
                    wait(dve, it, "inverted", qt + 1)
                    sig(V.scalar_tensor_tensor(out=rinv[:, qt, :, :], in0=mx[:, 1, qt * H:(qt + 1) * H].unsqueeze(2).broadcast_to([P, H, DK]), scalar=0.5 * MASKED,
                                               in1=sums[:, 1, qt, :].unsqueeze(2).broadcast_to([P, H, DK]), op0=ALU.is_gt, op1=ALU.mult), "rinv")

                def inverse_T(layer, qt):
                    n = (qt + 1) * (PAIRS // T) + qt
                    wait(dve, it, "wT_psum", layer * SLOTS + n + 1)
                    sig(V.tensor_copy(RT[:, qt, :, :], bank(4 + n % 2)[:, 0:D].rearrange("p (g q) -> p g q", g=C)), "wT_sbuf")

                def finish(layer):
                    wait(dve, it, "pv_psum", layer * T + T)
                    for qt in range(T):
                        wait(dve, it, "wT_sbuf", layer * SLOTS + (qt + 1) * (PAIRS // T + 1))
                        po = bank(6)[:, qt * D:(qt + 1) * D].rearrange("p (g q) -> p g q", g=C)
                        dst = OT[:, :, qt * P:(qt + 1) * P]
                        if layer == 0:
                            wait(dve, it, "relv_loaded", 16 * (qt + 1))
                            sig(V.tensor_tensor(RVC[:, qt, :, :], po, RVC[:, qt, :, :], ALU.add), "o_sum")
                            wait(dve, it, "o_sum", qt + 1)
                            sig(V.tensor_tensor(dst, RVC[:, qt, :, :], RT[:, qt, :, :], ALU.mult), "oT")
                        else:
                            sig(V.tensor_tensor(dst, po, RT[:, qt, :, :], ALU.mult), "oT")

                def attention(layer):
                    for u in range(UNITS + 1):
                        if u < UNITS:
                            maxes(layer, u)
                        if u >= 1:
                            v = u - 1
                            probs_T(layer, 2 * v)
                            probs_T(layer, 2 * v + 1)
                            if v % 4 == 3:
                                inverse(layer, v // 4)
                                inverse_T(layer, v // 4)
                    finish(layer)

                def residual(layer):
                    wait(dve, it, "y_psum", layer * T + T)
                    wait(dve, it, "x_base", layer + 1)
                    dst = X
                    sig(V.tensor_tensor(dst[:, :, :], bank(0).rearrange("p (t d) -> p t d", t=T), XB[:, :, :], ALU.add), "x_new")

                wait(dve, it, "x_loaded", 16)
                sig(layernorm(0, X, XN_, LN_EPS, 1), "xn_ready")
                values(0)
                split(0, 3)
                wait(dve, it, "mask_loaded", 16)
                sig(V.scalar_tensor_tensor(out=MA[:, :, :], in0=MK[:, :, :], scalar=MASKED, in1=causal[:, :, :], op0=ALU.mult, op1=ALU.add), "mask_add")
                attention(0)
                residual(0)
                wait(dve, it, "x_new", 1)
                sig(layernorm(1, X, XN_, LN_EPS, 2), "xn_ready")
                wait(dve, it, "logits", 1)
                lp = bank(2)[:, 0:T * E].rearrange("p (t e) -> p t e", t=T)
                sig(V.tensor_reduce(lmax[:, :], lp, AX.X, ALU.max), "route")
                wait(dve, it, "route", 1)
                for t in range(T):
                    ins = V.tensor_scalar(lg[:, t, :], lp[:, t, :], lmax[:, t:t + 1], None, ALU.is_ge)
                sig(ins, "route")
                wait(dve, it, "route", 2)
                sig(V.tensor_tensor(lg[:, :, :], lg[:, :, :], firsts[:, :, :], ALU.mult), "route")
                wait(dve, it, "route", 3)
                sig(V.tensor_reduce(lmax[:, :], lg[:, :, :], AX.X, ALU.max), "route")
                wait(dve, it, "route", 4)
                for t in range(T):
                    V.tensor_scalar(oh[:, t, :], lg[:, t, :], lmax[:, t:t + 1], None, ALU.is_equal)
                    ins = V.tensor_scalar(oh12[:, t, :, :], lg[:, t:t + 1, :].broadcast_to([P, 3, E]), lmax[:, t:t + 1], None, ALU.is_equal)
                sig(ins, "onehot")
                wait(dve, it, "ohT_psum", 1)
                sig(V.tensor_copy(ohT[:, :], bank(3)[0:3 * E, 0:S // 2].bitcast(BF16)), "ohT_sbuf")
                for n in range(2):
                    wait(dve, it, "ohT_psum", 2 + n)
                    if n == 0:
                        wait(dve, it, "xT_sbuf", 2)
                    src = bank(4 + n).rearrange("p (e s) -> p e s", e=2)
                    for e in range(2):
                        ins = V.tensor_tensor(XE[:, 2 * n + e, :, :], XT[:, :, :], src[:, e:e + 1, :].broadcast_to([P, C, S]), ALU.mult)
                        sig(ins, "x_expert")
                wait(dve, it, "ffn_psum", 1)
                wait(dve, it, "ffn_base", 1)
                sig(V.tensor_tensor(XN_[:, :, :], bank(6).rearrange("p (t d) -> p t d", t=T), OT[:, :, :], ALU.add), "ffn_sum")
                wait(dve, it, "ffn_sum", 1)
                sig(layernorm(2, XN_, XN_, FFN_EPS, 3), "xn_ready")
                wait(dve, it, "xn_ready", 3)
                sig(V.tensor_tensor(XN_[:, :, :], XN_[:, :, :], rows[:, GAMMA:GAMMA + 1, :].broadcast_to([P, T, D]), ALU.mult), "ffn_scale")
                wait(dve, it, "ffn_scale", 1)
                sig(V.tensor_tensor(XN_[:, :, :], XN_[:, :, :], rows[:, BETA:BETA + 1, :].broadcast_to([P, T, D]), ALU.add), "ffn_scale")
                wait(dve, it, "ffn_scale", 2)
                sig(V.tensor_tensor(X[:, :, :], X[:, :, :], XN_[:, :, :], ALU.add), "x_new")
                wait(dve, it, "x_new", 2)
                sig(layernorm(3, X, XN_, LN_EPS, 4), "xn_ready")
                values(1)
                split(3, 2)
                wait(dve, it, "mask_add", 1)
                attention(1)
                residual(1)
                wait(dve, it, "x_new", 3)
                sig(layernorm(4, X, XN_, LN_EPS, 5), "xn_ready")
                wait(dve, it, "xn_ready", 5)
                sig(V.tensor_reduce(am[:, 0, :], XN_[:, :, :], AX.X, ALU.max, apply_absolute_value=True), "amax")
                wait(dve, it, "amax", 1)
                sig(V.tensor_scalar(am[:, 0, :], am[:, 0, :], BIT_EPS, None, ALU.add), "amax")
                wait(dve, it, "amax", 2)
                V.reciprocal(am[:, 1, :], am[:, 0, :])
                sig(V.tensor_scalar(am[:, 2, :], am[:, 0, :], wscale[:, :], 1.0 / 127.0, ALU.mult, ALU.mult), "amax")
                wait(dve, it, "amax", 3)
                for t in range(T):
                    ins = V.tensor_scalar(XN_[:, t, :], XN_[:, t, :], am[:, 1, t:t + 1], 127.0, ALU.mult, ALU.mult)
                sig(ins, "zq")
                wait(dve, it, "zq", 1)
                sig(V.tensor_scalar(XN_[:, :, :], XN_[:, :, :], 127.0, -128.0, ALU.min, ALU.max), "zq")
                wait(dve, it, "zq", 2)
                sig(V.tensor_scalar(XN_[:, :, :], XN_[:, :, :], ROUND, None, ALU.add), "zq")
                wait(dve, it, "zq", 3)
                sig(V.tensor_scalar(AQ[:, :, :], XN_[:, :, :], -ROUND, None, ALU.add), "aq")
                wait(dve, it, "aT_psum", 1)
                sig(V.tensor_copy(AQT[:, :, :], bank(1)[:, 0:D].bitcast(BF16).rearrange("p (c s) -> p c s", c=C)), "aT_sbuf")
                wait(dve, it, "bit_psum", 1)
                bp = bank(2).rearrange("p (t d) -> p t d", t=T)
                for t in range(T):
                    ins = V.scalar_tensor_tensor(out=XB[:, t, :], in0=bp[:, t, :], scalar=am[:, 2, t:t + 1], in1=X[:, t, :], op0=ALU.mult, op1=ALU.add)
                sig(ins, "out_sbuf")

        @block.tensor
        def _(pe):
            TE = nc.tensor
            pe.wait_ge(const_made, CONSTS)
            pe.wait_ge(w_loaded, 16 * 9)
            for m in range(8):
                if m >= 4:
                    pe.wait_ge(wtr_sbuf, m - 3)
                for c in range(C):
                    for o in range(C):
                        ins = TE.transpose(bank(m % 4)[:, c * D + o * P:c * D + (o + 1) * P], WST[:, m, o, c * P:(c + 1) * P], ident[:, :])
                ins.then_inc(wtr_psum, 1)
            pe.wait_ge(abs_psum, 1)
            TE.matmul(bank(4)[:, 0:1], ones[:, :], wsum, start=True, stop=True).then_inc(abs_psum, 1)
            pe.wait_ge(abs_psum, 3)
            wbps = bank(5)[:, 0:D].bitcast(BF16)
            for c in range(C):
                for o in range(C):
                    ins = TE.transpose(wbps[:, c * D + o * P:c * D + (o + 1) * P], wbbf[:, o, c * P:(c + 1) * P], ident_bf[:, :])
            ins.then_inc(abs_psum, 1)
            pe.wait_ge(setup_dve, 1)
            pe.wait_ge(wtr_sbuf, 8)
            with pe.Fori(0, BATCHES) as it:
                pe.wait_ge(batch_done, it + 1)

                def transpose_tiles(src, dst_bank, name):
                    for c in range(C):
                        for t in range(T):
                            ins = TE.transpose(bank(dst_bank)[:, c * S + t * P:c * S + (t + 1) * P], src[:, t, c * P:(c + 1) * P], ident[:, :])
                    sig(ins, name)

                def project_T(m, src, dst_bank, name):
                    for g in range(C):
                        for c in range(C):
                            ins = TE.matmul(bank(dst_bank)[:, g * S:(g + 1) * S], wT[:, m, c, g * P:(g + 1) * P], src[:, c, :], start=c == 0, stop=c == C - 1)
                    sig(ins, name)

                def project(m, src, dst_bank, name):
                    for t in range(T):
                        for c in range(C):
                            ins = TE.matmul(bank(dst_bank)[:, t * D:(t + 1) * D], src[:, c, t * P:(t + 1) * P], wT[:, m, c, :], start=c == 0, stop=c == C - 1)
                    sig(ins, name)

                def qkv(layer):
                    if layer == 0:
                        wait(pe, it, "ctx_loaded", 16)
                        transpose_tiles(CT, 0, "ctxT_psum")
                    wait(pe, it, "xn_ready", 1 if layer == 0 else 4)
                    transpose_tiles(XN_, 1, "xT_psum")
                    if layer == 0:
                        wait(pe, it, "ctxT_sbuf", 1)
                    project_T(4 * layer + 1, CTT, 3, "k_psum")
                    project(4 * layer + 2, CTT, 4, "v_psum")
                    wait(pe, it, "xT_sbuf", 1 if layer == 0 else 3)
                    project_T(4 * layer, XT, 2, "q_psum")

                def relative_scores():
                    wait(pe, it, "q_stacked", 96)
                    for n in range(8):
                        qt, q0 = n // 4, (n % 4) * 32
                        if n >= 4:
                            wait(pe, it, "rel_sbuf", n - 3)
                        elif n == 3:
                            wait(pe, it, "ctxT_sbuf", 1)
                        ps = bank([5, 6, 7, 0][n % 4])
                        for q in range(q0, q0 + 32):
                            lo = -q - XLO
                            ins = TE.matmul(ps[:, (q - q0) * H:(q - q0 + 1) * H], relk_st[:, 0, lo:lo + P], QS[:, :, qt * P + q], start=q == q0, stop=True, skip_group_check=True)
                        sig(ins, "rel_psum")
                    for n in range(T):
                        ps = bank(1)[0:R, n * 256:(n + 1) * 256]
                        for j in range(R):
                            q = (P - R + j) if n == 0 else (P + j)
                            lo = ((P if n == 0 else P - R) - q) - XLO
                            ins = TE.matmul(ps[:, j * H:(j + 1) * H], relk_st[:, 1 + n, lo:lo + R], QS[:, :, q], start=j == 0, stop=True, skip_group_check=True)
                        sig(ins, "rel_psum")

                def scores(layer, u):
                    qt, h0 = u // (UNITS // T), (u % (UNITS // T)) * UH
                    if u >= 2:
                        if layer == 0:
                            wait(pe, it, "exped", (u - 1) * UH)
                        else:
                            wait(pe, it, "masked", u - 1)
                    sv = PS[:, 2 * (u % 2):2 * (u % 2) + 2, :].rearrange("p b (h s) -> p (b h) s", h=2)
                    for i in range(UH):
                        h = h0 + i
                        q = QS[:, h, qt * P:(qt + 1) * P]
                        if layer == 1:
                            nk = S if qt else P
                            ins = TE.matmul(sv[:, i, 0:nk], q, KS[:, 0, h, 0:nk], start=True, stop=True)
                            continue
                        TE.matmul(sv[:, i, :], q, KS[:, qt, h, :], start=True, stop=False, skip_group_check=True)
                        TE.matmul(sv[:, i, qt * P:(qt + 1) * P], ET[:, qt, h, :], ident[:, :], start=False, stop=False, is_transpose=True, skip_group_check=True)
                        q0, k0 = (P - 2 * R, P) if qt == 0 else (0, P - R)
                        ins = TE.matmul(sv[q0:q0 + 2 * R, i, k0:k0 + R], EC[:, qt, h, :], ident[0:R, 0:R], start=False, stop=True, skip_group_check=True)
                    sig(ins, "scores")

                def probs_T(layer, p):
                    qt, hp = p // (PAIRS // T), p % (PAIRS // T)
                    n = p + qt
                    u = p // 2
                    wait(pe, it, "exped", layer * UNITS * UH + 2 * (p + 1))
                    if n >= 2:
                        wait(pe, it, "wT_sbuf", layer * SLOTS + n - 1)
                    nk = T if layer == 0 or qt else 1
                    for i in range(2):
                        for kt in range(nk):
                            ins = TE.transpose(bank(4 + n % 2)[:, (i * T + kt) * P:(i * T + kt + 1) * P],
                                               W[:, u % 2, 2 * (p % 2) + i, kt * P:(kt + 1) * P], ident[:, :])
                    sig(ins, "wT_psum")

                def weigh_values(layer, p):
                    qt, hp = p // (PAIRS // T), p % (PAIRS // T)
                    wait(pe, it, "wT_sbuf", layer * SLOTS + p + qt + 1)
                    nk = T if layer == 0 or qt else 1
                    g, row = hp // 4, 32 * (hp % 4)
                    ps = bank(6)[row:row + 32, qt * D + g * P:qt * D + (g + 1) * P]
                    for i in range(2):
                        h = 2 * hp + i
                        for kt in range(nk):
                            moved = 1 if layer == 0 and kt != qt else 0
                            ins = TE.matmul(ps, V2[:, moved, kt, h, :], WT_[:, qt, kt, h, :], start=i == 0 and kt == 0, stop=i == 1 and kt == nk - 1, skip_group_check=True)
                    if hp == PAIRS // T - 1:
                        sig(ins, "pv_psum")

                def relative_values(qt):
                    if qt == 1:
                        wait(pe, it, "relv_sbuf", 1)
                    for j in range(4):
                        for i in range(32):
                            q = 32 * j + i
                            seam = q >= P - R if qt == 0 else q < R
                            ps = bank(7)[32 * j:32 * j + 32, i * H:(i + 1) * H]
                            s = P - 1 - q
                            ins = TE.matmul(ps, relv_d[:, s:s + 2, :].rearrange("p s d -> p (s d)"), WT_[:, qt, qt, :, q], start=i == 0, stop=not seam, skip_group_check=True)
                            if seam:
                                s = (P - 1 if qt == 0 else R - 1) - q
                                ins = TE.matmul(ps, relv_o[:, qt, s:s + 2, :].rearrange("p s d -> p (s d)"), WT_[:, qt, 1 - qt, :, q], start=False, stop=True, skip_group_check=True)
                    sig(ins, "relv_psum")

                def inverse_T(layer, qt):
                    n = (qt + 1) * (PAIRS // T) + qt
                    wait(pe, it, "rinv", layer * T + qt + 1)
                    wait(pe, it, "wT_sbuf", layer * SLOTS + n - 1)
                    for g in range(C):
                        hs = H // C
                        ins = TE.transpose(bank(4 + n % 2)[:, g * P:(g + 1) * P],
                                           rinv[:, qt, g * hs:(g + 1) * hs, :].rearrange("p h d -> p (h d)"), ident[:, :])
                    sig(ins, "wT_psum")

                def attention(layer):
                    wait(pe, it, "q_stacked", 96 * (layer + 1))
                    wait(pe, it, "k_stacked", 192 if layer == 0 else 288)
                    wait(pe, it, "v_sbuf", 4 if layer == 0 else 6)
                    if layer == 0:
                        wait(pe, it, "rel_sbuf", 10)
                    for u in range(UNITS + 1):
                        if u < UNITS:
                            scores(layer, u)
                        if u >= 1:
                            v = u - 1
                            probs_T(layer, 2 * v)
                            if v % 4:
                                weigh_values(layer, 2 * v - 1)
                            probs_T(layer, 2 * v + 1)
                            weigh_values(layer, 2 * v)
                            if v % 4 == 3:
                                weigh_values(layer, 2 * v + 1)
                                if layer == 0:
                                    relative_values(v // 4)
                                inverse_T(layer, v // 4)

                def output(layer):
                    wait(pe, it, "oT", layer * T + T)
                    for t in range(T):
                        for c in range(C):
                            ins = TE.matmul(bank(0)[:, t * D:(t + 1) * D], OT[:, c, t * P:(t + 1) * P], wT[:, 4 * layer + 3, c, :], start=c == 0, stop=c == C - 1)
                        sig(ins, "y_psum")

                def ffn():
                    wait(pe, it, "xn_ready", 2)
                    transpose_tiles(XN_, 1, "xT_psum")
                    wait(pe, it, "xT_sbuf", 2)
                    for t in range(T):
                        for c in range(C):
                            ins = TE.matmul(bank(2)[:, t * E:(t + 1) * E], XT[:, c, t * P:(t + 1) * P], wr[:, c, :], start=c == 0, stop=c == C - 1)
                    sig(ins, "logits")
                    wait(pe, it, "onehot", 1)
                    ps = bank(3)[0:3 * E, 0:S // 2].bitcast(BF16)
                    for t in range(T):
                        ins = TE.transpose(ps[:, t * P:(t + 1) * P], oh12[:, t, :, :].rearrange("p a e -> p (a e)"), ident_bf[:, :])
                    sig(ins, "ohT_psum")
                    for n in range(2):
                        for e in range(2):
                            for t in range(T):
                                ins = TE.transpose(bank(4 + n)[:, e * S + t * P:e * S + (t + 1) * P],
                                                   oh[:, t, 2 * n + e:2 * n + e + 1].broadcast_to([P, P]), ident[:, :])
                        sig(ins, "ohT_psum")
                    wait(pe, it, "ohT_sbuf", 1)
                    wait(pe, it, "x_expert", E)
                    for i in range(IC):
                        if i % 2 == 0 and i >= 4:
                            wait(pe, it, "gelu", i // 2 - 1)
                        ps = bank((i // 2) % 2)[:, (i % 2) * S:(i % 2 + 1) * S]
                        TE.matmul(ps, b1p[:, i * P:(i + 1) * P], ohT[:, :], start=True, stop=False)
                        for e in range(E):
                            for c in range(C):
                                ins = TE.matmul(ps, w1[:, e, c, i * P:(i + 1) * P], XE[:, e, c, :], start=False, stop=e == E - 1 and c == C - 1)
                        if i % 2:
                            sig(ins, "h_psum")
                    wait(pe, it, "gelu", IC // 2)
                    for t in range(T):
                        for i in range(IC):
                            ins = TE.matmul(bank(6)[:, t * D:(t + 1) * D], GT[:, i, t * P:(t + 1) * P], wf[:, i, :], start=i == 0, stop=i == IC - 1)
                    sig(ins, "ffn_psum")

                def bitlinear():
                    wait(pe, it, "aq", 1)
                    ps = bank(1)[:, 0:D].bitcast(BF16)
                    for c in range(C):
                        for t in range(T):
                            ins = TE.transpose(ps[:, c * S + t * P:c * S + (t + 1) * P], AQ[:, t, c * P:(c + 1) * P], ident_bf[:, :])
                    sig(ins, "aT_psum")
                    wait(pe, it, "aT_sbuf", 1)
                    for t in range(T):
                        for c in range(C):
                            ins = TE.matmul(bank(2)[:, t * D:(t + 1) * D], AQT[:, c, t * P:(t + 1) * P], wbT[:, c, :], start=c == 0, stop=c == C - 1)
                    sig(ins, "bit_psum")

                qkv(0)
                relative_scores()
                attention(0)
                output(0)
                ffn()
                qkv(1)
                attention(1)
                output(1)
                bitlinear()

        assert raised == PER, [(n, raised[n], PER[n]) for n in PER if raised[n] != PER[n]]


_INS = ["x", "ctx_1024", "mask_BxSxS2_bf0", "L0_xattn_Wq", "L0_xattn_bq", "L0_xattn_Wk", "L0_xattn_bk", "L0_xattn_Wv",
        "L0_xattn_bv", "L0_xattn_Wo", "L0_xattn_bo", "L0_xattn_rel_k_table", "L0_xattn_rel_v_table", "L0_ffn_W_router",
        "L0_ffn_W1", "L0_ffn_b1", "L0_ffn_Wo", "L0_ffn_bo", "L0_ffn_ln_gamma", "L0_ffn_ln_beta", "L1_xattn_Wq",
        "L1_xattn_Wk", "L1_xattn_Wv", "L1_xattn_Wout", "L1_xattn_b_out", "L1_ffn_weight"]


def kernel(**inputs):
    import concourse.bacc as bacc
    from concourse.bass_utils import run_bass_kernel_spmd

    nc = bacc.Bacc("TRN2", target_bir_lowering=False, num_devices=1)
    arrays, args = {}, []
    for name in _INS:
        a = np.ascontiguousarray(inputs[name])
        arrays[f"in_{name}"] = a
        args.append(nc.dram_tensor(f"in_{name}", a.shape, mybir.dt.from_np(a.dtype), kind="ExternalInput").ap())
    args.append(nc.dram_tensor("out", (B, S, D), F32, kind="ExternalOutput").ap())
    _program(nc, *args)
    return run_bass_kernel_spmd(nc, [arrays], core_ids=[0]).results[0]["out"]
```

```python
from contextlib import ExitStack

import numpy as np

import concourse.bass as bass
from concourse import mybir

F32 = mybir.dt.float32
BF16 = mybir.dt.bfloat16
U8 = mybir.dt.uint8
ALU = mybir.AluOpType
ACT = mybir.ActivationFunctionType
AX = mybir.AxisListType

P = 128
B, S, D = 8, 256, 256
H = 16
DK = D // H
T = S // P
C = D // P
E, I = 4, 1024
IC = I // P
R = 16
NREL = 2 * R + 1
XLO = -(P + R)
XN = 2 * (P + R)
MASKED = -1.0e30
LN_EPS = 1e-5
FFN_EPS = 1e-12
BIT_EPS = 1e-8
ROUND = 1.5 * 2.0 ** 23

QPART = [0, 0, 1, 0, 2, 1]
KPART = [0, 1, 0, 2, 0, 1]
STACK = len(QPART) * DK

PAIRS = 16
QPAIRS = PAIRS // T
SLOTS = PAIRS + T
INV_SLOT = [QPAIRS + 1, SLOTS - 1]
W_RING = 3

PER_A = {
    "x_loaded": 16, "ctx_loaded": 16, "stats": 4, "rstd": 1, "xn_ready": 1, "base": 1, "ctx_copied": 1,
    "ctxT_psum": 1, "ctxT_sbuf": 1, "xT_psum": 1, "xT_sbuf": 1, "q_psum": 1, "k_psum": 1, "v_psum": 1, "v_sbuf": 4,
    "f32_ready": 3, "part1": 3, "resid": 3, "part2": 3, "part3": 3,
    "q_written": 16, "k0_written": 16, "k1_written": 16, "q_stacked": 96, "k_stacked": 192, "rel_psum": 9, "rel_sbuf": 9 + T - 1,
    "scores": PAIRS, "negmax": PAIRS, "exped": 2 * PAIRS, "wT_psum": SLOTS, "wT_sbuf": SLOTS, "pv_psum": T, "rinv": T,
    "relv_psum": T, "relv_sbuf": T, "relv_written": T * 64, "relv_loaded": T * 16,
    "o_sum": 1, "oT": 1, "y_psum": 1, "x1_ready": 1,
}
PER_B = {
    "stats": 4 * 4, "rstd": 4, "xn_ready": 4, "ffn_base": 1, "base": 1, "xT_psum": 2, "xT_sbuf": 2,
    "logits": 1, "route": 4, "onehot": 1, "ohT_psum": 3, "ohT_sbuf": 1, "x_expert": E, "h_psum": IC // 2, "gelu": IC // 2,
    "ffn_psum": 1, "ffn_sum": 1, "ffn_scale": 2, "x2_ready": 1,
    "q_psum": 1, "k_psum": 1, "v_psum": 1, "v_sbuf": 2,
    "f32_ready": 2, "part1": 2, "resid": 2, "part2": 2, "part3": 2,
    "k_written": 16, "q_written": 16, "q_stacked": 96, "k_stacked": 96,
    "mask_loaded": 16, "mask_scaled": 1, "mask_ready": T,
    "scores": PAIRS, "masked": PAIRS, "negmax": PAIRS, "exped": 2 * PAIRS, "wT_psum": SLOTS, "wT_sbuf": SLOTS,
    "weighed": PAIRS, "inverted": T, "rinv": T, "oT": 1, "y_psum": 1, "x3_ready": 1,
    "amax": 3, "zq": 3, "aq": 1, "aT_psum": 1, "aT_sbuf": 1, "bit_psum": 1, "out_sbuf": 1, "stored": 16,
}

def attention_steps(thread):
    out = []
    for p in range(PAIRS):
        out.append(("S", p))
        if p == QPAIRS + 2 and thread == "A":
            out += [("W", p - 3)] + [("R", j) for j in range(4)] + [("T", p - 2), ("I", 0)]
            continue
        out += [("T", p - 2)] if p >= 2 else []
        out += [("W", p - 3)] if p >= 3 else []
        out += [("I", 0)] if p == QPAIRS + 2 else []
    out += [("T", PAIRS - 2), ("W", PAIRS - 3), ("T", PAIRS - 1), ("W", PAIRS - 2), ("W", PAIRS - 1)]
    return out + ([("R", 4 + j) for j in range(4)] if thread == "A" else []) + [("I", 1)]


FFN_START = {("S", 0): [("mask", 0), ("stats", 0), ("normed", 0)], ("S", 1): [("ffn_xT", 0)], ("S", 2): [("router", 0)],
             ("T", 1): [("onehot_T", 0), ("experts", 0)], ("S", 4): [("experts", 1), ("mask", 1)]}
BESIDE = [[("B", "up", n)] + ([("B", "gelu", n // 4 - 1)] if n % 4 == 0 and n else []) for n in range(2 * IC)]
BESIDE += [[("B",) + s for s in group] for group in (
    [("down", 0), ("gelu", 3)], [("down", 1)], [("down", 2)], [("down", 3), ("l1_k", 0)], [("ffn_sum", 0), ("l1_v", 0), ("l1_f32", 0)],
    [("ffn_end", 0)], [("l1_parts", 0)], [("stats", 2)], [("normed", 2)], [("l1_stack", 0), ("l1_xT", 0)])]
BESIDE += [[("A", "copy", 0), ("P", "ctxT", 0)], [("B", "l1_q", 0), ("P", "stats", 0)], [("B", "l1_f32", 1), ("P", "normed", 0)],
           [("B", "l1_parts", 1), ("P", "xT", 0)], [("P", "q", 0)], [("B", "l1_stack", 1)],
           [("P", "f32", 0)], [("P", "parts", 0)], [("P", "k", 0)], [("P", "f32", 1)], [("P", "q_stack", 0), ("P", "parts", 1)]]
LATER = [("P", "parts", 2), ("P", "k_stack", 0), ("P", "v", 0)]
RELATIVE = [("P", "rel", n) for n in range(9)]


def order(with_a, with_b, with_prep):
    there = {"A": with_a, "B": with_b, "P": with_prep}
    out = [("P", "load", 0)]
    groups, started, last = list(BESIDE), False, False
    for step in attention_steps("A"):
        out.append(("A",) + step)
        out += [("B",) + s for s in FFN_START.get(step, [])]
        started = started or step == ("S", 4)
        last = last or step == ("S", PAIRS - 1)
        if started and groups and (last or groups[0] != [("P", "f32", 0)]):
            out += groups.pop(0)
    out += [s for group in groups for s in group]
    out += [("P", "f32", 2)] + RELATIVE[:2]
    rest = LATER + RELATIVE[2:]
    steps = [("B", "l1_" + s, n) for s, n in attention_steps("B")]
    for at, step in enumerate(steps):
        out.append(step)
        if at == 1:
            out += [("A", "finish", 0), ("A", "output", 0), ("P", "base", 0)]
        if step[1] == "l1_S" and step[2] > 0 and rest:
            out.append(rest.pop(0))
    out += [("B", "l1_finish", 0), ("B", "l1_output", 0)]
    out += [("B", s, n) for s, n in [("stats", 3), ("normed", 3), ("quantise", 0), ("bit_T", 0), ("bit", 0)]] + rest
    return [s for s in out if there[s[0]]]


def slot(n_pair):
    return n_pair + (1 if n_pair > QPAIRS else 0)


def _program(nc, x, ctx_in, mask, Wq0, bq0, Wk0, bk0, Wv0, bv0, Wo0, bo0, relk, relv,
             Wr, W1, b1, Wf, bf, gamma, beta, Wq1, Wk1, Wv1, Wo1, bo1, Wb, out):
    with ExitStack() as stack:
        def sb(name, shape, dt=F32):
            return stack.enter_context(nc.sbuf_tensor(name, shape, dt))

        def dram(name, shape, dt=F32):
            return nc.dram_tensor(name, shape, dt, kind="Internal").ap()

        def new_sem(name):
            return stack.enter_context(nc.semaphore(name))

        ident = sb("ident", [P, P])
        ident_bf = sb("ident_bf", [P, P], BF16)
        wT = sb("wT", [P, 8, C, D])
        wr = sb("wr", [P, C, E])
        w1 = sb("w1", [P, E, C, I])
        wf = sb("wf", [P, IC, D])
        wbT = sb("wbT", [P, C, D], BF16)
        wscale = sb("wscale", [P, 1])
        rows = sb("rows", [P, 8, D])
        BV_D, BV_O0, BV_O1, BO0, BF_, GAMMA, BETA, BO1 = range(8)
        chb = sb("chb", [P, 6, C])
        relk_st = sb("relk_st", [STACK, 3, XN], BF16)
        relv_d = sb("relv_d", [P, P + 1, DK])
        relv_o = sb("relv_o", [P, T, R + 1, DK])
        halfs = sb("halfs", [P, T])
        firsts = sb("firsts", [P, T, E])
        low_rows = sb("low_rows", [64, T * H * 2 * R])
        b1p = low_rows[0:3 * E, :].bitcast(BF16)[:, 0:I]
        EC0 = 2 * R
        EC = low_rows[EC0:EC0 + R, :].rearrange("p (t h s) -> p t h s", t=T, h=H)

        X = sb("X", [P, T, D])
        CT = sb("CT", [P, T, D])
        CTT = sb("CTT", [P, C, S])
        XT = sb("XT", [P, C, S])
        XO = sb("XO", [P, T, D])
        QS = sb("QS", [STACK, H, S], BF16)
        KS = sb("KS", [STACK, T, H, S], BF16)
        V2 = sb("V2", [P, 2, T, H, 2 * DK])
        ET = sb("ET", [P, T, H, P])

        Y = sb("Y", [P, T, D])
        Z = sb("Z", [P, T, D])
        FB = sb("FB", [P, T, D])
        XNB = sb("XNB", [P, T, D])
        XTB = sb("XTB", [P, C, S])
        CTB = sb("CTB", [P, C, S])
        MK = sb("MK", [P, T, S], U8)
        MA = sb("MA", [P, T, S])
        V2B = sb("V2B", [P, T, H, 2 * DK])
        q1_mem = sb("q1_mem", [P, 2048])
        k1_mem = sb("k1_mem", [P, 2048])
        QSB = q1_mem[0:STACK, :].bitcast(BF16).rearrange("p (h s) -> p h s", h=H)
        KSB = k1_mem[0:STACK, :].bitcast(BF16).rearrange("p (h s) -> p h s", h=H)
        XE = k1_mem[:, :].rearrange("p (e c s) -> p e c s", e=E, c=C)
        GT = q1_mem[:, :].rearrange("p (i s) -> p i s", i=IC)
        AQ = q1_mem[:, 0:256].bitcast(BF16).rearrange("p (t d) -> p t d", t=T)
        AQT = q1_mem[:, 256:512].bitcast(BF16).rearrange("p (c s) -> p c s", c=C)

        W = sb("W", [P, W_RING, 2, S])
        wt_mem = sb("wt_mem", [P, 4096])
        WT_ = wt_mem[:, :].rearrange("p (k h q) -> p k h q", k=T, h=H)
        WTB = wt_mem[:, 0:1024].rearrange("p (a k h q) -> p a k h q", a=2, k=T, h=2)
        SM = wt_mem[:, 1024:2048].rearrange("p (a h s) -> p a h s", a=2, h=2)
        RT = sb("RT", [P, T, C, P])
        RV = sb("RV", [P, H, 2 * R])
        OT = sb("OT", [P, C, S])
        rinv = sb("rinv", [P, H, DK])

        small = {}
        for th, n_pairs in (("A", 1), ("B", 1)):
            small[th] = dict(st6=sb("st6" + th, [P, T, 6]), mv=sb("mv" + th, [P, T, 2]), ve=sb("ve" + th, [P, T]), rs=sb("rs" + th, [P, T]),
                             nm=sb("nm" + th, [P, 2 * PAIRS]), sums=sb("sums" + th, [P, T, H]))
        small["P"] = small["A"]
        mx = sb("mx", [P, 2 * PAIRS])
        oh = sb("oh", [P, T, E])
        lg = sb("lg", [P, T, E])
        lmax = sb("lmax", [P, T])
        gate = sb("gate", [P, 1])
        oh12 = sb("oh12", [P, T, 3, E], BF16)
        ohT = sb("ohT", [3 * E, S], BF16)
        hold = sb("hold", [P, 1])
        am = sb("am", [P, 3, T])
        wsum = sb("wsum", [P, 2])

        def split_room(mem, at):
            return (mem[:, at:at + C * S].rearrange("p (c s) -> p c s", c=C), mem[:, at + C * S:at + 2 * C * S].rearrange("p (c s) -> p c s", c=C),
                    mem[:, at + 2 * C * S:at + 7 * C * S // 2].bitcast(BF16).rearrange("p (i c s) -> p i c s", i=3, c=C))
        et_mem = ET[:, :, :, :].rearrange("p t h q -> p (t h q)")
        room_a = [split_room(et_mem, 0), split_room(et_mem, 7 * C * S // 2), split_room(wt_mem[:, :], 2048)]
        room_b = [split_room(q1_mem[:, :], 0)] * 2

        PS = stack.enter_context(nc.psum_tensor("PS", [P, 8, 512], F32))
        PW0, PO, RVB, FB0, FB1 = 2, 4, 5, 6, 7

        def bank(n):
            return PS[:, n, :]

        def halves(n, a=C):
            return bank(n).rearrange("p (c s) -> p c s", c=a)

        scr = {"A": dict(q=dram("q_scr", (3, C, P, S), BF16), k=[dram(f"k_scr{v}", (3, C, P, S), BF16) for v in range(T)]),
               "B": dict(q=dram("qb_scr", (3, C, P, S), BF16), k=[dram("kb_scr", (3, C, P, S), BF16)])}
        rv_scr = dram("rv_scr", (T, H, DK, P))
        relv_small = dram("relv_small", (3, NREL, DK))
        relv_pad = dram("relv_pad", (3, XN, DK))

        sems = {("A", n): new_sem("a_" + n) for n in PER_A}
        sems.update({("B", n): new_sem("b_" + n) for n in PER_B})
        PER = {k: (PER_A if k[0] == "A" else PER_B)[k[1]] for k in sems}
        SHIFT = {"A": 0, "P": 1, "B": -1, "a": -1, "b": -2}
        raised = dict.fromkeys(PER, 0)
        batches_setup = new_sem("setup_pool")
        w_loaded, aux_loaded, const_made = new_sem("w_loaded"), new_sem("aux_loaded"), new_sem("const_made")
        big_loaded, sync_passed = new_sem("big_loaded"), new_sem("sync_passed")
        wtr_psum, wtr_sbuf = new_sem("wtr_psum"), new_sem("wtr_sbuf")
        rel_step, rel_dma, setup_dve = new_sem("rel_step"), new_sem("rel_dma"), new_sem("setup_dve")
        relk_done, relv_tab, abs_psum, setup_act = new_sem("relk_done"), new_sem("relv_tab"), new_sem("abs_psum"), new_sem("setup_act")

        def sem_of(thread, name):
            return ("B" if thread in "Bb" else "A", name)

        def sig(ins, thread, name, by=1):
            ins.then_inc(sems[sem_of(thread, name)], by)
            raised[sem_of(thread, name)] += by

        def waiter(eng, it, off, carrier=None):
            def wait(thread, *names, n=None):
                for name in names:
                    key = sem_of(thread, name)
                    per = PER[key]
                    value = (off + SHIFT[thread] + (1 if key[0] == "B" else 0)) * per + (per if n is None else n)
                    assert n is None or 0 < n <= per, (key, n)
                    if isinstance(it, int):
                        if 0 <= it + off + SHIFT[thread] < B:
                            eng.wait_ge(sems[key], it * per + value)
                    else:
                        assert value > 0, (key, value)
                        eng.wait_ge(sems[key], it * per + value)
                        if carrier is not None:
                            eng.nop().then_inc(carrier, 1)
            return wait

        def iterations(eng, body, before_loop=None):
            body(0, -1, order(False, False, True), False)
            body(0, 0, order(True, False, True), True)
            if before_loop:
                before_loop()
            with eng.Fori(0, B - 2) as it:
                body(it, 1, order(True, True, True), True)
            body(0, B - 1, order(True, True, False), True)
            body(0, B, order(False, True, False), False)

        k1f = k1_mem[:, :]
        rk = k1f[0:DK, 0:NREL]
        rkd = k1f[0:DK, 64:64 + 3 * NREL].rearrange("p (a b) -> p a b", a=3)
        rkpad = et_mem[0:DK, 2048:2048 + 3 * XN].rearrange("p (a b) -> p a b", a=3)
        rkres = et_mem[0:DK, 2048 + 3 * XN:2048 + 6 * XN].rearrange("p (a b) -> p a b", a=3)
        rkP = [KS[0:DK, :, :, :].rearrange("p t h s -> p (t h s)")[:, i * 3 * XN:(i + 1) * 3 * XN].rearrange("p (a b) -> p a b", a=3) for i in range(3)]
        rv3 = Z[0:NREL, 0, 0:3 * DK].rearrange("p (a d) -> p a d", a=3)
        rvb = Z[0:NREL, 1, 0:2 * DK].rearrange("p (a d) -> p a d", a=2)
        rvrow = OT[:, 0, 0:2 * DK].rearrange("p (a d) -> p a d", a=2)
        b1v = [et_mem[0:E, i * I:(i + 1) * I] for i in range(2)]
        b1bf = [QS[0:E, 4 * i:4 * i + 4, :].rearrange("p h s -> p (h s)") for i in range(3)]
        wb = CTB[:, :, :]
        wbq = XTB[:, :, :]
        wbbf = AQ
        ones = W[:, 0, 0, 0:P]
        WST = wt_mem[:, :].rearrange("p (m o d) -> p m o d", m=8, o=C)

        block = stack.enter_context(nc.Block())
        AUX = 16 * (6 + 2 * (2 + P // DK) + 2 * C + 4)
        CONSTS = 7 + 1 + T * E

        def setup_over(eng):
            eng.wait_ge(batches_setup, 1)
            eng.wait_ge(setup_dve, 1)
            eng.wait_ge(wtr_sbuf, 8)

        @block.sync
        def _(sp):
            for m, w in enumerate([Wq0, Wk0, Wv0, Wo0, Wq1, Wk1, Wv1, Wo1]):
                sp.dma_start(WST[:, m, :, :], w.rearrange("(o p) d -> p o d", p=P)).then_inc(w_loaded, 16)
            sp.dma_start(wb, Wb.rearrange("(o p) d -> p o d", p=P)).then_inc(w_loaded, 16)
            sp.wait_ge(rel_step, 1)
            for a in range(3):
                sp.dma_start(relv_small[a], rv3[:, a, :]).then_inc(rel_dma, 16)
            sp.wait_ge(rel_dma, 48)
            low, mid = -R - XLO + 1, NREL - 2
            for a in range(3):
                sp.dma_start(relv_pad[a, 0:low, :], relv_small[a, 0:1, :].broadcast_to([low, DK])).then_inc(rel_dma, 16)
                sp.dma_start(relv_pad[a, low:low + mid, :], relv_small[a, 1:1 + mid, :]).then_inc(rel_dma, 16)
                sp.dma_start(relv_pad[a, low + mid:XN, :], relv_small[a, NREL - 1:NREL, :].broadcast_to([XN - low - mid, DK])).then_inc(rel_dma, 16)
            sp.wait_ge(rel_dma, 48 + 144)

            def toeplitz(a, first, n):
                return bass.AP(relv_pad.tensor, (a * XN + first) * DK, [[DK, P], [1, n * DK]])
            sp.dma_start(relv_d[:, :, :].rearrange("p s d -> p (s d)"), toeplitz(0, -(P - 1) - XLO, P + 1)).then_inc(relv_tab, 16)
            sp.dma_start(relv_o[:, 0, :, :].rearrange("p s d -> p (s d)"), toeplitz(1, 1 - XLO, R + 1)).then_inc(relv_tab, 16)
            sp.dma_start(relv_o[:, 1, :, :].rearrange("p s d -> p (s d)"), toeplitz(2, -(P + R - 1) - XLO, R + 1)).then_inc(relv_tab, 16)
            sp.wait_ge(relk_done, 1)
            for j, part in enumerate(KPART):
                sp.dma_start(relk_st[j * DK:(j + 1) * DK, :, :], rkP[part]).then_inc(relv_tab, 16)
            for i in range(3):
                sp.dma_start(b1p[i * E:(i + 1) * E, :], b1bf[i]).then_inc(relv_tab, 16)
            sp.wait_ge(relv_tab, 16 * 12)

            def body(it, off, steps, with_a):
                wait = waiter(sp, it, off, sync_passed)

                def batch_of(t, thread):
                    first = off + SHIFT[thread]
                    return (t[first:B] if first else t)[bass.ds(it, 1)] if not isinstance(it, int) else t[first:first + 1]

                def tiles(ap):
                    return ap.rearrange("o (t p) d -> p (o t) d", p=P)

                def write(thread, kind, room, dst, o, done):
                    wait(thread, "part2", "part3", n=o + 1)
                    if o < 2 or thread == "B":
                        wait({"P": "A", "B": "b"}[thread], kind + "_stacked")
                    sig(sp.dma_start(dst.rearrange("i g p t -> p (i g) t"), room[2].rearrange("p i g t -> p (i g) t")), thread, done, 16)

                def stack_up(thread, kind, src, dst):
                    for j, part in enumerate(QPART if kind == "q" else KPART):
                        sig(sp.dma_start(dst[j * DK:(j + 1) * DK, :, :], src[part].rearrange("g (h d) t -> d (g h) t", d=DK)), thread, kind + "_stacked", 16)

                for thread, step, n in steps:
                    if (thread, step) == ("P", "load"):
                        wait("A", "xT_psum")
                        sig(sp.dma_start(CT[:, :, :], tiles(batch_of(ctx_in, "P"))), "P", "ctx_loaded", 16)
                        wait("A", "base")
                        sig(sp.dma_start(X[:, :, :], tiles(batch_of(x, "P"))), "P", "x_loaded", 16)
                    elif (thread, step) == ("P", "parts"):
                        kind, v = [("q", 0), ("k", 0), ("k", 1)][n]
                        write("P", kind, room_a[n], scr["A"]["k"][v] if kind == "k" else scr["A"]["q"], n, ("q_written", "k0_written", "k1_written")[n])
                    elif (thread, step) == ("P", "k_stack"):
                        for v in range(T):
                            wait("P", f"k{v}_written")
                            stack_up("P", "k", scr["A"]["k"][v], KS[:, v, :, :])
                    elif (thread, step) == ("P", "q_stack"):
                        wait("P", "q_written")
                        stack_up("P", "q", scr["A"]["q"], QS[:, :, :])
                    elif (thread, step) == ("A", "R") and n % 4 == 3:
                        qt = n // 4
                        wait("A", "relv_sbuf", n=qt + 1)
                        if qt == 0:
                            wait("a", "relv_loaded")
                        for j in range(4):
                            sig(sp.dma_start(rv_scr[qt].rearrange("h d q -> d h q")[:, :, j * 2 * R:(j + 1) * 2 * R],
                                             RV[2 * R * j:2 * R * j + DK, :, :]), "A", "relv_written", 16)
                        wait("A", "relv_written", n=64 * (qt + 1))
                        if qt == 0:
                            wait("a", "y_psum")
                            wait("b", "y_psum")
                        sig(sp.dma_start(OT[:, :, qt * P:(qt + 1) * P], rv_scr[qt].rearrange("(g h) d q -> (h d) g q", g=C)), "A", "relv_loaded", 16)
                    elif (thread, step) == ("B", "mask") and n == 0:
                        wait("b", "mask_scaled")
                        sig(sp.dma_start(MK[:, :, :], tiles(batch_of(mask, "B"))), "B", "mask_loaded", 16)
                    elif (thread, step) == ("B", "l1_parts"):
                        write("B", "kq"[n], room_b[n], scr["B"]["k"][0] if n == 0 else scr["B"]["q"], n, "kq"[n] + "_written")
                    elif (thread, step) == ("B", "l1_stack"):
                        if n == 0:
                            wait("B", "k_written")
                            wait("B", "h_psum")
                        else:
                            wait("B", "q_written")
                        stack_up("B", "kq"[n], scr["B"]["k"][0] if n == 0 else scr["B"]["q"], (KSB, QSB)[n])
                    elif (thread, step) == ("B", "bit"):
                        wait("B", "out_sbuf")
                        sig(sp.dma_start(tiles(batch_of(out, "B")), FB[:, :, :]), "B", "stored", 16)
            iterations(sp, body)
            sp.wait_ge(sems["B", "stored"], (1 + B) * 16)

        @block.gpsimd
        def _(pool):
            G = nc.gpsimd
            G.memset(ident[:, :], 0.0).then_inc(const_made, 1)
            G.memset(ones, 1.0).then_inc(const_made, 1)
            G.memset(halfs[:, :], -0.5).then_inc(const_made, 1)
            G.memset(V2[:, :, :, :, :], 0.0).then_inc(const_made, 1)
            G.memset(V2B[:, :, :, :], 0.0).then_inc(const_made, 1)
            pool.wait_ge(const_made, 5)
            G.memset(EC, 0.0).then_inc(const_made, 1)
            pool.wait_ge(const_made, 6)
            G.affine_select(out=ident[:, :], in_=ident[:, :], compare_op=ALU.not_equal, fill=1.0, base=0,
                            pattern=[[-1, P]], channel_multiplier=1).then_inc(const_made, 1)
            pool.wait_ge(const_made, 7)
            G.tensor_copy(ident_bf[:, :], ident[:, :]).then_inc(const_made, 1)
            for t in range(T):
                for e in range(E):
                    G.memset(firsts[:, t, e:e + 1], float(E - e)).then_inc(const_made, 1)
            for a, r in enumerate([0, NREL - 1]):
                pool.dma_start(rvrow[:, a, :], relv[r].partition_broadcast(P)).then_inc(aux_loaded, 16)
                pool.dma_start(rvb[:, a, :], relv[r].partition_broadcast(NREL)).then_inc(aux_loaded, 16)
                for h in range(P // DK):
                    pool.dma_start(chb[h * DK:(h + 1) * DK, 2 + a, 0:1], relk[r].rearrange("(d o) -> d o", o=1)).then_inc(aux_loaded, 16)
            pool.dma_start(rk, relk.rearrange("r d -> d r"), allow_slow_non_contiguous=True).then_inc(aux_loaded, 16)
            pool.dma_start(rv3[:, 0, :], relv).then_inc(aux_loaded, 16)
            pool.dma_start(b1v[0], b1).then_inc(aux_loaded, 16)
            for g in range(C):
                for a, b_ in enumerate([bq0, bk0]):
                    pool.dma_start(chb[:, a, g:g + 1], b_[g * P:(g + 1) * P].rearrange("(p o) -> p o", o=1)).then_inc(aux_loaded, 16)
            for row, src in [(BV_D, bv0), (BO0, bo0), (BF_, bf), (GAMMA, gamma), (BETA, beta), (BO1, bo1)]:
                pool.dma_start(rows[:, row, :], src.partition_broadcast(P)).then_inc(aux_loaded, 16)
            pool.dma_start(wr[:, :, :], Wr.rearrange("(c p) e -> p c e", p=P)).then_inc(aux_loaded, 16)
            pool.dma_start(w1[:, :, :, :], W1.rearrange("e (c p) i -> p e c i", p=P)).then_inc(big_loaded, 16)
            pool.dma_start(wf[:, :, :], Wf.rearrange("(i p) d -> p i d", p=P)).then_inc(big_loaded, 16)
            pool.wait_ge(aux_loaded, AUX)
            pool.wait_ge(const_made, CONSTS)
            for n, times in PER_B.items():
                pool.nop().then_inc(sems["B", n], times)
            pool.nop().then_inc(batches_setup, 1)
            setup_over(pool)

            def body(it, off, steps, with_a):
                wait = waiter(pool, it, off)

                def power(thread, n):
                    m = small[thread]
                    wait(thread, "stats", n=4 * (n + 1))
                    sig(G.tensor_tensor(m["rs"][:, :], m["ve"][:, :], halfs[:, :], ALU.pow), thread, "rstd")

                def carry():
                    G.tensor_tensor(hold[:, :], halfs[:, 0:1], halfs[:, 1:2], ALU.add)

                def add_row(dst, src, row):
                    return G.tensor_tensor(dst[:, :, :], src[:, :, :], rows[:, row:row + 1, :].broadcast_to([P, T, D]), ALU.add)

                for thread, step, n in steps:
                    if step == "stats":
                        power(thread, n)
                    elif (thread, step) == ("B", "ffn_sum"):
                        power("B", 1)
                    elif (thread, step) == ("P", "base"):
                        wait("P", "x_loaded")
                        wait("A", "x1_ready")
                        sig(add_row(XO, X, BO0), "P", "base")
                    elif (thread, step) == ("A", "copy"):
                        wait("B", "k_psum", "v_psum")
                        wait("A", "ctxT_sbuf")
                        carry()
                        sig(G.tensor_copy(CTB[:, :, :], CTT[:, :, :]), "A", "ctx_copied")
                    elif (thread, step) == ("B", "ffn_xT"):
                        wait("B", "xn_ready", n=1)
                        wait("b", "stored")
                        sig(add_row(FB, XNB, BF_), "B", "ffn_base")
                    elif (thread, step) == ("B", "ffn_end"):
                        wait("B", "x2_ready")
                        sig(add_row(FB, Z, BO1), "B", "base")
                    elif (thread, step) == ("B", "mask") and n == 1:
                        wait("B", "mask_loaded")
                        wait("b", "masked")
                        carry()
                        sig(G.tensor_scalar(MA[:, :, :], MK[:, :, :], MASKED, None, ALU.mult), "B", "mask_scaled")
                        wait("B", "mask_scaled")
                        carry()
                        for t in range(T):
                            sig(G.affine_select(out=MA[:, t, :], in_=MA[:, t, :], compare_op=ALU.is_ge, fill=MASKED,
                                                base=t * P, pattern=[[-1, S]], channel_multiplier=1), "B", "mask_ready")
            iterations(pool, body)

        @block.scalar
        def _(act):
            A = nc.scalar
            for m in range(8):
                act.wait_ge(wtr_psum, m + 1)
                A.activation(wT[:, m, :, :], halves(m % 4), ACT.Copy).then_inc(wtr_sbuf, 1)
            setup_over(act)

            def body(it, off, steps, with_a):
                wait = waiter(act, it, off)
                other = "A" if with_a else "b"

                def parts(thread, room, o):
                    full, resid, part = room
                    wait(thread, "f32_ready", n=o + 1)
                    sig(A.activation(part[:, 0, :, :], full, ACT.Copy), thread, "part1")
                    wait(thread, "resid", n=o + 1)
                    sig(A.activation(part[:, 1, :, :], resid, ACT.Copy), thread, "part2")

                def exponentials(thread, p):
                    m = small[thread]
                    qt = p // QPAIRS
                    nk = S if thread == "A" or qt else P
                    wait(thread, "negmax", n=p + 1)
                    if p >= W_RING:
                        wait(thread, "wT_psum", n=slot(p - W_RING) + 1)
                    elif p == 0 and thread == "A":
                        wait("a", "wT_psum", "rinv")
                        wait("b", "wT_psum")
                    elif p == 0:
                        wait(other, "wT_psum")
                        wait("b", "rinv")
                    for i in range(2):
                        h = 2 * p + i
                        src = bank(p % 2)[:, i * S:i * S + nk] if thread == "A" else SM[:, p % 2, i, 0:nk]
                        sig(A.activation(W[:, p % W_RING, i, 0:nk], src, ACT.Exp, bias=m["nm"][:, h:h + 1],
                                         scale=1.0 if thread == "A" else DK ** -0.5,
                                         accum_out=m["sums"][:, qt, h % H:h % H + 1]), thread, "exped")

                for thread, step, n in steps:
                    if (thread, step) == ("P", "ctxT"):
                        wait("P", "ctxT_psum")
                        wait("A", "k_psum", "v_psum", "ctx_copied")
                        sig(A.activation(CTT[:, :, :], halves(6), ACT.Copy), "P", "ctxT_sbuf")
                    elif (thread, step) == ("P", "xT"):
                        wait("P", "xT_psum")
                        wait("A", "q_psum")
                        sig(A.activation(XT[:, :, :], halves(6), ACT.Copy), "P", "xT_sbuf")
                    elif (thread, step) == ("P", "f32") and n == 0:
                        wait("P", "q_psum")
                        wait("A", "scores")
                        for g in range(C):
                            ins = A.activation(room_a[0][0][:, g, :], halves(6)[:, g, :], ACT.Identity, bias=chb[:, 0, g:g + 1])
                        sig(ins, "P", "f32_ready")
                    elif (thread, step) == ("P", "f32"):
                        v = n - 1
                        wait("P", "k_psum")
                        if v == 1:
                            wait("A", "relv_psum", "pv_psum")
                        for g in range(C):
                            for kt in range(T):
                                col = 1 if kt == v else (5 if kt > v else 4)
                                ins = A.activation(room_a[n][0][:, g, kt * P:(kt + 1) * P], halves(6)[:, g, kt * P:(kt + 1) * P], ACT.Identity, bias=chb[:, col, g:g + 1])
                        sig(ins, "P", "f32_ready")
                    elif (thread, step) == ("P", "parts"):
                        parts("P", room_a[n], n)
                    elif (thread, step) == ("P", "rel"):
                        wait("P", "rel_psum", n=n + 1)
                        if n == 0:
                            wait("P", "q_written", "k0_written")
                        if n < 8:
                            sig(A.activation(ET[:, n // 4, :, (n % 4) * 32:(n % 4 + 1) * 32],
                                             bank(7 - n % 2).rearrange("p (q h) -> p h q", h=H), ACT.Copy), "P", "rel_sbuf")
                        else:
                            for t in range(T):
                                at = R if t == 0 else 0
                                sig(A.activation(EC[:, t, :, at:at + R],
                                                 bank(7)[EC0:EC0 + R, t * 256:(t + 1) * 256].rearrange("p (q h) -> p h q", h=H), ACT.Copy), "P", "rel_sbuf")
                    elif (thread, step) == ("A", "S"):
                        exponentials("A", n)
                    elif (thread, step) == ("A", "R") and n % 4 == 3:
                        qt = n // 4
                        wait("A", "relv_psum", n=qt + 1)
                        if qt == 0:
                            wait("a", "relv_written")
                        else:
                            wait("A", "relv_written", n=64)
                        sig(A.activation(RV[:, :, :], bank(RVB).rearrange("p (q h) -> p h q", h=H), ACT.Copy), "A", "relv_sbuf")
                    elif (thread, step) == ("B", "ffn_xT"):
                        wait("B", "xT_psum", n=1)
                        wait("b", "q_psum")
                        sig(A.activation(XTB[:, :, :], halves(6), ACT.Copy), "B", "xT_sbuf")
                    elif (thread, step) == ("B", "gelu"):
                        wait("B", "h_psum", n=n + 1)
                        if n == 0:
                            wait("b", "bit_psum")
                        sig(A.activation(GT[:, 2 * n:2 * n + 2, :], bank(6 + n % 2).rearrange("p (i s) -> p i s", i=2), ACT.Gelu), "B", "gelu")
                    elif (thread, step) == ("B", "l1_xT"):
                        wait("B", "xT_psum", n=2)
                        wait("B", "x_expert", "logits")
                        sig(A.activation(XTB[:, :, :], halves(7), ACT.Copy), "B", "xT_sbuf")
                    elif (thread, step) == ("B", "l1_f32"):
                        if n == 0:
                            wait("B", "k_psum", "ffn_psum")
                        else:
                            wait("B", "q_psum", "k_written")
                        sig(A.activation(room_b[n][0], halves(7), ACT.Copy), "B", "f32_ready")
                    elif (thread, step) == ("B", "l1_parts"):
                        parts("B", room_b[n], n)
                    elif (thread, step) == ("B", "l1_S"):
                        exponentials("B", n)
            iterations(act, body)

        @block.vector
        def _(dve):
            V = nc.vector
            done = [0]

            def after(ins):
                done[0] += 1
                ins.then_inc(setup_act, 1)
                dve.wait_ge(setup_act, done[0])

            dve.wait_ge(batches_setup, 1)
            after(V.tensor_tensor(rv3[:, 1, :], rv3[:, 0, :], rvb[:, 1, :], ALU.subtract))
            V.tensor_tensor(rv3[:, 2, :], rv3[:, 0, :], rvb[:, 0, :], ALU.subtract).then_inc(rel_step, 1)
            bvh = rows[:, BV_D, :].rearrange("p (h d) -> p h d", h=H)
            after(V.tensor_tensor(rows[:, BV_O0, :].rearrange("p (h d) -> p h d", h=H), bvh, rvrow[:, 0:1, :].broadcast_to([P, H, DK]), ALU.add))
            after(V.tensor_tensor(rows[:, BV_O1, :].rearrange("p (h d) -> p h d", h=H), bvh, rvrow[:, 1:2, :].broadcast_to([P, H, DK]), ALU.add))
            for a in range(2):
                after(V.tensor_scalar(chb[:, 4 + a, :], chb[:, 1, :], chb[:, 2 + a, 0:1], None, ALU.add))
            after(V.tensor_copy(rkd[:, 0, :], rk))
            after(V.tensor_scalar(rkd[:, 1, :], rk, rk[:, NREL - 1:NREL], None, ALU.subtract))
            after(V.tensor_scalar(rkd[:, 2, :], rk, rk[:, 0:1], None, ALU.subtract))
            low, mid = -R - XLO + 1, NREL - 2
            for a in range(3):
                after(V.tensor_copy(rkpad[:, a, 0:low], rkd[:, a, 0:1].broadcast_to([DK, low])))
                after(V.tensor_copy(rkpad[:, a, low:low + mid], rkd[:, a, 1:1 + mid]))
                after(V.tensor_copy(rkpad[:, a, low + mid:XN], rkd[:, a, NREL - 1:NREL].broadcast_to([DK, XN - low - mid])))
            after(V.tensor_copy(rkP[0], rkpad))
            after(V.tensor_tensor(rkres, rkpad, rkP[0], ALU.subtract))
            after(V.tensor_copy(rkP[1], rkres))
            after(V.tensor_tensor(rkP[2], rkres, rkP[1], ALU.subtract))
            after(V.tensor_copy(b1bf[0], b1v[0]))
            after(V.tensor_tensor(b1v[1], b1v[0], b1bf[0], ALU.subtract))
            after(V.tensor_copy(b1bf[1], b1v[1]))
            after(V.tensor_tensor(b1bf[2], b1v[1], b1bf[1], ALU.subtract))
            dve.nop().then_inc(relk_done, 1)
            dve.wait_ge(w_loaded, 16 * 9)
            after(V.tensor_reduce(wsum[:, 0:1], wb, AX.XY, ALU.add, apply_absolute_value=True))
            dve.nop().then_inc(abs_psum, 1)
            dve.wait_ge(abs_psum, 2)
            after(V.tensor_scalar(wscale[:, :], bank(4)[:, 0:1], 1.0 / (D * D), BIT_EPS, ALU.mult, ALU.add))
            after(V.reciprocal(wsum[:, 1:2], wscale[:, :]))
            after(V.tensor_scalar(wbq, wb, wsum[:, 1:2], ROUND, ALU.mult, ALU.add))
            after(V.tensor_scalar(wbq, wbq, -ROUND, 1.0, ALU.add, ALU.min))
            after(V.tensor_scalar(wbbf, wbq, -1.0, None, ALU.max))
            dve.nop().then_inc(abs_psum, 1)
            dve.wait_ge(abs_psum, 4)
            after(V.tensor_copy(wbT[:, :, :], bank(5)[:, 0:D].bitcast(BF16).rearrange("p (c d) -> p c d", c=C)))
            dve.wait_ge(relv_tab, 16 * 12)
            dve.nop().then_inc(setup_dve, 1)
            setup_over(dve)

            def body(it, off, steps, with_a):
                wait = waiter(dve, it, off)
                other = "A" if with_a else "b"

                def stats(thread, n, src, eps):
                    m = small[thread]
                    for t in range(T):
                        ins = V.bn_stats(m["st6"][:, t, :], src[:, t, :])
                    sig(ins, thread, "stats")
                    wait(thread, "stats", n=4 * n + 1)
                    V.memset(gate[:, :], 0.0)
                    for t in range(T):
                        ins = V.bn_aggr(m["mv"][:, t, :], m["st6"][:, t, :])
                    sig(ins, thread, "stats", 2)
                    wait(thread, "stats", n=4 * n + 3)
                    sig(V.tensor_scalar(m["ve"][:, :], m["mv"][:, :, 1], eps, None, ALU.add), thread, "stats")

                def normed(thread, n, src, dst):
                    m = small[thread]
                    wait(thread, "rstd", n=n + 1)
                    for t in range(T):
                        ins = V.tensor_scalar(dst[:, t, :], src[:, t, :], m["mv"][:, t, 0:1], m["rs"][:, t:t + 1], ALU.subtract, ALU.mult)
                    sig(ins, thread, "xn_ready")

                def parts(thread, room, o):
                    full, resid, part = room
                    wait(thread, "part1", n=o + 1)
                    sig(V.tensor_tensor(resid, full, part[:, 0, :, :], ALU.subtract), thread, "resid")
                    wait(thread, "part2", n=o + 1)
                    sig(V.tensor_tensor(part[:, 2, :, :], resid, part[:, 1, :, :], ALU.subtract), thread, "part3")

                def largest(thread, p):
                    nm = small[thread]["nm"]
                    wait(thread, "scores", n=p + 1)
                    sv = bank(p % 2).rearrange("p (h s) -> p h s", h=2)
                    if thread == "A":
                        sig(V.tensor_reduce(nm[:, 2 * p:2 * p + 2], sv, AX.X, ALU.max, negate=True), thread, "negmax")
                        return
                    qt = p // QPAIRS
                    nk = S if qt else P
                    if p >= 2:
                        wait("B", "exped", n=2 * (p - 1))
                    elif p == 0:
                        wait("B", "mask_ready")
                        if with_a:
                            wait("A", "relv_psum", "pv_psum")
                        else:
                            wait("b", "exped")
                    V.memset(gate[:, :], 0.0)
                    for i in range(2):
                        ins = V.tensor_tensor_reduce(out=SM[:, p % 2, i, 0:nk], in0=sv[:, i, 0:nk], in1=MA[:, qt, 0:nk], scale=1.0,
                                                     scalar=-3.0e38, op0=ALU.add, op1=ALU.max, accum_out=mx[:, 2 * p + i:2 * p + i + 1])
                    sig(ins, "B", "masked")
                    wait("B", "masked", n=p + 1)
                    sig(V.tensor_scalar(nm[:, 2 * p:2 * p + 2], mx[:, 2 * p:2 * p + 2], -(DK ** -0.5), None, ALU.mult), "B", "negmax")

                def probs_T(thread, p):
                    qt, hp = p // QPAIRS, p % QPAIRS
                    nk = T if thread == "A" or qt else 1
                    wait(thread, "wT_psum", n=slot(p) + 1)
                    src = bank(PW0 + slot(p) % 2).rearrange("p (h k q) -> p k h q", h=2, k=T)[:, 0:nk, :, :]
                    if thread == "A":
                        if p == 0:
                            wait("a", "relv_psum", "pv_psum")
                            wait("b", "weighed", "exped")
                            wait("A", "k1_written")
                        elif p == QPAIRS:
                            wait("A", "relv_psum", "pv_psum", n=1)
                        sig(V.tensor_copy(WT_[:, 0:nk, 2 * hp:2 * hp + 2, :], src), "A", "wT_sbuf")
                    else:
                        if p >= 2:
                            wait("B", "weighed", n=p - 1)
                        elif not with_a:
                            wait("b", "weighed")
                        sig(V.tensor_copy(WTB[:, p % 2, 0:nk, :, :], src), "B", "wT_sbuf")

                def inverse(thread, qt):
                    m = small[thread]
                    wait(thread, "exped", n=(qt + 1) * H)
                    if qt:
                        wait(thread, "wT_psum", n=INV_SLOT[0] + 1)
                    elif thread == "A":
                        wait("a", "wT_psum")
                        wait("b", "wT_psum")
                    else:
                        wait(other, "wT_psum")
                    if thread == "A":
                        sig(V.reciprocal(rinv[:, :, :], m["sums"][:, qt, :].unsqueeze(2).broadcast_to([P, H, DK])), "A", "rinv")
                    else:
                        sig(V.reciprocal(m["sums"][:, qt, :], m["sums"][:, qt, :]), "B", "inverted")
                        wait("B", "inverted", n=qt + 1)
                        sig(V.scalar_tensor_tensor(out=rinv[:, :, :], in0=mx[:, qt * H:(qt + 1) * H].unsqueeze(2).broadcast_to([P, H, DK]), scalar=0.5 * MASKED,
                                                   in1=m["sums"][:, qt, :].unsqueeze(2).broadcast_to([P, H, DK]), op0=ALU.is_gt, op1=ALU.mult), "B", "rinv")
                    wait(thread, "wT_psum", n=INV_SLOT[qt] + 1)
                    sig(V.tensor_copy(RT[:, qt, :, :], bank(PW0 + INV_SLOT[qt] % 2)[:, 0:D].rearrange("p (g q) -> p g q", g=C)), thread, "wT_sbuf")

                po = bank(PO).rearrange("p (t g q) -> p g t q", t=T, g=C)
                ot = OT[:, :, :].rearrange("p g (t q) -> p g t q", t=T)
                rt = RT[:, :, :, :].rearrange("p t g q -> p g t q")

                for thread, step, n in steps:
                    if (thread, step) == ("P", "stats"):
                        wait("P", "x_loaded")
                        stats("P", 0, X, LN_EPS)
                    elif (thread, step) == ("P", "normed"):
                        wait("P", "ctxT_psum")
                        normed("P", 0, X, CT)
                    elif (thread, step) == ("P", "v"):
                        wait("P", "v_psum")
                        wait("A", "pv_psum")
                        vp = bank(5).rearrange("p (k h a d) -> p k h a d", k=T, a=2, d=DK)
                        for a in range(2):
                            for var in range(2):
                                dst = V2[:, var, :, :, :].rearrange("p k (h a) d -> p k h a d", a=2)[:, :, :, a, a * DK:(a + 1) * DK]
                                first, last = (BV_D, BV_D) if var == 0 else (BV_O0, BV_O1)
                                row = rows[:, first:last + 1, :].rearrange("p k (h a d) -> p k h a d", a=2, d=DK)[:, :, :, a, :]
                                if var == 0:
                                    row = row.broadcast_to([P, T, H // 2, DK])
                                sig(V.tensor_tensor(dst, vp[:, :, :, a, :], row, ALU.add), "P", "v_sbuf")
                    elif (thread, step) == ("P", "parts"):
                        parts("P", room_a[n], n)
                    elif step == "S" or step == "l1_S":
                        largest(thread, n)
                    elif step == "T" or step == "l1_T":
                        probs_T(thread, n)
                    elif step == "I" or step == "l1_I":
                        inverse(thread, n)
                    elif (thread, step) == ("A", "finish"):
                        wait("A", "pv_psum", "wT_sbuf", "relv_loaded")
                        sig(V.tensor_tensor(ot, po, ot, ALU.add), "A", "o_sum")
                        wait("A", "o_sum")
                        sig(V.tensor_tensor(ot, ot, rt, ALU.mult), "A", "oT")
                    elif (thread, step) == ("A", "output"):
                        wait("A", "y_psum", "base")
                        wait("B", "x2_ready")
                        sig(V.tensor_tensor(Y[:, :, :], halves(RVB), XO[:, :, :], ALU.add), "A", "x1_ready")
                    elif (thread, step) == ("B", "stats"):
                        if n == 0:
                            wait("a", "x1_ready")
                        stats("B", n, (Y, None, Z, Z)[n], LN_EPS)
                    elif (thread, step) == ("B", "normed"):
                        if n == 0:
                            wait("b", "aq")
                        normed("B", n, (Y, None, Z, Z)[n], XNB)
                    elif (thread, step) == ("B", "router"):
                        wait("B", "logits")
                        wait("b", "ohT_psum")
                        lp = bank(7)[:, 0:T * E].rearrange("p (t e) -> p t e", t=T)
                        sig(V.tensor_reduce(lmax[:, :], lp, AX.X, ALU.max), "B", "route")
                        wait("B", "route", n=1)
                        for t in range(T):
                            ins = V.tensor_scalar(lg[:, t, :], lp[:, t, :], lmax[:, t:t + 1], None, ALU.is_ge)
                        sig(ins, "B", "route")
                        wait("B", "route", n=2)
                        sig(V.tensor_tensor(lg[:, :, :], lg[:, :, :], firsts[:, :, :], ALU.mult), "B", "route")
                        wait("B", "route", n=3)
                        sig(V.tensor_reduce(lmax[:, :], lg[:, :, :], AX.X, ALU.max), "B", "route")
                        wait("B", "route", n=4)
                        for t in range(T):
                            V.tensor_scalar(oh[:, t, :], lg[:, t, :], lmax[:, t:t + 1], None, ALU.is_equal)
                            ins = V.tensor_scalar(oh12[:, t, :, :], lg[:, t:t + 1, :].broadcast_to([P, 3, E]), lmax[:, t:t + 1], None, ALU.is_equal)
                        sig(ins, "B", "onehot")
                    elif (thread, step) == ("B", "experts"):
                        if n == 0:
                            wait("B", "ohT_psum", n=1)
                            wait("b", "h_psum")
                            sig(V.tensor_copy(ohT[:, :], bank(6)[0:3 * E, 0:S // 2].bitcast(BF16)), "B", "ohT_sbuf")
                            wait("B", "xT_sbuf", n=1)
                            wait("b", "scores")
                        wait("B", "ohT_psum", n=2 + n)
                        for e in range(2):
                            sig(V.tensor_tensor(XE[:, 2 * n + e, :, :], XTB[:, :, :], bank(7 - n).rearrange("p (e s) -> p e s", e=2)[:, e:e + 1, :].broadcast_to([P, C, S]), ALU.mult), "B", "x_expert")
                    elif (thread, step) == ("B", "ffn_sum"):
                        wait("B", "ffn_psum", "ffn_base")
                        sig(V.tensor_tensor(XNB[:, :, :], halves(6), FB[:, :, :], ALU.add), "B", "ffn_sum")
                        wait("B", "ffn_sum")
                        stats("B", 1, XNB, FFN_EPS)
                    elif (thread, step) == ("B", "ffn_end"):
                        normed("B", 1, XNB, XNB)
                        wait("B", "xn_ready", n=2)
                        sig(V.tensor_tensor(XNB[:, :, :], XNB[:, :, :], rows[:, GAMMA:GAMMA + 1, :].broadcast_to([P, T, D]), ALU.mult), "B", "ffn_scale")
                        wait("B", "ffn_scale", n=1)
                        sig(V.tensor_tensor(XNB[:, :, :], XNB[:, :, :], rows[:, BETA:BETA + 1, :].broadcast_to([P, T, D]), ALU.add), "B", "ffn_scale")
                        wait("B", "ffn_scale", n=2)
                        sig(V.tensor_tensor(Z[:, :, :], Y[:, :, :], XNB[:, :, :], ALU.add), "B", "x2_ready")
                        wait("B", "x2_ready")
                    elif (thread, step) == ("B", "l1_v"):
                        wait("B", "v_psum")
                        wait("b", "weighed")
                        vp = bank(6).rearrange("p (k h a d) -> p k h a d", k=T, a=2, d=DK)
                        for a in range(2):
                            dst = V2B[:, :, :, :].rearrange("p k (h a) d -> p k h a d", a=2)[:, :, :, a, a * DK:(a + 1) * DK]
                            sig(V.tensor_copy(dst, vp[:, :, :, a, :]), "B", "v_sbuf")
                    elif (thread, step) == ("B", "l1_parts"):
                        parts("B", room_b[n], n)
                    elif (thread, step) == ("B", "l1_finish"):
                        wait("B", "weighed", "wT_sbuf")
                        wait(other, "y_psum")
                        sig(V.tensor_tensor(ot, po, rt, ALU.mult), "B", "oT")
                    elif (thread, step) == ("B", "l1_output"):
                        wait("B", "y_psum", "base")
                        sig(V.tensor_tensor(Z[:, :, :], halves(5), FB[:, :, :], ALU.add), "B", "x3_ready")
                        wait("B", "x3_ready")
                    elif (thread, step) == ("B", "quantise"):
                        wait("B", "xn_ready")
                        sig(V.tensor_reduce(am[:, 0, :], XNB[:, :, :], AX.X, ALU.max, apply_absolute_value=True), "B", "amax")
                        wait("B", "amax", n=1)
                        sig(V.tensor_scalar(am[:, 0, :], am[:, 0, :], BIT_EPS, None, ALU.add), "B", "amax")
                        wait("B", "amax", n=2)
                        V.reciprocal(am[:, 1, :], am[:, 0, :])
                        sig(V.tensor_scalar(am[:, 2, :], am[:, 0, :], wscale[:, :], 1.0 / 127.0, ALU.mult, ALU.mult), "B", "amax")
                        wait("B", "amax", n=3)
                        for t in range(T):
                            ins = V.tensor_scalar(XNB[:, t, :], XNB[:, t, :], am[:, 1, t:t + 1], 127.0, ALU.mult, ALU.mult)
                        sig(ins, "B", "zq")
                        wait("B", "zq", n=1)
                        sig(V.tensor_scalar(XNB[:, :, :], XNB[:, :, :], 127.0, -128.0, ALU.min, ALU.max), "B", "zq")
                        wait("B", "zq", n=2)
                        sig(V.tensor_scalar(XNB[:, :, :], XNB[:, :, :], ROUND, None, ALU.add), "B", "zq")
                        wait("B", "zq", n=3)
                        sig(V.tensor_scalar(AQ, XNB[:, :, :], -ROUND, None, ALU.add), "B", "aq")
                    elif (thread, step) == ("B", "bit_T"):
                        wait("B", "aT_psum")
                        sig(V.tensor_copy(AQT, bank(5)[:, 0:D].bitcast(BF16).rearrange("p (c s) -> p c s", c=C)), "B", "aT_sbuf")
                    elif (thread, step) == ("B", "bit"):
                        wait("B", "bit_psum")
                        for t in range(T):
                            ins = V.scalar_tensor_tensor(out=FB[:, t, :], in0=halves(5)[:, t, :], scalar=am[:, 2, t:t + 1], in1=Z[:, t, :], op0=ALU.mult, op1=ALU.add)
                        sig(ins, "B", "out_sbuf")
            iterations(dve, body)

        @block.tensor
        def _(pe):
            TE = nc.tensor
            pe.wait_ge(const_made, CONSTS)
            pe.wait_ge(w_loaded, 16 * 9)
            for m in range(8):
                if m >= 4:
                    pe.wait_ge(wtr_sbuf, m - 3)
                for c in range(C):
                    for o in range(C):
                        ins = TE.transpose(bank(m % 4)[:, c * D + o * P:c * D + (o + 1) * P], WST[:, m, o, c * P:(c + 1) * P], ident[:, :])
                ins.then_inc(wtr_psum, 1)
            pe.wait_ge(abs_psum, 1)
            TE.matmul(bank(4)[:, 0:1], ones, wsum[:, 0:1], start=True, stop=True).then_inc(abs_psum, 1)
            pe.wait_ge(abs_psum, 3)
            wbps = bank(5)[:, 0:D].bitcast(BF16)
            for c in range(C):
                for o in range(C):
                    ins = TE.transpose(wbps[:, c * D + o * P:c * D + (o + 1) * P], wbbf[:, o, c * P:(c + 1) * P], ident_bf[:, :])
            ins.then_inc(abs_psum, 1)
            setup_over(pe)

            def body(it, off, steps, with_a):
                wait = waiter(pe, it, off)
                other = "A" if with_a else "b"

                def transpose_tiles(src, dst_bank, thread, name):
                    for c in range(C):
                        for t in range(T):
                            ins = TE.transpose(bank(dst_bank)[:, c * S + t * P:c * S + (t + 1) * P], src[:, t, c * P:(c + 1) * P], ident[:, :])
                    sig(ins, thread, name)

                def project_T(m, src, dst_bank, thread, name):
                    for g in range(C):
                        for c in range(C):
                            ins = TE.matmul(bank(dst_bank)[:, g * S:(g + 1) * S], wT[:, m, c, g * P:(g + 1) * P], src[:, c, :], start=c == 0, stop=c == C - 1)
                    sig(ins, thread, name)

                def project(m, src, dst_bank, thread, name):
                    for t in range(T):
                        for c in range(C):
                            ins = TE.matmul(bank(dst_bank)[:, t * D:(t + 1) * D], src[:, c, t * P:(t + 1) * P], wT[:, m, c, :], start=c == 0, stop=c == C - 1)
                    sig(ins, thread, name)

                def scores(thread, p):
                    qt, hp = p // QPAIRS, p % QPAIRS
                    if p >= 2:
                        if thread == "A":
                            wait("A", "exped", n=2 * (p - 1))
                        else:
                            wait("B", "masked", n=p - 1)
                    elif p == 0:
                        wait(thread, "q_stacked", "k_stacked")
                        if thread == "A":
                            wait("A", "rel_sbuf")
                            wait("a", "exped")
                            wait("b", "masked")
                        elif with_a:
                            wait("A", "exped")
                        else:
                            wait("b", "masked")
                    sv = bank(p % 2).rearrange("p (h s) -> p h s", h=2)
                    for i in range(2):
                        h = 2 * hp + i
                        if thread == "B":
                            nk = S if qt else P
                            ins = TE.matmul(sv[:, i, 0:nk], QSB[:, h, qt * P:(qt + 1) * P], KSB[:, h, 0:nk], start=True, stop=True)
                            continue
                        TE.matmul(sv[:, i, :], QS[:, h, qt * P:(qt + 1) * P], KS[:, qt, h, :], start=True, stop=False, skip_group_check=True)
                        TE.matmul(sv[:, i, qt * P:(qt + 1) * P], ET[:, qt, h, :], ident[:, :], start=False, stop=False, is_transpose=True, skip_group_check=True)
                        q0, k0 = (P - 2 * R, P) if qt == 0 else (0, P - R)
                        ins = TE.matmul(sv[q0:q0 + 2 * R, i, k0:k0 + R], EC[:, qt, h, :], ident[EC0:EC0 + R, EC0:EC0 + R], start=False, stop=True, skip_group_check=True)
                    sig(ins, thread, "scores")

                def probs_T(thread, p):
                    qt = p // QPAIRS
                    at = slot(p)
                    wait(thread, "exped", n=2 * (p + 1))
                    if at >= 2:
                        wait(thread, "wT_sbuf", n=at - 1)
                    elif thread == "A":
                        wait("a", "wT_sbuf")
                        wait("b", "wT_sbuf")
                    else:
                        wait(other, "wT_sbuf")
                    for i in range(2):
                        for kt in range(T if thread == "A" or qt else 1):
                            ins = TE.transpose(bank(PW0 + at % 2)[:, (i * T + kt) * P:(i * T + kt + 1) * P], W[:, p % W_RING, i, kt * P:(kt + 1) * P], ident[:, :])
                    sig(ins, thread, "wT_psum")

                def weigh_values(thread, p):
                    qt, hp = p // QPAIRS, p % QPAIRS
                    wait(thread, "wT_sbuf", n=slot(p) + 1)
                    if p == 0:
                        wait(thread, "v_sbuf")
                        if thread == "A":
                            wait("a", "o_sum")
                            wait("b", "oT")
                        else:
                            wait(other, "oT")
                    nk = T if thread == "A" or qt else 1
                    g, row = hp // 4, 32 * (hp % 4)
                    ps = bank(PO)[row:row + 32, qt * D + g * P:qt * D + (g + 1) * P]
                    for i in range(2):
                        h = 2 * hp + i
                        for kt in range(nk):
                            if thread == "A":
                                v, w = V2[:, int(kt != qt), kt, h, :], WT_[:, kt, h, :]
                            else:
                                v, w = V2B[:, kt, h, :], WTB[:, p % 2, kt, i, :]
                            ins = TE.matmul(ps, v, w, start=i == 0 and kt == 0, stop=i == 1 and kt == nk - 1, skip_group_check=True)
                    if thread == "B":
                        sig(ins, "B", "weighed")
                    elif hp == QPAIRS - 1:
                        sig(ins, "A", "pv_psum")

                def relative_values(qt, j):
                    if j == 0 and qt == 0:
                        wait("b", "out_sbuf")
                    elif j == 0:
                        wait("A", "relv_sbuf", n=1)
                    for i in range(32):
                        q = 32 * j + i
                        seam = q >= P - R if qt == 0 else q < R
                        ps = bank(RVB)[32 * j:32 * j + 32, i * H:(i + 1) * H]
                        s = P - 1 - q
                        ins = TE.matmul(ps, relv_d[:, s:s + 2, :].rearrange("p s d -> p (s d)"), WT_[:, qt, :, q], start=i == 0, stop=not seam, skip_group_check=True)
                        if seam:
                            s = (P - 1 if qt == 0 else R - 1) - q
                            ins = TE.matmul(ps, relv_o[:, qt, s:s + 2, :].rearrange("p s d -> p (s d)"), WT_[:, 1 - qt, :, q], start=False, stop=True, skip_group_check=True)
                    if j == 3:
                        sig(ins, "A", "relv_psum")

                def inverse_T(thread, qt):
                    at = INV_SLOT[qt]
                    wait(thread, "rinv", n=qt + 1)
                    wait(thread, "wT_sbuf", n=at - 1)
                    for g in range(C):
                        hs = H // C
                        ins = TE.transpose(bank(PW0 + at % 2)[:, g * P:(g + 1) * P], rinv[:, g * hs:(g + 1) * hs, :].rearrange("p h d -> p (h d)"), ident[:, :])
                    sig(ins, thread, "wT_psum")

                for thread, step, n in steps:
                    if (thread, step) == ("P", "ctxT"):
                        wait("P", "ctx_loaded")
                        wait("B", "v_sbuf")
                        transpose_tiles(CT, 6, "P", "ctxT_psum")
                    elif (thread, step) == ("P", "k"):
                        wait("P", "f32_ready", n=1)
                        project_T(1, CTT, 6, "P", "k_psum")
                    elif (thread, step) == ("P", "v"):
                        wait("A", "x1_ready")
                        project(2, CTT, 5, "P", "v_psum")
                    elif (thread, step) == ("P", "xT"):
                        wait("P", "xn_ready", "ctxT_sbuf")
                        transpose_tiles(CT, 6, "P", "xT_psum")
                    elif (thread, step) == ("P", "q"):
                        wait("P", "xT_sbuf")
                        project_T(0, XT, 6, "P", "q_psum")
                    elif (thread, step) == ("P", "rel") and n < 8:
                        if n == 0:
                            wait("P", "q_stacked")
                            wait("B", "f32_ready")
                        elif n == 1:
                            wait("P", "f32_ready")
                        else:
                            wait("P", "rel_sbuf", n=n - 1)
                        qt, q0 = n // 4, (n % 4) * 32
                        for q in range(q0, q0 + 32):
                            lo = -q - XLO
                            ins = TE.matmul(bank(7 - n % 2)[:, (q - q0) * H:(q - q0 + 1) * H], relk_st[:, 0, lo:lo + P], QS[:, :, qt * P + q], start=q == q0, stop=True, skip_group_check=True)
                        sig(ins, "P", "rel_psum")
                    elif (thread, step) == ("P", "rel"):
                        wait("P", "rel_sbuf", n=7)
                        for t in range(T):
                            for j in range(R):
                                q = (P - R + j) if t == 0 else (P + j)
                                lo = ((P if t == 0 else P - R) - q) - XLO
                                ins = TE.matmul(bank(7)[EC0:EC0 + R, t * 256 + j * H:t * 256 + (j + 1) * H], relk_st[:, 1 + t, lo:lo + R], QS[:, :, q], start=t == 0 and j == 0, stop=True, skip_group_check=True)
                        sig(ins, "P", "rel_psum")
                    elif step == "S" or step == "l1_S":
                        scores(thread, n)
                    elif step == "T" or step == "l1_T":
                        probs_T(thread, n)
                    elif step == "W" or step == "l1_W":
                        weigh_values(thread, n)
                    elif step == "R":
                        relative_values(n // 4, n % 4)
                    elif step == "I" or step == "l1_I":
                        inverse_T(thread, n)
                    elif (thread, step) == ("A", "output"):
                        wait("A", "oT", "relv_sbuf")
                        project(3, OT, RVB, "A", "y_psum")
                    elif (thread, step) == ("B", "ffn_xT"):
                        wait("B", "xn_ready", n=1)
                        wait("b", "v_sbuf")
                        if with_a:
                            wait("A", "rel_sbuf")
                        transpose_tiles(XNB, 6, "B", "xT_psum")
                    elif (thread, step) == ("B", "router"):
                        wait("B", "xT_sbuf", n=1)
                        wait("b", "f32_ready")
                        for t in range(T):
                            for c in range(C):
                                ins = TE.matmul(bank(7)[:, t * E:(t + 1) * E], XTB[:, c, t * P:(t + 1) * P], wr[:, c, :], start=c == 0, stop=c == C - 1)
                        sig(ins, "B", "logits")
                    elif (thread, step) == ("B", "onehot_T"):
                        wait("B", "onehot")
                        for t in range(T):
                            ins = TE.transpose(bank(6)[0:3 * E, 0:S // 2].bitcast(BF16)[:, t * P:(t + 1) * P], oh12[:, t, :, :].rearrange("p a e -> p (a e)"), ident_bf[:, :])
                        sig(ins, "B", "ohT_psum")
                    elif (thread, step) == ("B", "experts"):
                        if n == 1:
                            wait("B", "ohT_sbuf")
                        for e in range(2):
                            for t in range(T):
                                ins = TE.transpose(bank(7 - n)[:, e * S + t * P:e * S + (t + 1) * P], oh[:, t, 2 * n + e:2 * n + e + 1].broadcast_to([P, P]), ident[:, :])
                        sig(ins, "B", "ohT_psum")
                    elif (thread, step) == ("B", "up"):
                        i, half = n // 2, n % 2
                        if n == 0:
                            wait("B", "ohT_sbuf", "x_expert")
                        elif n % 4 == 0 and n >= 8:
                            wait("B", "gelu", n=n // 4 - 1)
                        ps = bank(6 + (i // 2) % 2)[:, (i % 2) * S:(i % 2 + 1) * S]
                        if half == 0:
                            TE.matmul(ps, b1p[:, i * P:(i + 1) * P], ohT[:, :], start=True, stop=False)
                        for e in range(2 * half, 2 * half + 2):
                            for c in range(C):
                                ins = TE.matmul(ps, w1[:, e, c, i * P:(i + 1) * P], XE[:, e, c, :], start=False, stop=e == E - 1 and c == C - 1)
                        if n % 4 == 3:
                            sig(ins, "B", "h_psum")
                    elif (thread, step) == ("B", "down"):
                        wait("B", "gelu", n=max(3, n + 1))
                        for i in range(2 * n, 2 * n + 2):
                            for t in range(T):
                                ins = TE.matmul(bank(6)[:, t * D:(t + 1) * D], GT[:, i, t * P:(t + 1) * P], wf[:, i, :], start=i == 0 and t == 0, stop=i == IC - 1, skip_group_check=True)
                        if n == 3:
                            sig(ins, "B", "ffn_psum")
                    elif (thread, step) == ("B", "l1_k"):
                        wait("B", "gelu")
                        wait("a", "ctx_copied")
                        project_T(5, CTB, 7, "B", "k_psum")
                    elif (thread, step) == ("B", "l1_v"):
                        wait("B", "ffn_sum")
                        project(6, CTB, 6, "B", "v_psum")
                    elif (thread, step) == ("B", "l1_xT"):
                        wait("B", "xn_ready", n=3)
                        wait("B", "f32_ready", n=1)
                        transpose_tiles(XNB, 7, "B", "xT_psum")
                    elif (thread, step) == ("B", "l1_q"):
                        wait("B", "xT_sbuf")
                        project_T(4, XTB, 7, "B", "q_psum")
                    elif (thread, step) == ("B", "l1_output"):
                        wait("B", "oT")
                        wait("P", "v_sbuf")
                        wait("A", "x1_ready")
                        wait("b", "out_sbuf")
                        project(7, OT, 5, "B", "y_psum")
                    elif (thread, step) == ("B", "bit_T"):
                        wait("B", "aq", "x3_ready")
                        for c in range(C):
                            for t in range(T):
                                ins = TE.transpose(bank(5)[:, 0:D].bitcast(BF16)[:, c * S + t * P:c * S + (t + 1) * P], AQ[:, t, c * P:(c + 1) * P], ident_bf[:, :])
                        sig(ins, "B", "aT_psum")
                    elif (thread, step) == ("B", "bit"):
                        wait("B", "aT_sbuf")
                        for t in range(T):
                            for c in range(C):
                                ins = TE.matmul(bank(5)[:, t * D:(t + 1) * D], AQT[:, c, t * P:(t + 1) * P], wbT[:, c, :], start=c == 0, stop=c == C - 1)
                        sig(ins, "B", "bit_psum")

            def before_loop():
                pe.wait_ge(big_loaded, 32)
            iterations(pe, body, before_loop)

        emitted = 3
        assert all(raised[n] == emitted * PER[n] for n in PER), [(n, raised[n], PER[n]) for n in PER if raised[n] != emitted * PER[n]]


_INS = ["x", "ctx_1024", "mask_BxSxS2_bf0", "L0_xattn_Wq", "L0_xattn_bq", "L0_xattn_Wk", "L0_xattn_bk", "L0_xattn_Wv",
        "L0_xattn_bv", "L0_xattn_Wo", "L0_xattn_bo", "L0_xattn_rel_k_table", "L0_xattn_rel_v_table", "L0_ffn_W_router",
        "L0_ffn_W1", "L0_ffn_b1", "L0_ffn_Wo", "L0_ffn_bo", "L0_ffn_ln_gamma", "L0_ffn_ln_beta", "L1_xattn_Wq",
        "L1_xattn_Wk", "L1_xattn_Wv", "L1_xattn_Wout", "L1_xattn_b_out", "L1_ffn_weight"]


def kernel(**inputs):
    import concourse.bacc as bacc
    from concourse.bass_utils import run_bass_kernel_spmd

    nc = bacc.Bacc("TRN2", target_bir_lowering=False, num_devices=1)
    arrays, args = {}, []
    for name in _INS:
        a = np.ascontiguousarray(inputs[name])
        arrays[f"in_{name}"] = a
        args.append(nc.dram_tensor(f"in_{name}", a.shape, mybir.dt.from_np(a.dtype), kind="ExternalInput").ap())
    args.append(nc.dram_tensor("out", (B, S, D), F32, kind="ExternalOutput").ap())
    _program(nc, *args)
    return run_bass_kernel_spmd(nc, [arrays], core_ids=[0]).results[0]["out"]
```

```python
from contextlib import ExitStack

import numpy as np

import concourse.bass as bass
from concourse import mybir

F32 = mybir.dt.float32
BF16 = mybir.dt.bfloat16
U8 = mybir.dt.uint8
ALU = mybir.AluOpType
ACT = mybir.ActivationFunctionType
AX = mybir.AxisListType

P = 128
B, S, D = 8, 256, 256
H = 16
DK = D // H
T = S // P
C = D // P
E, I = 4, 1024
IC = I // P
R = 16
NREL = 2 * R + 1
XLO = -(P + R)
XN = 2 * (P + R)
MASKED = -1.0e30
LN_EPS = 1e-5
FFN_EPS = 1e-12
BIT_EPS = 1e-8
ROUND = 1.5 * 2.0 ** 23

QPART = [0, 0, 1, 0, 2, 1]
KPART = [0, 1, 0, 2, 0, 1]
STACK = len(QPART) * DK

PAIRS = 16
QPAIRS = PAIRS // T
SLOTS = PAIRS + T
INV_AFTER = QPAIRS + 3
INV_SLOT = [INV_AFTER + 1, SLOTS - 1]
W_RING = 3

PER_A = {
    "x_loaded": 16, "ctx_loaded": 16, "stats": 4, "rstd": 1, "xn_ready": 1, "base": 1, "ctx_copied": 1,
    "ctxT_psum": 1, "ctxT_sbuf": 1, "xT_psum": 1, "xT_sbuf": 1, "q_psum": 1, "k_psum": 1, "v_psum": 1, "v_sbuf": 4,
    "f32_ready": 3, "part1": 3, "resid": 3, "part2": 3, "part3": 3,
    "q_written": 16, "k0_written": 16, "k1_written": 16, "q_stacked": 96, "k_stacked": 192, "rel_psum": 9, "rel_sbuf": 9 + T - 1,
    "scores": PAIRS, "negmax": PAIRS, "exped": 2 * PAIRS, "wT_psum": SLOTS, "wT_sbuf": SLOTS, "pv_psum": T, "inverted": T, "rinv": T,
    "relv_psum": T, "relv_sbuf": T, "relv_written": T * 64, "relv_loaded": T * 16,
    "unloaded": 1, "relv_scaled": 1, "oT": 1, "y_psum": 1, "x1_ready": 1,
}
PER_B = {
    "stats": 4 * 4, "rstd": 4, "xn_ready": 4, "ffn_base": 1, "base": 1, "xT_psum": 2, "xT_sbuf": 2,
    "logits": 1, "route": 4, "onehot": 1, "ohT_psum": 3, "ohT_sbuf": 1, "x_expert": E, "h_psum": IC // 2, "gelu": IC // 2,
    "ffn_psum": 1, "ffn_sum": 1, "ffn_scale": 2, "x2_ready": 1,
    "q_psum": 1, "k_psum": 1, "v_psum": 1, "v_sbuf": 2,
    "f32_ready": 2, "part1": 2, "resid": 2, "part2": 2, "part3": 2,
    "k_written": 16, "q_written": 16, "q_stacked": 96, "k_stacked": 96,
    "mask_loaded": 16, "mask_scaled": 1, "mask_ready": T,
    "scores": PAIRS, "masked": PAIRS, "negmax": PAIRS, "exped": 2 * PAIRS, "wT_psum": SLOTS, "wT_sbuf": SLOTS,
    "weighed": PAIRS, "inverted": T, "rinv": T, "oT": 1, "y_psum": 1, "x3_ready": 1,
    "amax": 3, "zq": 3, "aq": 1, "aT_psum": 1, "aT_sbuf": 1, "bit_psum": 1, "out_sbuf": 1, "stored": 16,
}

def attention_steps(thread):
    out = []
    for p in range(PAIRS):
        out.append(("S", p))
        if p == QPAIRS + 2 and thread == "A":
            out += [("W", p - 3)] + [("R", j) for j in range(4)] + [("T", p - 2)]
            continue
        out += [("T", p - 2)] if p >= 2 else []
        out += [("N", 0)] if p - 2 == INV_AFTER - 1 else []
        out += [("W", p - 3)] if p >= 3 else []
        out += [("I", 0)] if p - 2 == INV_AFTER else []
    out += [("T", PAIRS - 2), ("W", PAIRS - 3), ("T", PAIRS - 1), ("N", 1), ("W", PAIRS - 2), ("W", PAIRS - 1)]
    return out + ([("R", 4), ("I", 1), ("R", 5), ("R", 6), ("R", 7)] if thread == "A" else [("I", 1)])


HEAD = 10
BESIDE_A = [
    [("B", "router", 0), ("P", "stats", 0)], [("B", "onehot_T", 0), ("B", "experts", 0)], [("B", "experts", 1), ("B", "mask", 1)],
    [("B", "up", 0), ("B", "up", 1)], [("B", "up", 2), ("B", "up", 3)], [("B", "up", 4), ("B", "up", 5), ("B", "gelu", 0)],
    [("B", "up", 8), ("B", "up", 9), ("B", "gelu", 1)], [("B", "up", 6), ("B", "up", 7)], [("B", "up", 10), ("B", "up", 11)],
    [("B", "up", 12), ("B", "up", 13), ("B", "gelu", 2)], [("B", "up", 14), ("B", "up", 15)], [("B", "down", 0), ("B", "gelu", 3)],
    [("B", "down", 1)], [("B", "down", 2), ("B", "ffn_sum", 0)], [("B", "down", 3), ("B", "l1_k", 0)], [], [("B", "l1_f32", 0)],
    [("B", "ffn_end", 0)], [("B", "l1_v", 0), ("B", "stats", 2)], [("B", "part1", 0)], [("B", "resid", 0), ("A", "copy", 0)], [("B", "part2", 0)], [],
    [], [("B", "normed", 2)], [("B", "part3", 0), ("P", "ctxT", 0), ("B", "l1_stack", 0)], [("P", "normed", 0)], [("B", "l1_xT", 0), ("P", "xT", 0)],
    [], [], [("B", "l1_f32", 1)], [("B", "l1_q", 0), ("B", "part1", 1)], [], [("P", "f32", 0), ("B", "part2", 1)],
    [("B", "resid", 1), ("P", "q", 0), ("P", "part1", 0)], [("B", "part3", 1), ("P", "resid", 0)], [("P", "part2", 0)],
    [("P", "part3", 0), ("B", "l1_stack", 1)], [("P", "q_stack", 0)], [("P", "f32", 1)], [("P", "part1", 1)], [("P", "k", 0)], [("P", "resid", 1)],
    [("P", "part2", 1)], [("P", "part3", 1)], [], [("A", "unload", 0)], [], [], [("A", "relv_load", 0), ("P", "f32", 2), ("P", "rel", 0)],
]
BESIDE_B = [
    [], [("P", "part1", 2), ("A", "scale", 0), ("P", "resid", 2), ("P", "rel", 1)], [("P", "part2", 2)], [], [], [], [],
    [("A", "finish", 0), ("P", "rel", 2)], [], [], [("A", "output", 0), ("P", "rel", 3)], [], [], [("P", "part3", 2), ("P", "v", 0)], [], [],
    [("P", "k_stack", 0), ("P", "base", 0)], [("P", "rel", 4)], [], [], [("P", "rel", 5)], [], [], [], [], [], [], [], [], [], [], [], [], [], [], [],
    [], [], [], [], [], [], [], [], [], [], [], [], [], [("P", "rel", 6)], [("P", "rel", 7)],
    [("B", "l1_finish", 0), ("P", "rel", 8), ("B", "l1_output", 0)],
]
BESIDE_NEXT = [
    [(0, "B", "stats", 3), (1, "B", "mask", 0)], [(0, "B", "normed", 3), (0, "B", "quantise", 0)], [], [], [], [],
    [(1, "B", "stats", 0), (0, "B", "bit_T", 0), (1, "B", "normed", 0)], [(0, "B", "bit", 0)], [], [(1, "B", "ffn_xT", 0)],
]


def order(k):
    attention = attention_steps("A")
    out = [(0, "P", "load", 0)]
    for step, beside in zip(attention[HEAD:], BESIDE_A):
        out += [(0, "A") + step] + [(0,) + s for s in beside]
    for step, beside in zip(attention_steps("B"), BESIDE_B):
        out += [(0, "B", "l1_" + step[0], step[1])] + [(0,) + s for s in beside]
    for step, beside in zip(attention[:HEAD], BESIDE_NEXT):
        out += [(1, "A") + step] + beside
    shift = {"A": 0, "P": 1, "B": -1}
    return [s for s in out if 0 <= k + s[0] + shift[s[1]] < B]


def slot(n_pair):
    return n_pair + (1 if n_pair > INV_AFTER else 0)


def _program(nc, x, ctx_in, mask, Wq0, bq0, Wk0, bk0, Wv0, bv0, Wo0, bo0, relk, relv,
             Wr, W1, b1, Wf, bf, gamma, beta, Wq1, Wk1, Wv1, Wo1, bo1, Wb, out):
    with ExitStack() as stack:
        def sb(name, shape, dt=F32):
            return stack.enter_context(nc.sbuf_tensor(name, shape, dt))

        def dram(name, shape, dt=F32):
            return nc.dram_tensor(name, shape, dt, kind="Internal").ap()

        def new_sem(name):
            return stack.enter_context(nc.semaphore(name))

        ident = sb("ident", [P, P])
        ident_bf = sb("ident_bf", [P, P], BF16)
        wT = sb("wT", [P, 8, C, D])
        wr = sb("wr", [P, C, E])
        w1 = sb("w1", [P, E, C, I])
        wf = sb("wf", [P, IC, D])
        wbT = sb("wbT", [P, C, D], BF16)
        wscale = sb("wscale", [P, 1])
        rows = sb("rows", [P, 8, D])
        BV_D, BV_O0, BV_O1, BO0, BF_, GAMMA, BETA, BO1 = range(8)
        chb = sb("chb", [P, 6, C])
        relk_st = sb("relk_st", [STACK, 3, XN], BF16)
        relv_d = sb("relv_d", [P, P + 1, DK])
        relv_o = sb("relv_o", [P, T, R + 1, DK])
        halfs = sb("halfs", [P, T])
        firsts = sb("firsts", [P, T, E])
        low_rows = sb("low_rows", [64, T * H * 2 * R])
        b1p = low_rows[0:3 * E, :].bitcast(BF16)[:, 0:I]
        EC0 = 2 * R
        EC = low_rows[EC0:EC0 + R, :].rearrange("p (t h s) -> p t h s", t=T, h=H)

        X = sb("X", [P, T, D])
        CT = sb("CT", [P, T, D])
        CTT = sb("CTT", [P, C, S])
        XT = sb("XT", [P, C, S])
        XO = sb("XO", [P, T, D])
        QS = sb("QS", [STACK, H, S], BF16)
        KS = sb("KS", [STACK, T, H, S], BF16)
        V2 = sb("V2", [P, 2, T, H, 2 * DK])
        ET = sb("ET", [P, T, H, P])

        Y = sb("Y", [P, T, D])
        Z = sb("Z", [P, T, D])
        FB = sb("FB", [P, T, D])
        XNB = sb("XNB", [P, T, D])
        RVC = XNB[:, :, :]
        XTB = sb("XTB", [P, C, S])
        CTB = sb("CTB", [P, C, S])
        MK = sb("MK", [P, T, S], U8)
        MA = sb("MA", [P, T, S])
        V2B = sb("V2B", [P, T, H, 2 * DK])
        q1_mem = sb("q1_mem", [P, 2048])
        k1_mem = sb("k1_mem", [P, 2048])
        QSB = q1_mem[0:STACK, :].bitcast(BF16).rearrange("p (h s) -> p h s", h=H)
        KSB = k1_mem[0:STACK, :].bitcast(BF16).rearrange("p (h s) -> p h s", h=H)
        XE = k1_mem[:, :].rearrange("p (e c s) -> p e c s", e=E, c=C)
        GT = q1_mem[:, :].rearrange("p (i s) -> p i s", i=IC)
        AQ = q1_mem[:, 0:256].bitcast(BF16).rearrange("p (t d) -> p t d", t=T)
        AQT = q1_mem[:, 256:512].bitcast(BF16).rearrange("p (c s) -> p c s", c=C)

        W = sb("W", [P, W_RING, 2, S])
        wt_mem = sb("wt_mem", [P, 4096])
        WT_ = wt_mem[:, :].rearrange("p (k h q) -> p k h q", k=T, h=H)
        WTB = wt_mem[:, 0:1024].rearrange("p (a k h q) -> p a k h q", a=2, k=T, h=2)
        SM = wt_mem[:, 1024:2048].rearrange("p (a h s) -> p a h s", a=2, h=2)
        RT = sb("RT", [P, T, C, P])
        RV = sb("RV", [P, H, 2 * R])
        OT = sb("OT", [P, C, S])
        rinv = sb("rinv", [P, H, DK])

        small = {}
        for th in "AB":
            small[th] = dict(st6=sb("st6" + th, [P, T, 6]), mv=sb("mv" + th, [P, T, 2]), ve=sb("ve" + th, [P, T]), rs=sb("rs" + th, [P, T]),
                             nm=sb("nm" + th, [P, 2 * PAIRS]), sums=sb("sums" + th, [P, T, H]))
        small["P"] = small["A"]
        mx = sb("mx", [P, 2 * PAIRS])
        oh = sb("oh", [P, T, E])
        lg = sb("lg", [P, T, E])
        lmax = sb("lmax", [P, T])
        gate = sb("gate", [P, 1])
        oh12 = sb("oh12", [P, T, 3, E], BF16)
        ohT = sb("ohT", [3 * E, S], BF16)
        hold = sb("hold", [P, 1])
        am = sb("am", [P, 3, T])
        wsum = sb("wsum", [P, 2])

        def split_room(mem, at):
            return (mem[:, at:at + C * S].rearrange("p (c s) -> p c s", c=C), mem[:, at + C * S:at + 2 * C * S].rearrange("p (c s) -> p c s", c=C),
                    mem[:, at + 2 * C * S:at + 7 * C * S // 2].bitcast(BF16).rearrange("p (i c s) -> p i c s", i=3, c=C))
        et_mem = ET[:, :, :, :].rearrange("p t h q -> p (t h q)")
        room_a = [split_room(et_mem, 0), split_room(et_mem, H * P), split_room(wt_mem[:, :], 2048)]
        room_b = [split_room(q1_mem[:, :], 0)] * 2

        PS = stack.enter_context(nc.psum_tensor("PS", [P, 8, 512], F32))
        PW0, PO, RVB, FB0, FB1 = 2, 4, 5, 6, 7

        def bank(n):
            return PS[:, n, :]

        def halves(n, a=C):
            return bank(n).rearrange("p (c s) -> p c s", c=a)

        scr = {"A": dict(q=dram("q_scr", (3, C, P, S), BF16), k=[dram(f"k_scr{v}", (3, C, P, S), BF16) for v in range(T)]),
               "B": dict(q=dram("qb_scr", (3, C, P, S), BF16), k=[dram("kb_scr", (3, C, P, S), BF16)])}
        rv_scr = dram("rv_scr", (T, H, DK, P))
        relv_small = dram("relv_small", (3, NREL, DK))
        relv_pad = dram("relv_pad", (3, XN, DK))

        sems = {("A", n): new_sem("a_" + n) for n in PER_A}
        sems.update({("B", n): new_sem("b_" + n) for n in PER_B})
        PER = {k: (PER_A if k[0] == "A" else PER_B)[k[1]] for k in sems}
        SHIFT = {"A": 0, "P": 1, "B": -1, "a": -1, "b": -2}
        raised = dict.fromkeys(PER, 0)
        batches_setup = new_sem("batches_setup")
        w_loaded, aux_loaded, const_made = new_sem("w_loaded"), new_sem("aux_loaded"), new_sem("const_made")
        big_loaded, sync_passed = new_sem("big_loaded"), new_sem("sync_passed")
        wtr_psum, wtr_sbuf = new_sem("wtr_psum"), new_sem("wtr_sbuf")
        rel_step, rel_dma, setup_dve = new_sem("rel_step"), new_sem("rel_dma"), new_sem("setup_dve")
        relk_done, relv_tab, abs_psum, setup_act = new_sem("relk_done"), new_sem("relv_tab"), new_sem("abs_psum"), new_sem("setup_act")
        relk_loaded, b1_done, b1_loaded = new_sem("relk_loaded"), new_sem("b1_done"), new_sem("b1_loaded")

        def sem_of(thread, name):
            return ("B" if thread in "Bb" else "A", name)

        def sig(ins, thread, name, by=1):
            ins.then_inc(sems[sem_of(thread, name)], by)
            raised[sem_of(thread, name)] += by

        def waiter(eng, it, off, carrier=None):
            def wait(thread, *names, n=None):
                for name in names:
                    key = sem_of(thread, name)
                    per = PER[key]
                    value = (off + SHIFT[thread] + (1 if key[0] == "B" else 0)) * per + (per if n is None else n)
                    assert n is None or 0 < n <= per, (key, n)
                    if isinstance(it, int):
                        if 0 <= it + off + SHIFT[thread] < B:
                            eng.wait_ge(sems[key], it * per + value)
                    else:
                        assert value > 0, (key, value)
                        eng.wait_ge(sems[key], it * per + value)
                        if carrier is not None:
                            eng.nop().then_inc(carrier, 1)
            return wait

        def iterations(eng, body, after_first=None, before_loop=None, after_start=None):
            def setup(more):
                if more is not None:
                    more()

            body(0, -1, order(-1)[1:4])
            setup(after_start)
            body(0, -1, order(-1)[4:])
            setup(after_first)
            body(0, 0, order(0))
            setup(before_loop)
            with eng.Fori(0, B - 2) as it:
                assert order(1) == order(B - 2)
                body(it, 1, order(1))
            body(0, B - 1, order(B - 1))
            body(0, B, order(B))

        k1f = k1_mem[:, :]
        rk = k1f[0:DK, 0:NREL]
        rkd = k1f[0:DK, 64:64 + 3 * NREL].rearrange("p (a b) -> p a b", a=3)
        rkpad = k1f[0:DK, 256:256 + 3 * XN].rearrange("p (a b) -> p a b", a=3)
        rkres = k1f[0:DK, 256 + 3 * XN:256 + 6 * XN].rearrange("p (a b) -> p a b", a=3)
        rkP = [W[0:DK, i, :, :].rearrange("p h s -> p (h s)").bitcast(BF16)[:, 0:3 * XN].rearrange("p (a b) -> p a b", a=3) for i in range(3)]
        rv3 = Z[0:NREL, 0, 0:3 * DK].rearrange("p (a d) -> p a d", a=3)
        rvb = Z[0:NREL, 1, 0:2 * DK].rearrange("p (a d) -> p a d", a=2)
        rvrow = OT[:, 0, 0:2 * DK].rearrange("p (a d) -> p a d", a=2)
        b1v = [q1_mem[0:E, i * I:(i + 1) * I] for i in range(2)]
        b1bf = [m[0:E, :, :].rearrange("p t d -> p (t d)").bitcast(BF16) for m in (Y, XNB, MA)]
        wb = CTB[:, :, :]
        wbq = XTB[:, :, :]
        wbbf = FB[:, 0, :].bitcast(BF16).rearrange("p (t d) -> p t d", t=T)
        ones = FB[:, 1, 0:P]
        WST = wt_mem[:, :].rearrange("p (m o d) -> p m o d", m=8, o=C)

        block = stack.enter_context(nc.Block())
        AUX = 16 * (6 + 2 * 3 + 2 + 4)
        CONSTS = 7 + 1 + T * E

        @block.sync
        def _(sp):
            def body(it, first, steps):

                def batch_of(t, thread):
                    at = off + SHIFT[thread]
                    return t[at:at + 1] if isinstance(it, int) else t[at:B][bass.ds(it, 1)]

                def tiles(ap):
                    return ap.rearrange("o (t p) d -> p (o t) d", p=P)

                def write(thread, kind, room, dst, o, done):
                    wait(thread, "part2", "part3", n=o + 1)
                    if o < 2 or thread == "B":
                        wait({"P": "A", "B": "b"}[thread], kind + "_stacked")
                    sig(sp.dma_start(dst.rearrange("i g p t -> p (i g) t"), room[2].rearrange("p i g t -> p (i g) t")), thread, done, 16)

                def stack_up(thread, kind, src, dst):
                    for j, part in enumerate(QPART if kind == "q" else KPART):
                        sig(sp.dma_start(dst[j * DK:(j + 1) * DK, :, :], src[part].rearrange("g (h d) t -> d (g h) t", d=DK)), thread, kind + "_stacked", 16)

                for ahead, thread, step, n in steps:
                    off = first + ahead
                    wait = waiter(sp, it, off, sync_passed)
                    if (thread, step) == ("P", "load"):
                        wait("A", "xT_psum")
                        sig(sp.dma_start(CT[:, :, :], tiles(batch_of(ctx_in, "P"))), "P", "ctx_loaded", 16)
                        wait("A", "base")
                        sig(sp.dma_start(X[:, :, :], tiles(batch_of(x, "P"))), "P", "x_loaded", 16)
                    elif (thread, step) == ("P", "part3"):
                        kind, v = [("q", 0), ("k", 0), ("k", 1)][n]
                        write("P", kind, room_a[n], scr["A"]["k"][v] if kind == "k" else scr["A"]["q"], n, ("q_written", "k0_written", "k1_written")[n])
                    elif (thread, step) == ("P", "k_stack"):
                        for v in range(T):
                            wait("P", f"k{v}_written")
                            stack_up("P", "k", scr["A"]["k"][v], KS[:, v, :, :])
                    elif (thread, step) == ("P", "q_stack"):
                        wait("P", "q_written")
                        wait("A", "scores")
                        stack_up("P", "q", scr["A"]["q"], QS[:, :, :])
                    elif (thread, step) == ("A", "R") and n % 4 == 3:
                        qt = n // 4
                        wait("A", "relv_sbuf", n=qt + 1)
                        if qt == 0:
                            wait("a", "relv_loaded")
                        for j in range(4):
                            sig(sp.dma_start(rv_scr[qt].rearrange("h d q -> d h q")[:, :, j * 2 * R:(j + 1) * 2 * R],
                                             RV[2 * R * j:2 * R * j + DK, :, :]), "A", "relv_written", 16)
                    elif (thread, step) == ("A", "relv_load"):
                        wait("A", "relv_written")
                        wait("B", "xT_psum")
                        for qt in range(T):
                            sig(sp.dma_start(RVC[:, :, qt * P:(qt + 1) * P], rv_scr[qt].rearrange("(g h) d q -> (h d) g q", g=C)), "A", "relv_loaded", 16)
                    elif (thread, step) == ("B", "mask") and n == 0:
                        wait("b", "mask_scaled")
                        sig(sp.dma_start(MK[:, :, :], tiles(batch_of(mask, "B"))), "B", "mask_loaded", 16)
                    elif (thread, step) == ("B", "part3"):
                        write("B", "kq"[n], room_b[n], scr["B"]["k"][0] if n == 0 else scr["B"]["q"], n, "kq"[n] + "_written")
                    elif (thread, step) == ("B", "l1_stack"):
                        if n == 0:
                            wait("B", "k_written")
                            wait("B", "h_psum")
                        else:
                            wait("B", "q_written")
                        stack_up("B", "kq"[n], scr["B"]["k"][0] if n == 0 else scr["B"]["q"], (KSB, QSB)[n])
                    elif (thread, step) == ("B", "bit"):
                        wait("B", "out_sbuf")
                        sig(sp.dma_start(tiles(batch_of(out, "B")), FB[:, :, :]), "B", "stored", 16)
            for m, w in enumerate([Wq0, Wk0, Wv0, Wo0, Wq1, Wk1, Wv1, Wo1]):
                sp.dma_start(WST[:, m, :, :], w.rearrange("(o p) d -> p o d", p=P)).then_inc(w_loaded, 16)
            sp.dma_start(wb, Wb.rearrange("(o p) d -> p o d", p=P)).then_inc(w_loaded, 16)
            body(0, -1, order(-1)[0:1])
            sp.wait_ge(relk_done, 1)
            for j, part in enumerate(KPART):
                sp.dma_start(relk_st[j * DK:(j + 1) * DK, :, :], rkP[part]).then_inc(relk_loaded, 16)


            def after_first():
                sp.wait_ge(rel_step, 1)
                for a in range(3):
                    sp.dma_start(relv_small[a], rv3[:, a, :]).then_inc(rel_dma, 16)
                sp.wait_ge(rel_dma, 48)
                low, mid = -R - XLO + 1, NREL - 2
                for a in range(3):
                    sp.dma_start(relv_pad[a, 0:low, :], relv_small[a, 0:1, :].broadcast_to([low, DK])).then_inc(rel_dma, 16)
                    sp.dma_start(relv_pad[a, low:low + mid, :], relv_small[a, 1:1 + mid, :]).then_inc(rel_dma, 16)
                    sp.dma_start(relv_pad[a, low + mid:XN, :], relv_small[a, NREL - 1:NREL, :].broadcast_to([XN - low - mid, DK])).then_inc(rel_dma, 16)
                sp.wait_ge(rel_dma, 48 + 144)

                def toeplitz(a, first, n):
                    return bass.AP(relv_pad.tensor, (a * XN + first) * DK, [[DK, P], [1, n * DK]])
                sp.dma_start(relv_d[:, :, :].rearrange("p s d -> p (s d)"), toeplitz(0, -(P - 1) - XLO, P + 1)).then_inc(relv_tab, 16)
                sp.dma_start(relv_o[:, 0, :, :].rearrange("p s d -> p (s d)"), toeplitz(1, 1 - XLO, R + 1)).then_inc(relv_tab, 16)
                sp.dma_start(relv_o[:, 1, :, :].rearrange("p s d -> p (s d)"), toeplitz(2, -(P + R - 1) - XLO, R + 1)).then_inc(relv_tab, 16)
                sp.wait_ge(b1_done, 1)
                for i in range(3):
                    sp.dma_start(b1p[i * E:(i + 1) * E, :], b1bf[i]).then_inc(b1_loaded, 16)
                sp.wait_ge(b1_loaded, 48)
                sp.wait_ge(setup_dve, 2)
            iterations(sp, body, after_first)
            sp.wait_ge(sems["B", "stored"], (1 + B) * 16)

        @block.gpsimd
        def _(pool):
            G = nc.gpsimd
            G.memset(ident[:, :], 0.0).then_inc(const_made, 1)
            G.memset(ones, 1.0).then_inc(const_made, 1)
            G.memset(halfs[:, :], -0.5).then_inc(const_made, 1)
            G.memset(V2[:, :, :, :, :], 0.0).then_inc(const_made, 1)
            G.memset(V2B[:, :, :, :], 0.0).then_inc(const_made, 1)
            pool.wait_ge(const_made, 5)
            G.memset(EC, 0.0).then_inc(const_made, 1)
            pool.wait_ge(const_made, 6)
            G.affine_select(out=ident[:, :], in_=ident[:, :], compare_op=ALU.not_equal, fill=1.0, base=0,
                            pattern=[[-1, P]], channel_multiplier=1).then_inc(const_made, 1)
            pool.wait_ge(const_made, 7)
            G.tensor_copy(ident_bf[:, :], ident[:, :]).then_inc(const_made, 1)
            for t in range(T):
                for e in range(E):
                    G.memset(firsts[:, t, e:e + 1], float(E - e)).then_inc(const_made, 1)
            pool.wait_ge(aux_loaded, AUX)
            pool.wait_ge(w_loaded, 16 * 9)
            pool.dma_start(w1[:, :, :, :], W1.rearrange("e (c p) i -> p e c i", p=P)).then_inc(big_loaded, 16)
            pool.dma_start(wf[:, :, :], Wf.rearrange("(i p) d -> p i d", p=P)).then_inc(big_loaded, 16)
            pool.wait_ge(const_made, CONSTS)
            for n, times in PER_B.items():
                pool.nop().then_inc(sems["B", n], times)
            pool.nop().then_inc(batches_setup, 1)

            def body(it, first, steps):

                def power(thread, n):
                    m = small[thread]
                    wait(thread, "stats", n=4 * (n + 1))
                    sig(G.tensor_tensor(m["rs"][:, :], m["ve"][:, :], halfs[:, :], ALU.pow), thread, "rstd")

                def carry():
                    G.tensor_tensor(hold[:, :], halfs[:, 0:1], halfs[:, 1:2], ALU.add)

                def add_row(dst, src, row):
                    return G.tensor_tensor(dst[:, :, :], src[:, :, :], rows[:, row:row + 1, :].broadcast_to([P, T, D]), ALU.add)

                for ahead, thread, step, n in steps:
                    off = first + ahead
                    wait = waiter(pool, it, off)
                    if step == "stats":
                        power(thread, n)
                    elif (thread, step) == ("B", "ffn_sum"):
                        power("B", 1)
                    elif (thread, step) == ("P", "resid"):
                        full, resid, part = room_a[n]
                        wait("P", "part1", n=n + 1)
                        sig(G.tensor_tensor(resid, full, part[:, 0, :, :], ALU.subtract), "P", "resid")
                    elif (thread, step) == ("P", "part3"):
                        full, resid, part = room_a[n]
                        wait("P", "part2", n=n + 1)
                        sig(G.tensor_tensor(part[:, 2, :, :], resid, part[:, 1, :, :], ALU.subtract), "P", "part3")
                    elif (thread, step) == ("A", "scale"):
                        wait("A", "relv_loaded", "wT_sbuf")
                        sig(G.tensor_tensor(RVC.rearrange("p g (t q) -> p g t q", t=T), RVC.rearrange("p g (t q) -> p g t q", t=T),
                                            RT[:, :, :, :].rearrange("p t g q -> p g t q"), ALU.mult), "A", "relv_scaled")
                    elif (thread, step) == ("P", "base"):
                        wait("P", "x_loaded")
                        wait("A", "x1_ready")
                        sig(add_row(XO, X, BO0), "P", "base")
                    elif (thread, step) == ("A", "copy"):
                        wait("B", "k_psum", "v_psum")
                        wait("A", "ctxT_sbuf")
                        carry()
                        sig(G.tensor_copy(CTB[:, :, :], CTT[:, :, :]), "A", "ctx_copied")
                    elif (thread, step) == ("B", "ffn_xT"):
                        wait("B", "xn_ready", n=1)
                        wait("b", "stored")
                        sig(add_row(FB, XNB, BF_), "B", "ffn_base")
                    elif (thread, step) == ("B", "ffn_end"):
                        wait("B", "x2_ready")
                        sig(add_row(FB, Z, BO1), "B", "base")
                    elif (thread, step) == ("B", "mask") and n == 1:
                        wait("B", "mask_loaded")
                        wait("b", "masked")
                        carry()
                        sig(G.tensor_scalar(MA[:, :, :], MK[:, :, :], MASKED, None, ALU.mult), "B", "mask_scaled")
                        wait("B", "mask_scaled")
                        carry()
                        for t in range(T):
                            sig(G.affine_select(out=MA[:, t, :], in_=MA[:, t, :], compare_op=ALU.is_ge, fill=MASKED,
                                                base=t * P, pattern=[[-1, S]], channel_multiplier=1), "B", "mask_ready")

            def after_first():
                pool.wait_ge(setup_dve, 2)
            iterations(pool, body, after_first, lambda: pool.wait_ge(b1_loaded, 48))

        @block.scalar
        def _(act):
            A = nc.scalar
            act.dma_start(rk, relk.rearrange("r d -> d r"), allow_slow_non_contiguous=True).then_inc(aux_loaded, 16)
            act.dma_start(rv3[:, 0, :], relv).then_inc(aux_loaded, 16)
            for a, r in enumerate([0, NREL - 1]):
                act.dma_start(rvb[:, a, :], relv[r].partition_broadcast(NREL)).then_inc(aux_loaded, 16)
                act.dma_start(rvrow[:, a, :], relv[r].partition_broadcast(P)).then_inc(aux_loaded, 16)
                act.dma_start(chb[:, 2 + a, 0:1], bass.AP(relk.tensor, r * DK, [[0, P // DK], [1, DK], [1, 1]])).then_inc(aux_loaded, 16)
            act.dma_start(b1v[0], b1).then_inc(aux_loaded, 16)
            for a, b_ in enumerate([bq0, bk0]):
                act.dma_start(chb[:, a, :], b_.rearrange("(g p) -> p g", p=P), allow_slow_non_contiguous=True).then_inc(aux_loaded, 16)
            for row, src in [(BV_D, bv0), (BO0, bo0), (BF_, bf), (GAMMA, gamma), (BETA, beta), (BO1, bo1)]:
                act.dma_start(rows[:, row, :], src.partition_broadcast(P)).then_inc(aux_loaded, 16)
            act.dma_start(wr[:, :, :], Wr.rearrange("(c p) e -> p c e", p=P)).then_inc(aux_loaded, 16)
            for m in range(8):
                act.wait_ge(wtr_psum, m + 1)
                A.activation(wT[:, m, :, :], halves(m % 4), ACT.Copy).then_inc(wtr_sbuf, 1)
            act.wait_ge(batches_setup, 1)
            act.wait_ge(setup_dve, 1)

            def body(it, first, steps):

                def cut(thread, step, o):
                    full, resid, part = (room_a if thread == "P" else room_b)[o]
                    if step == "part1":
                        wait(thread, "f32_ready", n=o + 1)
                        sig(A.activation(part[:, 0, :, :], full, ACT.Copy), thread, "part1")
                    else:
                        wait(thread, "resid", n=o + 1)
                        sig(A.activation(part[:, 1, :, :], resid, ACT.Copy), thread, "part2")

                def exponentials(thread, p):
                    m = small[thread]
                    qt = p // QPAIRS
                    nk = S if thread == "A" or qt else P
                    wait(thread, "negmax", n=p + 1)
                    if p >= W_RING:
                        wait(thread, "wT_psum", n=slot(p - W_RING) + 1)
                    elif p == 0 and thread == "A":
                        wait("a", "wT_psum", "rinv")
                        wait("b", "wT_psum")
                    elif p == 0:
                        wait(other, "wT_psum")
                        wait("b", "rinv")
                    for i in range(2):
                        h = 2 * p + i
                        src = bank(p % 2)[:, i * S:i * S + nk] if thread == "A" else SM[:, p % 2, i, 0:nk]
                        sig(A.activation(W[:, p % W_RING, i, 0:nk], src, ACT.Exp, bias=m["nm"][:, h:h + 1],
                                         scale=1.0 if thread == "A" else DK ** -0.5,
                                         accum_out=m["sums"][:, qt, h % H:h % H + 1]), thread, "exped")

                for ahead, thread, step, n in steps:
                    off = first + ahead
                    wait = waiter(act, it, off)
                    with_a = not isinstance(it, int) or 0 <= off < B
                    other = "A" if with_a else "b"
                    if (thread, step) == ("P", "ctxT"):
                        wait("P", "ctxT_psum")
                        wait("A", "k_psum", "v_psum", "ctx_copied")
                        sig(A.activation(CTT[:, :, :], halves(6), ACT.Copy), "P", "ctxT_sbuf")
                    elif (thread, step) == ("P", "xT"):
                        wait("P", "xT_psum")
                        wait("A", "q_psum")
                        sig(A.activation(XT[:, :, :], halves(6), ACT.Copy), "P", "xT_sbuf")
                    elif (thread, step) == ("P", "f32") and n == 0:
                        wait("P", "q_psum")
                        wait("A", "scores", n=QPAIRS)
                        for g in range(C):
                            ins = A.activation(room_a[0][0][:, g, :], halves(6)[:, g, :], ACT.Identity, bias=chb[:, 0, g:g + 1])
                        sig(ins, "P", "f32_ready")
                    elif (thread, step) == ("P", "f32"):
                        v = n - 1
                        wait("P", "k_psum")
                        wait("A", "scores")
                        if v == 1:
                            wait("A", "relv_psum", "pv_psum")
                        for g in range(C):
                            for kt in range(T):
                                col = 1 if kt == v else (5 if kt > v else 4)
                                ins = A.activation(room_a[n][0][:, g, kt * P:(kt + 1) * P], halves(7)[:, g, kt * P:(kt + 1) * P], ACT.Identity, bias=chb[:, col, g:g + 1])
                        sig(ins, "P", "f32_ready")
                    elif step in ("part1", "part2"):
                        cut(thread, step, n)
                    elif (thread, step) == ("P", "rel"):
                        wait("P", "rel_psum", n=n + 1)
                        if n % 4 == 0 and n < 8:
                            wait("P", ("q_written", "k0_written")[n // 4])
                        if n == 0:
                            wait("P", "part3", n=1)
                        if n < 8:
                            sig(A.activation(ET[:, n // 4, :, (n % 4) * 32:(n % 4 + 1) * 32],
                                             bank(6 + n % 2).rearrange("p (q h) -> p h q", h=H), ACT.Copy), "P", "rel_sbuf")
                        else:
                            for t in range(T):
                                at = R if t == 0 else 0
                                sig(A.activation(EC[:, t, :, at:at + R],
                                                 bank(6)[EC0:EC0 + R, t * 256:(t + 1) * 256].rearrange("p (q h) -> p h q", h=H), ACT.Copy), "P", "rel_sbuf")
                    elif (thread, step) == ("A", "S"):
                        exponentials("A", n)
                    elif (thread, step) == ("A", "R") and n % 4 == 3:
                        qt = n // 4
                        wait("A", "relv_psum", n=qt + 1)
                        if qt == 0:
                            wait("a", "relv_written")
                        else:
                            wait("A", "relv_written", n=64)
                        sig(A.activation(RV[:, :, :], bank(RVB).rearrange("p (q h) -> p h q", h=H), ACT.Copy), "A", "relv_sbuf")
                    elif (thread, step) == ("B", "ffn_xT"):
                        wait("B", "xT_psum", n=1)
                        wait("b", "q_psum")
                        sig(A.activation(XTB[:, :, :], halves(6), ACT.Copy), "B", "xT_sbuf")
                    elif (thread, step) == ("B", "gelu"):
                        wait("B", "h_psum", n=n + 1)
                        if n == 0:
                            wait("b", "bit_psum")
                        sig(A.activation(GT[:, 2 * n:2 * n + 2, :], bank(6 + n % 2).rearrange("p (i s) -> p i s", i=2), ACT.Gelu), "B", "gelu")
                    elif (thread, step) == ("B", "l1_xT"):
                        wait("B", "xT_psum", n=2)
                        wait("B", "x_expert", "logits")
                        sig(A.activation(XTB[:, :, :], halves(7), ACT.Copy), "B", "xT_sbuf")
                    elif (thread, step) == ("B", "l1_f32"):
                        if n == 0:
                            wait("B", "k_psum", "ffn_psum")
                        else:
                            wait("B", "q_psum", "k_written")
                        sig(A.activation(room_b[n][0], halves(7), ACT.Copy), "B", "f32_ready")
                    elif (thread, step) == ("B", "l1_S"):
                        exponentials("B", n)
            iterations(act, body, lambda: act.wait_ge(setup_dve, 2))

        @block.vector
        def _(dve):
            V = nc.vector
            done = [0]

            def after(ins):
                done[0] += 1
                ins.then_inc(setup_act, 1)
                dve.wait_ge(setup_act, done[0])

            dve.wait_ge(batches_setup, 1)
            after(V.tensor_tensor(rv3[:, 1, :], rv3[:, 0, :], rvb[:, 1, :], ALU.subtract))
            V.tensor_tensor(rv3[:, 2, :], rv3[:, 0, :], rvb[:, 0, :], ALU.subtract).then_inc(rel_step, 1)
            bvh = rows[:, BV_D, :].rearrange("p (h d) -> p h d", h=H)
            after(V.tensor_tensor(rows[:, BV_O0, :].rearrange("p (h d) -> p h d", h=H), bvh, rvrow[:, 0:1, :].broadcast_to([P, H, DK]), ALU.add))
            after(V.tensor_tensor(rows[:, BV_O1, :].rearrange("p (h d) -> p h d", h=H), bvh, rvrow[:, 1:2, :].broadcast_to([P, H, DK]), ALU.add))
            for a in range(2):
                after(V.tensor_scalar(chb[:, 4 + a, :], chb[:, 1, :], chb[:, 2 + a, 0:1], None, ALU.add))
            dve.nop().then_inc(setup_dve, 1)

            def relative_keys():
                after(V.tensor_copy(rkd[:, 0, :], rk))
                after(V.tensor_scalar(rkd[:, 1, :], rk, rk[:, NREL - 1:NREL], None, ALU.subtract))
                after(V.tensor_scalar(rkd[:, 2, :], rk, rk[:, 0:1], None, ALU.subtract))
                low, mid = -R - XLO + 1, NREL - 2
                for a in range(3):
                    after(V.tensor_copy(rkpad[:, a, 0:low], rkd[:, a, 0:1].broadcast_to([DK, low])))
                    after(V.tensor_copy(rkpad[:, a, low:low + mid], rkd[:, a, 1:1 + mid]))
                    after(V.tensor_copy(rkpad[:, a, low + mid:XN], rkd[:, a, NREL - 1:NREL].broadcast_to([DK, XN - low - mid])))
                after(V.tensor_copy(rkP[0], rkpad))
                after(V.tensor_tensor(rkres, rkpad, rkP[0], ALU.subtract))
                after(V.tensor_copy(rkP[1], rkres))
                after(V.tensor_tensor(rkP[2], rkres, rkP[1], ALU.subtract))
                dve.nop().then_inc(relk_done, 1)

            def rest_of_setup():
                after(V.tensor_copy(b1bf[0], b1v[0]))
                after(V.tensor_tensor(b1v[1], b1v[0], b1bf[0], ALU.subtract))
                after(V.tensor_copy(b1bf[1], b1v[1]))
                after(V.tensor_tensor(b1bf[2], b1v[1], b1bf[1], ALU.subtract))
                dve.nop().then_inc(b1_done, 1)
                dve.wait_ge(w_loaded, 16 * 9)
                after(V.tensor_reduce(wsum[:, 0:1], wb, AX.XY, ALU.add, apply_absolute_value=True))
                dve.nop().then_inc(abs_psum, 1)
                dve.wait_ge(abs_psum, 2)
                after(V.tensor_scalar(wscale[:, :], bank(7)[:, 0:1], 1.0 / (D * D), BIT_EPS, ALU.mult, ALU.add))
                after(V.reciprocal(wsum[:, 1:2], wscale[:, :]))
                after(V.tensor_scalar(wbq, wb, wsum[:, 1:2], ROUND, ALU.mult, ALU.add))
                after(V.tensor_scalar(wbq, wbq, -ROUND, 1.0, ALU.add, ALU.min))
                after(V.tensor_scalar(wbbf, wbq, -1.0, None, ALU.max))
                dve.nop().then_inc(abs_psum, 1)
                dve.wait_ge(abs_psum, 4)
                after(V.tensor_copy(wbT[:, :, :], bank(7)[:, 0:D].bitcast(BF16).rearrange("p (c d) -> p c d", c=C)))
                dve.nop().then_inc(setup_dve, 1)

            def body(it, first, steps):

                def stats(thread, n, src, eps):
                    m = small[thread]
                    for t in range(T):
                        ins = V.bn_stats(m["st6"][:, t, :], src[:, t, :])
                    sig(ins, thread, "stats")
                    wait(thread, "stats", n=4 * n + 1)
                    V.memset(gate[:, :], 0.0)
                    for t in range(T):
                        ins = V.bn_aggr(m["mv"][:, t, :], m["st6"][:, t, :])
                    sig(ins, thread, "stats", 2)
                    wait(thread, "stats", n=4 * n + 3)
                    sig(V.tensor_scalar(m["ve"][:, :], m["mv"][:, :, 1], eps, None, ALU.add), thread, "stats")

                def normed(thread, n, src, dst):
                    m = small[thread]
                    wait(thread, "rstd", n=n + 1)
                    for t in range(T):
                        ins = V.tensor_scalar(dst[:, t, :], src[:, t, :], m["mv"][:, t, 0:1], m["rs"][:, t:t + 1], ALU.subtract, ALU.mult)
                    sig(ins, thread, "xn_ready")

                def cut(thread, step, o):
                    full, resid, part = room_b[o]
                    if step == "resid":
                        wait(thread, "part1", n=o + 1)
                        sig(V.tensor_tensor(resid, full, part[:, 0, :, :], ALU.subtract), thread, "resid")
                    else:
                        wait(thread, "part2", n=o + 1)
                        sig(V.tensor_tensor(part[:, 2, :, :], resid, part[:, 1, :, :], ALU.subtract), thread, "part3")

                def largest(thread, p):
                    nm = small[thread]["nm"]
                    wait(thread, "scores", n=p + 1)
                    sv = bank(p % 2).rearrange("p (h s) -> p h s", h=2)
                    if thread == "A":
                        sig(V.tensor_reduce(nm[:, 2 * p:2 * p + 2], sv, AX.X, ALU.max, negate=True), thread, "negmax")
                        return
                    qt = p // QPAIRS
                    nk = S if qt else P
                    if p >= 2:
                        wait("B", "exped", n=2 * (p - 1))
                    elif p == 0:
                        wait("B", "mask_ready")
                        if with_a:
                            wait("A", "relv_psum", "pv_psum")
                        else:
                            wait("b", "exped")
                    V.memset(gate[:, :], 0.0)
                    for i in range(2):
                        ins = V.tensor_tensor_reduce(out=SM[:, p % 2, i, 0:nk], in0=sv[:, i, 0:nk], in1=MA[:, qt, 0:nk], scale=1.0,
                                                     scalar=-3.0e38, op0=ALU.add, op1=ALU.max, accum_out=mx[:, 2 * p + i:2 * p + i + 1])
                    sig(ins, "B", "masked")
                    wait("B", "masked", n=p + 1)
                    sig(V.tensor_scalar(nm[:, 2 * p:2 * p + 2], mx[:, 2 * p:2 * p + 2], -(DK ** -0.5), None, ALU.mult), "B", "negmax")

                def probs_T(thread, p):
                    qt, hp = p // QPAIRS, p % QPAIRS
                    nk = T if thread == "A" or qt else 1
                    wait(thread, "wT_psum", n=slot(p) + 1)
                    src = bank(PW0 + slot(p) % 2).rearrange("p (h k q) -> p k h q", h=2, k=T)[:, 0:nk, :, :]
                    if thread == "A":
                        if p == 0:
                            wait("a", "relv_psum", "pv_psum")
                            wait("b", "weighed", "exped")
                            wait("A", "k1_written")
                        elif p == QPAIRS:
                            wait("A", "relv_psum", "pv_psum", n=1)
                        sig(V.tensor_copy(WT_[:, 0:nk, 2 * hp:2 * hp + 2, :], src), "A", "wT_sbuf")
                    else:
                        if p >= 2:
                            wait("B", "weighed", n=p - 1)
                        elif not with_a:
                            wait("b", "weighed")
                        sig(V.tensor_copy(WTB[:, p % 2, 0:nk, :, :], src), "B", "wT_sbuf")

                def inverse(thread, qt):
                    sums = small[thread]["sums"][:, qt, :]
                    wait(thread, "exped", n=(qt + 1) * H)
                    sig(V.reciprocal(sums, sums), thread, "inverted")
                    if qt:
                        wait(thread, "wT_psum", n=INV_SLOT[0] + 1)
                    elif thread == "A":
                        wait("a", "wT_psum")
                        wait("b", "wT_psum")
                    else:
                        wait(other, "wT_psum")
                    wait(thread, "inverted", n=qt + 1)
                    each = sums.unsqueeze(2).broadcast_to([P, H, DK])
                    if thread == "A":
                        sig(V.tensor_copy(rinv[:, :, :], each), "A", "rinv")
                    else:
                        sig(V.scalar_tensor_tensor(out=rinv[:, :, :], in0=mx[:, qt * H:(qt + 1) * H].unsqueeze(2).broadcast_to([P, H, DK]), scalar=0.5 * MASKED,
                                                   in1=each, op0=ALU.is_gt, op1=ALU.mult), "B", "rinv")

                def inverse_T(thread, qt):
                    wait(thread, "wT_psum", n=INV_SLOT[qt] + 1)
                    sig(V.tensor_copy(RT[:, qt, :, :], bank(PW0 + INV_SLOT[qt] % 2)[:, 0:D].rearrange("p (g q) -> p g q", g=C)), thread, "wT_sbuf")

                po = bank(PO).rearrange("p (t g q) -> p g t q", t=T, g=C)
                ot = OT[:, :, :].rearrange("p g (t q) -> p g t q", t=T)
                rt = RT[:, :, :, :].rearrange("p t g q -> p g t q")

                for ahead, thread, step, n in steps:
                    off = first + ahead
                    wait = waiter(dve, it, off)
                    with_a = not isinstance(it, int) or 0 <= off < B
                    other = "A" if with_a else "b"
                    if (thread, step) == ("P", "stats"):
                        wait("P", "x_loaded")
                        stats("P", 0, X, LN_EPS)
                    elif (thread, step) == ("P", "normed"):
                        wait("P", "ctxT_psum")
                        normed("P", 0, X, CT)
                    elif (thread, step) == ("P", "v"):
                        wait("P", "v_psum")
                        wait("A", "pv_psum")
                        vp = bank(5).rearrange("p (k h a d) -> p k h a d", k=T, a=2, d=DK)
                        for a in range(2):
                            for var in range(2):
                                dst = V2[:, var, :, :, :].rearrange("p k (h a) d -> p k h a d", a=2)[:, :, :, a, a * DK:(a + 1) * DK]
                                low_row, high_row = (BV_D, BV_D) if var == 0 else (BV_O0, BV_O1)
                                row = rows[:, low_row:high_row + 1, :].rearrange("p k (h a d) -> p k h a d", a=2, d=DK)[:, :, :, a, :]
                                if var == 0:
                                    row = row.broadcast_to([P, T, H // 2, DK])
                                sig(V.tensor_tensor(dst, vp[:, :, :, a, :], row, ALU.add), "P", "v_sbuf")
                    elif thread == "B" and step in ("resid", "part3"):
                        cut(thread, step, n)
                    elif step == "S" or step == "l1_S":
                        largest(thread, n)
                    elif step == "T" or step == "l1_T":
                        probs_T(thread, n)
                    elif step == "N" or step == "l1_N":
                        inverse(thread, n)
                    elif step == "I" or step == "l1_I":
                        inverse_T(thread, n)
                    elif (thread, step) == ("A", "unload"):
                        wait("A", "pv_psum", "wT_sbuf")
                        wait("b", "y_psum")
                        wait("a", "y_psum")
                        sig(V.tensor_tensor(ot, po, rt, ALU.mult), "A", "unloaded")
                    elif (thread, step) == ("A", "finish"):
                        wait("A", "relv_scaled", "unloaded")
                        sig(V.tensor_tensor(OT[:, :, :], OT[:, :, :], RVC, ALU.add), "A", "oT")
                    elif (thread, step) == ("A", "output"):
                        wait("A", "y_psum", "base")
                        if off == 0:
                            dve.wait_ge(b1_loaded, 48)
                        wait("B", "x2_ready")
                        sig(V.tensor_tensor(Y[:, :, :], halves(RVB), XO[:, :, :], ALU.add), "A", "x1_ready")
                    elif (thread, step) == ("B", "stats"):
                        if n == 0:
                            wait("a", "x1_ready")
                        stats("B", n, (Y, None, Z, Z)[n], LN_EPS)
                    elif (thread, step) == ("B", "normed"):
                        if n == 0:
                            wait("b", "aq")
                        normed("B", n, (Y, None, Z, Z)[n], XNB)
                    elif (thread, step) == ("B", "router"):
                        wait("B", "logits")
                        wait("b", "ohT_psum")
                        lp = bank(7)[:, 0:T * E].rearrange("p (t e) -> p t e", t=T)
                        sig(V.tensor_reduce(lmax[:, :], lp, AX.X, ALU.max), "B", "route")
                        wait("B", "route", n=1)
                        for t in range(T):
                            ins = V.tensor_scalar(lg[:, t, :], lp[:, t, :], lmax[:, t:t + 1], None, ALU.is_ge)
                        sig(ins, "B", "route")
                        wait("B", "route", n=2)
                        sig(V.tensor_tensor(lg[:, :, :], lg[:, :, :], firsts[:, :, :], ALU.mult), "B", "route")
                        wait("B", "route", n=3)
                        sig(V.tensor_reduce(lmax[:, :], lg[:, :, :], AX.X, ALU.max), "B", "route")
                        wait("B", "route", n=4)
                        for t in range(T):
                            V.tensor_scalar(oh[:, t, :], lg[:, t, :], lmax[:, t:t + 1], None, ALU.is_equal)
                            ins = V.tensor_scalar(oh12[:, t, :, :], lg[:, t:t + 1, :].broadcast_to([P, 3, E]), lmax[:, t:t + 1], None, ALU.is_equal)
                        sig(ins, "B", "onehot")
                    elif (thread, step) == ("B", "experts"):
                        if n == 0:
                            wait("B", "ohT_psum", n=1)
                            wait("b", "h_psum")
                            sig(V.tensor_copy(ohT[:, :], bank(6)[0:3 * E, 0:S // 2].bitcast(BF16)), "B", "ohT_sbuf")
                            wait("B", "xT_sbuf", n=1)
                            wait("b", "scores")
                        wait("B", "ohT_psum", n=2 + n)
                        for e in range(2):
                            sig(V.tensor_tensor(XE[:, 2 * n + e, :, :], XTB[:, :, :], bank(7 - n).rearrange("p (e s) -> p e s", e=2)[:, e:e + 1, :].broadcast_to([P, C, S]), ALU.mult), "B", "x_expert")
                    elif (thread, step) == ("B", "ffn_sum"):
                        wait("B", "ffn_psum", "ffn_base")
                        sig(V.tensor_tensor(XNB[:, :, :], halves(6), FB[:, :, :], ALU.add), "B", "ffn_sum")
                        wait("B", "ffn_sum")
                        stats("B", 1, XNB, FFN_EPS)
                    elif (thread, step) == ("B", "ffn_end"):
                        normed("B", 1, XNB, XNB)
                        wait("B", "xn_ready", n=2)
                        sig(V.tensor_tensor(XNB[:, :, :], XNB[:, :, :], rows[:, GAMMA:GAMMA + 1, :].broadcast_to([P, T, D]), ALU.mult), "B", "ffn_scale")
                        wait("B", "ffn_scale", n=1)
                        sig(V.tensor_tensor(XNB[:, :, :], XNB[:, :, :], rows[:, BETA:BETA + 1, :].broadcast_to([P, T, D]), ALU.add), "B", "ffn_scale")
                        wait("B", "ffn_scale", n=2)
                        sig(V.tensor_tensor(Z[:, :, :], Y[:, :, :], XNB[:, :, :], ALU.add), "B", "x2_ready")
                        wait("B", "x2_ready")
                    elif (thread, step) == ("B", "l1_v"):
                        wait("B", "v_psum")
                        wait("b", "weighed")
                        vp = bank(6).rearrange("p (k h a d) -> p k h a d", k=T, a=2, d=DK)
                        for a in range(2):
                            dst = V2B[:, :, :, :].rearrange("p k (h a) d -> p k h a d", a=2)[:, :, :, a, a * DK:(a + 1) * DK]
                            sig(V.tensor_copy(dst, vp[:, :, :, a, :]), "B", "v_sbuf")
                    elif (thread, step) == ("B", "l1_finish"):
                        wait("B", "weighed", "wT_sbuf")
                        wait(other, "y_psum")
                        sig(V.tensor_tensor(ot, po, rt, ALU.mult), "B", "oT")
                    elif (thread, step) == ("B", "l1_output"):
                        wait("B", "y_psum", "base")
                        sig(V.tensor_tensor(Z[:, :, :], halves(5), FB[:, :, :], ALU.add), "B", "x3_ready")
                        wait("B", "x3_ready")
                    elif (thread, step) == ("B", "quantise"):
                        wait("B", "xn_ready")
                        sig(V.tensor_reduce(am[:, 0, :], XNB[:, :, :], AX.X, ALU.max, apply_absolute_value=True), "B", "amax")
                        wait("B", "amax", n=1)
                        sig(V.tensor_scalar(am[:, 0, :], am[:, 0, :], BIT_EPS, None, ALU.add), "B", "amax")
                        wait("B", "amax", n=2)
                        V.reciprocal(am[:, 1, :], am[:, 0, :])
                        sig(V.tensor_scalar(am[:, 2, :], am[:, 0, :], wscale[:, :], 1.0 / 127.0, ALU.mult, ALU.mult), "B", "amax")
                        wait("B", "amax", n=3)
                        for t in range(T):
                            ins = V.tensor_scalar(XNB[:, t, :], XNB[:, t, :], am[:, 1, t:t + 1], 127.0, ALU.mult, ALU.mult)
                        sig(ins, "B", "zq")
                        wait("B", "zq", n=1)
                        sig(V.tensor_scalar(XNB[:, :, :], XNB[:, :, :], 127.0, -128.0, ALU.min, ALU.max), "B", "zq")
                        wait("B", "zq", n=2)
                        sig(V.tensor_scalar(XNB[:, :, :], XNB[:, :, :], ROUND, None, ALU.add), "B", "zq")
                        wait("B", "zq", n=3)
                        sig(V.tensor_scalar(AQ, XNB[:, :, :], -ROUND, None, ALU.add), "B", "aq")
                    elif (thread, step) == ("B", "bit_T"):
                        wait("B", "aT_psum")
                        sig(V.tensor_copy(AQT, bank(5)[:, 0:D].bitcast(BF16).rearrange("p (c s) -> p c s", c=C)), "B", "aT_sbuf")
                    elif (thread, step) == ("B", "bit"):
                        wait("B", "bit_psum")
                        for t in range(T):
                            ins = V.scalar_tensor_tensor(out=FB[:, t, :], in0=halves(5)[:, t, :], scalar=am[:, 2, t:t + 1], in1=Z[:, t, :], op0=ALU.mult, op1=ALU.add)
                        sig(ins, "B", "out_sbuf")
            iterations(dve, body, rest_of_setup, lambda: dve.wait_ge(relv_tab, 48), relative_keys)

        @block.tensor
        def _(pe):
            TE = nc.tensor
            pe.wait_ge(const_made, CONSTS)
            pe.wait_ge(w_loaded, 16 * 9)
            for m in range(8):
                if m >= 4:
                    pe.wait_ge(wtr_sbuf, m - 3)
                for c in range(C):
                    for o in range(C):
                        ins = TE.transpose(bank(m % 4)[:, c * D + o * P:c * D + (o + 1) * P], WST[:, m, o, c * P:(c + 1) * P], ident[:, :])
                ins.then_inc(wtr_psum, 1)
            pe.wait_ge(wtr_sbuf, 8)

            def body(it, first, steps):

                def transpose_tiles(src, dst_bank, thread, name):
                    for c in range(C):
                        for t in range(T):
                            ins = TE.transpose(bank(dst_bank)[:, c * S + t * P:c * S + (t + 1) * P], src[:, t, c * P:(c + 1) * P], ident[:, :])
                    sig(ins, thread, name)

                def project_T(m, src, dst_bank, thread, name):
                    for g in range(C):
                        for c in range(C):
                            ins = TE.matmul(bank(dst_bank)[:, g * S:(g + 1) * S], wT[:, m, c, g * P:(g + 1) * P], src[:, c, :], start=c == 0, stop=c == C - 1)
                    sig(ins, thread, name)

                def project(m, src, dst_bank, thread, name):
                    for t in range(T):
                        for c in range(C):
                            ins = TE.matmul(bank(dst_bank)[:, t * D:(t + 1) * D], src[:, c, t * P:(t + 1) * P], wT[:, m, c, :], start=c == 0, stop=c == C - 1)
                    sig(ins, thread, name)

                def scores(thread, p):
                    qt, hp = p // QPAIRS, p % QPAIRS
                    if p >= 2:
                        if thread == "A":
                            wait("A", "exped", n=2 * (p - 1))
                        else:
                            wait("B", "masked", n=p - 1)
                    elif p == 0:
                        wait(thread, "q_stacked", "k_stacked")
                        if thread == "A":
                            wait("A", "rel_sbuf")
                            wait("a", "exped")
                            wait("b", "masked")
                        elif with_a:
                            wait("A", "exped")
                        else:
                            wait("b", "masked")
                    sv = bank(p % 2).rearrange("p (h s) -> p h s", h=2)
                    for i in range(2):
                        h = 2 * hp + i
                        if thread == "B":
                            nk = S if qt else P
                            ins = TE.matmul(sv[:, i, 0:nk], QSB[:, h, qt * P:(qt + 1) * P], KSB[:, h, 0:nk], start=True, stop=True)
                            continue
                        TE.matmul(sv[:, i, :], QS[:, h, qt * P:(qt + 1) * P], KS[:, qt, h, :], start=True, stop=False, skip_group_check=True)
                        TE.matmul(sv[:, i, qt * P:(qt + 1) * P], ET[:, qt, h, :], ident[:, :], start=False, stop=False, is_transpose=True, skip_group_check=True)
                        q0, k0 = (P - 2 * R, P) if qt == 0 else (0, P - R)
                        ins = TE.matmul(sv[q0:q0 + 2 * R, i, k0:k0 + R], EC[:, qt, h, :], ident[EC0:EC0 + R, EC0:EC0 + R], start=False, stop=True, skip_group_check=True)
                    sig(ins, thread, "scores")

                def probs_T(thread, p):
                    qt = p // QPAIRS
                    at = slot(p)
                    wait(thread, "exped", n=2 * (p + 1))
                    if at >= 2:
                        wait(thread, "wT_sbuf", n=at - 1)
                    elif thread == "A":
                        wait("a", "wT_sbuf")
                        wait("b", "wT_sbuf")
                    else:
                        wait(other, "wT_sbuf")
                    for i in range(2):
                        for kt in range(T if thread == "A" or qt else 1):
                            ins = TE.transpose(bank(PW0 + at % 2)[:, (i * T + kt) * P:(i * T + kt + 1) * P], W[:, p % W_RING, i, kt * P:(kt + 1) * P], ident[:, :])
                    sig(ins, thread, "wT_psum")

                def weigh_values(thread, p):
                    qt, hp = p // QPAIRS, p % QPAIRS
                    wait(thread, "wT_sbuf", n=slot(p) + 1)
                    if p == 0:
                        wait(thread, "v_sbuf")
                        if thread == "A":
                            wait("a", "unloaded")
                            wait("b", "oT")
                        elif with_a:
                            wait("A", "unloaded")
                        else:
                            wait("b", "oT")
                    nk = T if thread == "A" or qt else 1
                    g, row = hp // 4, 32 * (hp % 4)
                    ps = bank(PO)[row:row + 32, qt * D + g * P:qt * D + (g + 1) * P]
                    for i in range(2):
                        h = 2 * hp + i
                        for kt in range(nk):
                            if thread == "A":
                                v, w = V2[:, int(kt != qt), kt, h, :], WT_[:, kt, h, :]
                            else:
                                v, w = V2B[:, kt, h, :], WTB[:, p % 2, kt, i, :]
                            ins = TE.matmul(ps, v, w, start=i == 0 and kt == 0, stop=i == 1 and kt == nk - 1, skip_group_check=True)
                    if thread == "B":
                        sig(ins, "B", "weighed")
                    elif hp == QPAIRS - 1:
                        sig(ins, "A", "pv_psum")

                def relative_values(qt, j):
                    if j == 0 and qt == 0:
                        wait("b", "out_sbuf")
                    elif j == 0:
                        wait("A", "relv_sbuf", n=1)
                    for i in range(32):
                        q = 32 * j + i
                        seam = q >= P - R if qt == 0 else q < R
                        ps = bank(RVB)[32 * j:32 * j + 32, i * H:(i + 1) * H]
                        s = P - 1 - q
                        ins = TE.matmul(ps, relv_d[:, s:s + 2, :].rearrange("p s d -> p (s d)"), WT_[:, qt, :, q], start=i == 0, stop=not seam, skip_group_check=True)
                        if seam:
                            s = (P - 1 if qt == 0 else R - 1) - q
                            ins = TE.matmul(ps, relv_o[:, qt, s:s + 2, :].rearrange("p s d -> p (s d)"), WT_[:, 1 - qt, :, q], start=False, stop=True, skip_group_check=True)
                    if j == 3:
                        sig(ins, "A", "relv_psum")

                def inverse_T(thread, qt):
                    at = INV_SLOT[qt]
                    wait(thread, "rinv", n=qt + 1)
                    wait(thread, "wT_sbuf", n=at - 1)
                    for g in range(C):
                        hs = H // C
                        ins = TE.transpose(bank(PW0 + at % 2)[:, g * P:(g + 1) * P], rinv[:, g * hs:(g + 1) * hs, :].rearrange("p h d -> p (h d)"), ident[:, :])
                    sig(ins, thread, "wT_psum")

                for ahead, thread, step, n in steps:
                    off = first + ahead
                    wait = waiter(pe, it, off)
                    with_a = not isinstance(it, int) or 0 <= off < B
                    other = "A" if with_a else "b"
                    if (thread, step) == ("P", "ctxT"):
                        wait("P", "ctx_loaded")
                        wait("B", "v_sbuf")
                        transpose_tiles(CT, 6, "P", "ctxT_psum")
                    elif (thread, step) == ("P", "k"):
                        wait("P", "ctxT_sbuf")
                        wait("B", "f32_ready")
                        project_T(1, CTT, 7, "P", "k_psum")
                    elif (thread, step) == ("P", "v"):
                        wait("A", "x1_ready")
                        project(2, CTT, 5, "P", "v_psum")
                    elif (thread, step) == ("P", "xT"):
                        wait("P", "xn_ready", "ctxT_sbuf")
                        transpose_tiles(CT, 6, "P", "xT_psum")
                    elif (thread, step) == ("P", "q"):
                        wait("P", "xT_sbuf")
                        project_T(0, XT, 6, "P", "q_psum")
                    elif (thread, step) == ("P", "rel") and n < 8:
                        if n == 0:
                            if off == -1:
                                pe.wait_ge(relk_loaded, 16 * len(KPART))
                            wait("P", "q_stacked")
                            wait("P", "f32_ready", n=1)
                        elif n == 1:
                            wait("P", "f32_ready")
                        else:
                            wait("P", "rel_sbuf", n=n - 1)
                        qt, q0 = n // 4, (n % 4) * 32
                        for q in range(q0, q0 + 32):
                            lo = -q - XLO
                            ins = TE.matmul(bank(6 + n % 2)[:, (q - q0) * H:(q - q0 + 1) * H], relk_st[:, 0, lo:lo + P], QS[:, :, qt * P + q], start=q == q0, stop=True, skip_group_check=True)
                        sig(ins, "P", "rel_psum")
                    elif (thread, step) == ("P", "rel"):
                        wait("P", "rel_sbuf", n=7)
                        for t in range(T):
                            for j in range(R):
                                q = (P - R + j) if t == 0 else (P + j)
                                lo = ((P if t == 0 else P - R) - q) - XLO
                                ins = TE.matmul(bank(6)[EC0:EC0 + R, t * 256 + j * H:t * 256 + (j + 1) * H], relk_st[:, 1 + t, lo:lo + R], QS[:, :, q], start=t == 0 and j == 0, stop=True, skip_group_check=True)
                        sig(ins, "P", "rel_psum")
                    elif step == "S" or step == "l1_S":
                        scores(thread, n)
                    elif step == "T" or step == "l1_T":
                        probs_T(thread, n)
                    elif step == "W" or step == "l1_W":
                        weigh_values(thread, n)
                    elif step == "R":
                        relative_values(n // 4, n % 4)
                    elif step == "I" or step == "l1_I":
                        inverse_T(thread, n)
                    elif (thread, step) == ("A", "output"):
                        wait("A", "oT", "relv_sbuf")
                        project(3, OT, RVB, "A", "y_psum")
                    elif (thread, step) == ("B", "ffn_xT"):
                        wait("B", "xn_ready", n=1)
                        wait("b", "v_sbuf")
                        if with_a:
                            wait("A", "rel_sbuf")
                        transpose_tiles(XNB, 6, "B", "xT_psum")
                    elif (thread, step) == ("B", "router"):
                        wait("B", "xT_sbuf", n=1)
                        wait("b", "f32_ready")
                        for t in range(T):
                            for c in range(C):
                                ins = TE.matmul(bank(7)[:, t * E:(t + 1) * E], XTB[:, c, t * P:(t + 1) * P], wr[:, c, :], start=c == 0, stop=c == C - 1)
                        sig(ins, "B", "logits")
                    elif (thread, step) == ("B", "onehot_T"):
                        wait("B", "onehot")
                        for t in range(T):
                            ins = TE.transpose(bank(6)[0:3 * E, 0:S // 2].bitcast(BF16)[:, t * P:(t + 1) * P], oh12[:, t, :, :].rearrange("p a e -> p (a e)"), ident_bf[:, :])
                        sig(ins, "B", "ohT_psum")
                    elif (thread, step) == ("B", "experts"):
                        if n == 1:
                            wait("B", "ohT_sbuf")
                        for e in range(2):
                            for t in range(T):
                                ins = TE.transpose(bank(7 - n)[:, e * S + t * P:e * S + (t + 1) * P], oh[:, t, 2 * n + e:2 * n + e + 1].broadcast_to([P, P]), ident[:, :])
                        sig(ins, "B", "ohT_psum")
                    elif (thread, step) == ("B", "up"):
                        i, half = n // 2, n % 2
                        if n == 0:
                            wait("B", "ohT_sbuf", "x_expert")
                        elif n % 4 == 0 and n >= 8:
                            wait("B", "gelu", n=n // 4 - 1)
                        ps = bank(6 + (i // 2) % 2)[:, (i % 2) * S:(i % 2 + 1) * S]
                        if half == 0:
                            TE.matmul(ps, b1p[:, i * P:(i + 1) * P], ohT[:, :], start=True, stop=False)
                        for e in range(2 * half, 2 * half + 2):
                            for c in range(C):
                                ins = TE.matmul(ps, w1[:, e, c, i * P:(i + 1) * P], XE[:, e, c, :], start=False, stop=e == E - 1 and c == C - 1)
                        if n % 4 == 3:
                            sig(ins, "B", "h_psum")
                    elif (thread, step) == ("B", "down"):
                        wait("B", "gelu", n=max(3, n + 1))
                        for i in range(2 * n, 2 * n + 2):
                            for t in range(T):
                                ins = TE.matmul(bank(6)[:, t * D:(t + 1) * D], GT[:, i, t * P:(t + 1) * P], wf[:, i, :], start=i == 0 and t == 0, stop=i == IC - 1, skip_group_check=True)
                        if n == 3:
                            sig(ins, "B", "ffn_psum")
                    elif (thread, step) == ("B", "l1_k"):
                        wait("B", "gelu")
                        wait("a", "ctx_copied")
                        project_T(5, CTB, 7, "B", "k_psum")
                    elif (thread, step) == ("B", "l1_v"):
                        wait("B", "ffn_sum")
                        project(6, CTB, 6, "B", "v_psum")
                    elif (thread, step) == ("B", "l1_xT"):
                        wait("B", "xn_ready", n=3)
                        wait("B", "f32_ready", n=1)
                        transpose_tiles(XNB, 7, "B", "xT_psum")
                    elif (thread, step) == ("B", "l1_q"):
                        wait("B", "xT_sbuf")
                        project_T(4, XTB, 7, "B", "q_psum")
                    elif (thread, step) == ("B", "l1_output"):
                        wait("B", "oT")
                        wait("P", "v_sbuf")
                        wait("A", "x1_ready")
                        wait("b", "out_sbuf")
                        project(7, OT, 5, "B", "y_psum")
                    elif (thread, step) == ("B", "bit_T"):
                        wait("B", "aq", "x3_ready")
                        for c in range(C):
                            for t in range(T):
                                ins = TE.transpose(bank(5)[:, 0:D].bitcast(BF16)[:, c * S + t * P:c * S + (t + 1) * P], AQ[:, t, c * P:(c + 1) * P], ident_bf[:, :])
                        sig(ins, "B", "aT_psum")
                    elif (thread, step) == ("B", "bit"):
                        wait("B", "aT_sbuf")
                        for t in range(T):
                            for c in range(C):
                                ins = TE.matmul(bank(5)[:, t * D:(t + 1) * D], AQT[:, c, t * P:(t + 1) * P], wbT[:, c, :], start=c == 0, stop=c == C - 1)
                        sig(ins, "B", "bit_psum")

            def after_first():
                pe.wait_ge(abs_psum, 1)
                TE.matmul(bank(7)[:, 0:1], ones, wsum[:, 0:1], start=True, stop=True).then_inc(abs_psum, 1)
                pe.wait_ge(abs_psum, 3)
                wbps = bank(7)[:, 0:D].bitcast(BF16)
                for c in range(C):
                    for o in range(C):
                        ins = TE.transpose(wbps[:, c * D + o * P:c * D + (o + 1) * P], wbbf[:, o, c * P:(c + 1) * P], ident_bf[:, :])
                ins.then_inc(abs_psum, 1)
                pe.wait_ge(relv_tab, 48)
                pe.wait_ge(setup_dve, 2)

            def before_loop():
                pe.wait_ge(big_loaded, 32)
                pe.wait_ge(b1_loaded, 48)
            iterations(pe, body, after_first, before_loop)

        emitted = 3
        assert all(raised[n] == emitted * PER[n] for n in PER), [(n, raised[n], PER[n]) for n in PER if raised[n] != emitted * PER[n]]


_INS = ["x", "ctx_1024", "mask_BxSxS2_bf0", "L0_xattn_Wq", "L0_xattn_bq", "L0_xattn_Wk", "L0_xattn_bk", "L0_xattn_Wv",
        "L0_xattn_bv", "L0_xattn_Wo", "L0_xattn_bo", "L0_xattn_rel_k_table", "L0_xattn_rel_v_table", "L0_ffn_W_router",
        "L0_ffn_W1", "L0_ffn_b1", "L0_ffn_Wo", "L0_ffn_bo", "L0_ffn_ln_gamma", "L0_ffn_ln_beta", "L1_xattn_Wq",
        "L1_xattn_Wk", "L1_xattn_Wv", "L1_xattn_Wout", "L1_xattn_b_out", "L1_ffn_weight"]


def kernel(**inputs):
    import concourse.bacc as bacc
    from concourse.bass_utils import run_bass_kernel_spmd

    nc = bacc.Bacc("TRN2", target_bir_lowering=False, num_devices=1)
    arrays, args = {}, []
    for name in _INS:
        a = np.ascontiguousarray(inputs[name])
        arrays[f"in_{name}"] = a
        args.append(nc.dram_tensor(f"in_{name}", a.shape, mybir.dt.from_np(a.dtype), kind="ExternalInput").ap())
    args.append(nc.dram_tensor("out", (B, S, D), F32, kind="ExternalOutput").ap())
    _program(nc, *args)
    return run_bass_kernel_spmd(nc, [arrays], core_ids=[0]).results[0]["out"]
```
